# Optimizing a Trainium2 kernel written in Bass

```python
import numpy as np
import jax
import jax.numpy as jnp

def _softmax(x, axis=-1):
    return jax.nn.softmax(x, axis=axis)

def _gelu(x):
    return jax.nn.gelu(x, approximate=True)

def _silu(x):
    return jax.nn.silu(x)

def _sigmoid(x):
    return jax.nn.sigmoid(x)

def _layernorm(x, axis=-1, eps=1e-05):
    m = jnp.mean(x, axis=axis, keepdims=True)
    v = jnp.var(x, axis=axis, keepdims=True)
    return (x - m) / jnp.sqrt(v + eps)

def _scatter_add(tgt, idx, src, axis=0):
    return tgt.at[idx].add(src)

def _segment_sum(src, seg, n):
    return jax.ops.segment_sum(src, seg, n)
kernel_name = 'mk_early_fusion_d2_tok_img256_r4_729ce2'

def setup_inputs(seed: int=0):
    np.random.seed(seed)
    _w = jnp.asarray

    def _rec_inputs():
        import jax
        import jax.numpy as jnp
        _rk = jax.random.key(seed)
        x = -0.000596345 + 1.00056 * jax.random.normal(jax.random.fold_in(_rk, 1), (32, 64, 64, 3), jnp.float32)
        txt = -1.92552e-05 + 0.02 * jax.random.normal(jax.random.fold_in(_rk, 2), (32, 128, 64), jnp.float32)
        return (x, txt)
    x, txt = _rec_inputs()

    def _L0_tok_setup():
        import jax, jax.numpy as jnp
        import numpy as np
        M1 = 20
        M2 = 20

        def _spectral_conv(x, w):
            B, Cin, H, W = x.shape
            x_ft = jnp.fft.rfft2(x, norm='ortho')
            out = jnp.einsum('bixy,ioxy->boxy', x_ft[:, :, :M1, :M2], w.astype(x_ft.dtype))
            out_ft = jnp.zeros((B, w.shape[1], H, W // 2 + 1), dtype=x_ft.dtype)
            out_ft = out_ft.at[:, :, :M1, :M2].set(out)
            return jnp.fft.irfft2(out_ft, s=(H, W), norm='ortho')

        def _gelu(x):
            return jax.nn.gelu(x, approximate=False)
        key = jax.random.key(seed)
        ks = jax.random.split(key, 16)
        B, H, W, width = (16, 64, 64, 32)
        scale = 1.0 / (width * width)
        d = {}
        d['coords'] = jax.random.normal(ks[0], (B, H, W, 3), dtype=jnp.float32)
        d['fc0_w'] = jax.random.normal(ks[1], (3, width), dtype=jnp.float32) * 0.1
        d['fc0_b'] = jnp.zeros((width,), dtype=jnp.float32)
        for i in range(4):
            d[f'sw{i}'] = scale * jax.random.normal(ks[2 + i], (width, width, M1, M2), dtype=jnp.float32)
            d[f'cw{i}'] = jax.random.normal(ks[6 + i], (width, width), dtype=jnp.float32) * 0.1
            d[f'cb{i}'] = jnp.zeros((width,), dtype=jnp.float32)
        d['fc1_w'] = jax.random.normal(ks[10], (width, 64), dtype=jnp.float32) * 0.1
        d['fc1_b'] = jnp.zeros((64,), dtype=jnp.float32)
        d['fc2_w'] = jax.random.normal(ks[11], (64, 1), dtype=jnp.float32) * 0.1
        d['fc2_b'] = jnp.zeros((1,), dtype=jnp.float32)
        return d
    _L0_tok_all = _L0_tok_setup()
    _L0_tok_in = {k: v for k, v in _L0_tok_all.items() if k in ('fc0_w', 'fc0_b', 'sw0', 'cw0', 'cb0', 'sw1', 'cw1', 'cb1', 'sw2', 'cw2', 'cb2', 'sw3', 'cw3', 'cb3', 'fc1_w', 'fc1_b', 'fc2_w', 'fc2_b')}
    del _L0_tok_all

    def _L0_attn_setup():
        import jax, jax.numpy as jnp
        import numpy as np
        SEQ, BATCH, IN, HID = (512, 64, 64, 64)
        key = jax.random.key(seed)
        k1, k2, k3, k4, k5 = jax.random.split(key, 5)
        s = 1.0 / np.sqrt(HID)
        return {'x_in': jax.random.normal(k1, (SEQ, BATCH, IN), dtype=jnp.float32), 'W_ih': jax.random.uniform(k2, (HID, IN), jnp.float32, -s, s), 'W_hh': jax.random.uniform(k3, (HID, HID), jnp.float32, -s, s), 'b_ih': jax.random.uniform(k4, (HID,), jnp.float32, -s, s), 'b_hh': jax.random.uniform(k5, (HID,), jnp.float32, -s, s)}
    _L0_attn_all = _L0_attn_setup()
    _L0_attn_in = {k: v for k, v in _L0_attn_all.items() if k in ('W_ih', 'W_hh', 'b_ih', 'b_hh')}
    del _L0_attn_all

    def _L0_ffn_setup():
        import math
        import jax, jax.numpy as jnp
        import numpy as np
        CAPACITY_FACTOR = 1.25
        key = jax.random.key(seed)
        ks = jax.random.split(key, 5)
        B, L, D, F, E = (8, 2048, 64, 256, 8)
        h = jax.random.normal(ks[0], (B, L, D), dtype=jnp.float32)
        gate_w = jax.random.normal(ks[1], (D, E), dtype=jnp.float32) * 0.02
        gate_b = jnp.zeros((E,), dtype=jnp.float32)
        w1 = jax.random.normal(ks[2], (E, D, F), dtype=jnp.float32) * (1.0 / math.sqrt(D))
        b1 = jnp.zeros((E, F), dtype=jnp.float32)
        w2 = jax.random.normal(ks[3], (E, F, D), dtype=jnp.float32) * (1.0 / math.sqrt(F))
        b2 = jnp.zeros((E, D), dtype=jnp.float32)
        return {'h': h, 'gate_w': gate_w, 'gate_b': gate_b, 'w1': w1, 'b1': b1, 'w2': w2, 'b2': b2}
    _L0_ffn_all = _L0_ffn_setup()
    _L0_ffn_in = {k: v for k, v in _L0_ffn_all.items() if k in ('gate_w', 'gate_b', 'w1', 'b1', 'w2', 'b2')}
    del _L0_ffn_all

    def _L1_attn_setup():
        import jax, jax.numpy as jnp
        import numpy as np
        B, S, C = (8, 256, 64)
        H, KD = (8, 64)
        HEAD_DIM = KD // H
        key = jax.random.key(seed)
        ks = jax.random.split(key, 5)
        sc = 0.02
        return {'x': jax.random.normal(ks[0], (B, S, C), dtype=jnp.float32), 'Wq': jax.random.normal(ks[1], (H * KD, C), dtype=jnp.float32) * sc, 'Wk': jax.random.normal(ks[2], (KD, C), dtype=jnp.float32) * sc, 'Wv': jax.random.normal(ks[3], (KD, C), dtype=jnp.float32) * sc, 'Wo': jax.random.normal(ks[4], (C, H * KD), dtype=jnp.float32) * sc}
    _L1_attn_all = _L1_attn_setup()
    _L1_attn_in = {k: v for k, v in _L1_attn_all.items() if k in ('Wq', 'Wk', 'Wv', 'Wo')}
    del _L1_attn_all

    def _L1_ffn_setup():
        import jax, jax.numpy as jnp
        import numpy as np
        DIM = 64
        HEADS = 8
        NUM_KEYS = 64
        NUM_KV = NUM_KEYS ** 2
        PK_TOPK = 16
        FINAL_TOPK = 16
        DIM_KEY = DIM // 2
        P = 2

        def _pk(x, Wq_pk, pk_keys):
            b, n, _ = x.shape
            q = (x @ Wq_pk).reshape(b, n, P, HEADS, DIM_KEY).transpose(2, 0, 1, 3, 4)
            sim = jnp.einsum('pbnhd,pkhd->pbnhk', q, pk_keys)
            scores, idx = jax.lax.top_k(sim, PK_TOPK)
            idx0 = idx[0]
            idx1 = idx[1] * NUM_KEYS
            index = (idx0[..., :, None] + idx1[..., None, :]).reshape(b, n, HEADS, PK_TOPK * PK_TOPK)
            score = (scores[0][..., :, None] + scores[1][..., None, :]).reshape(b, n, HEADS, PK_TOPK * PK_TOPK)
            final_scores, pk_idx = jax.lax.top_k(score, FINAL_TOPK)
            final_indices = jnp.take_along_axis(index, pk_idx, axis=-1)
            final_scores = jax.nn.softmax(final_scores, axis=-1)
            return (final_scores, final_indices)
        key = jax.random.key(seed)
        ks = jax.random.split(key, 7)
        b, n = (2, 256)
        std = 0.02
        x = jax.random.normal(ks[0], (b, n, DIM), dtype=jnp.float32)
        Wq_pk = jax.random.normal(ks[1], (DIM, P * HEADS * DIM_KEY), dtype=jnp.float32) * std
        pk_keys = jax.random.normal(ks[2], (P, NUM_KEYS, HEADS, DIM_KEY), dtype=jnp.float32) * std
        Wq = jax.random.normal(ks[3], (DIM, HEADS * DIM), dtype=jnp.float32) * std
        keys_table = jax.random.normal(ks[4], (NUM_KV * HEADS, DIM), dtype=jnp.float32) * std
        values_table = jax.random.normal(ks[5], (NUM_KV * HEADS, DIM), dtype=jnp.float32) * std
        Wo = jax.random.normal(ks[6], (DIM * HEADS, DIM), dtype=jnp.float32) * std
        return {'x': x, 'Wq_pk': Wq_pk, 'pk_keys': pk_keys, 'Wq': Wq, 'keys_table': keys_table, 'values_table': values_table, 'Wo': Wo}
    _L1_ffn_all = _L1_ffn_setup()
    _L1_ffn_in = {k: v for k, v in _L1_ffn_all.items() if k in ('Wq_pk', 'pk_keys', 'Wq', 'keys_table', 'values_table', 'Wo')}
    del _L1_ffn_all
    return {'x': x, 'txt': txt, 'L0_tok_fc0_w': _L0_tok_in['fc0_w'], 'L0_tok_fc0_b': _L0_tok_in['fc0_b'], 'L0_tok_sw0': _L0_tok_in['sw0'], 'L0_tok_cw0': _L0_tok_in['cw0'], 'L0_tok_cb0': _L0_tok_in['cb0'], 'L0_tok_sw1': _L0_tok_in['sw1'], 'L0_tok_cw1': _L0_tok_in['cw1'], 'L0_tok_cb1': _L0_tok_in['cb1'], 'L0_tok_sw2': _L0_tok_in['sw2'], 'L0_tok_cw2': _L0_tok_in['cw2'], 'L0_tok_cb2': _L0_tok_in['cb2'], 'L0_tok_sw3': _L0_tok_in['sw3'], 'L0_tok_cw3': _L0_tok_in['cw3'], 'L0_tok_cb3': _L0_tok_in['cb3'], 'L0_tok_fc1_w': _L0_tok_in['fc1_w'], 'L0_tok_fc1_b': _L0_tok_in['fc1_b'], 'L0_tok_fc2_w': _L0_tok_in['fc2_w'], 'L0_tok_fc2_b': _L0_tok_in['fc2_b'], 'L0_attn_W_ih': _L0_attn_in['W_ih'], 'L0_attn_W_hh': _L0_attn_in['W_hh'], 'L0_attn_b_ih': _L0_attn_in['b_ih'], 'L0_attn_b_hh': _L0_attn_in['b_hh'], 'L0_ffn_gate_w': _L0_ffn_in['gate_w'], 'L0_ffn_gate_b': _L0_ffn_in['gate_b'], 'L0_ffn_w1': _L0_ffn_in['w1'], 'L0_ffn_b1': _L0_ffn_in['b1'], 'L0_ffn_w2': _L0_ffn_in['w2'], 'L0_ffn_b2': _L0_ffn_in['b2'], 'L1_attn_Wq': _L1_attn_in['Wq'], 'L1_attn_Wk': _L1_attn_in['Wk'], 'L1_attn_Wv': _L1_attn_in['Wv'], 'L1_attn_Wo': _L1_attn_in['Wo'], 'L1_ffn_Wq_pk': _L1_ffn_in['Wq_pk'], 'L1_ffn_pk_keys': _L1_ffn_in['pk_keys'], 'L1_ffn_Wq': _L1_ffn_in['Wq'], 'L1_ffn_keys_table': _L1_ffn_in['keys_table'], 'L1_ffn_values_table': _L1_ffn_in['values_table'], 'L1_ffn_Wo': _L1_ffn_in['Wo']}

def reference(x, txt, L0_tok_fc0_w, L0_tok_fc0_b, L0_tok_sw0, L0_tok_cw0, L0_tok_cb0, L0_tok_sw1, L0_tok_cw1, L0_tok_cb1, L0_tok_sw2, L0_tok_cw2, L0_tok_cb2, L0_tok_sw3, L0_tok_cw3, L0_tok_cb3, L0_tok_fc1_w, L0_tok_fc1_b, L0_tok_fc2_w, L0_tok_fc2_b, L0_attn_W_ih, L0_attn_W_hh, L0_attn_b_ih, L0_attn_b_hh, L0_ffn_gate_w, L0_ffn_gate_b, L0_ffn_w1, L0_ffn_b1, L0_ffn_w2, L0_ffn_b2, L1_attn_Wq, L1_attn_Wk, L1_attn_Wv, L1_attn_Wo, L1_ffn_Wq_pk, L1_ffn_pk_keys, L1_ffn_Wq, L1_ffn_keys_table, L1_ffn_values_table, L1_ffn_Wo):
    import jax
    import jax.numpy as jnp

    def _L0_tok_ref(coords, fc0_w, fc0_b, sw0, cw0, cb0, sw1, cw1, cb1, sw2, cw2, cb2, sw3, cw3, cb3, fc1_w, fc1_b, fc2_w, fc2_b):
        import jax, jax.numpy as jnp
        import numpy as np
        M1 = 20
        M2 = 20

        def _spectral_conv(x, w):
            B, Cin, H, W = x.shape
            x_ft = jnp.fft.rfft2(x, norm='ortho')
            out = jnp.einsum('bixy,ioxy->boxy', x_ft[:, :, :M1, :M2], w.astype(x_ft.dtype))
            out_ft = jnp.zeros((B, w.shape[1], H, W // 2 + 1), dtype=x_ft.dtype)
            out_ft = out_ft.at[:, :, :M1, :M2].set(out)
            return jnp.fft.irfft2(out_ft, s=(H, W), norm='ortho')

        def _gelu(x):
            return jax.nn.gelu(x, approximate=False)
        x = coords @ fc0_w + fc0_b
        x = jnp.transpose(x, (0, 3, 1, 2))
        for sw, cw, cb in ((sw0, cw0, cb0), (sw1, cw1, cb1), (sw2, cw2, cb2), (sw3, cw3, cb3)):
            x1 = _spectral_conv(x, sw)
            x2 = jnp.einsum('bchw,oc->bohw', x, cw) + cb[None, :, None, None]
            x = _gelu(x1 + x2)
        x = jnp.transpose(x, (0, 2, 3, 1))
        x = _gelu(x @ fc1_w + fc1_b)
        return (x @ fc2_w + fc2_b)[..., 0]

    def _L0_attn_ref(x_in, W_ih, W_hh, b_ih, b_hh):
        import jax, jax.numpy as jnp
        import numpy as np
        SEQ, BATCH, IN, HID = (512, 64, 64, 64)
        xp = jnp.einsum('tbi,hi->tbh', x_in, W_ih) + b_ih + b_hh
        h0 = jnp.zeros((x_in.shape[1], W_hh.shape[0]), dtype=x_in.dtype)

        def step(h, xp_t):
            h_new = jnp.tanh(xp_t + h @ W_hh.T)
            return (h_new, h_new)
        _, hiddens = jax.lax.scan(step, h0, xp)
        return hiddens

    def _L0_ffn_ref(h, gate_w, gate_b, w1, b1, w2, b2):
        import math
        import jax, jax.numpy as jnp
        import numpy as np
        CAPACITY_FACTOR = 1.25
        B, L, D = h.shape
        E = gate_w.shape[1]
        T = B * L
        C = max(1, math.ceil(CAPACITY_FACTOR * T / E))
        x = h.reshape(T, D)
        logits = x @ gate_w + gate_b
        probs = jax.nn.softmax(logits, axis=-1)
        idx = jnp.argmax(probs, axis=-1)
        prb = jnp.take_along_axis(probs, idx[:, None], axis=1)[:, 0]
        one_hot = jax.nn.one_hot(idx, E, dtype=jnp.float32)
        pos = (jnp.cumsum(one_hot, axis=0) * one_hot).sum(-1).astype(jnp.int32) - 1
        kept = pos < C
        pos_safe = jnp.where(kept, pos, C)
        buf = jnp.zeros((E, C, D), dtype=h.dtype).at[idx, pos_safe].set(x, mode='drop')
        hmid = jax.nn.relu(jnp.einsum('ecd,edf->ecf', buf, w1) + b1[:, None, :])
        ybuf = jnp.einsum('ecf,efd->ecd', hmid, w2) + b2[:, None, :]
        pos_g = jnp.minimum(pos, C - 1)
        y_tok = ybuf[idx, pos_g] * (prb * kept)[:, None]
        y = y_tok.reshape(B, L, D)
        y = jnp.nan_to_num(y, nan=0.0, posinf=10000.0, neginf=-10000.0)
        return y

    def _L1_attn_ref(x, Wq, Wk, Wv, Wo):
        import jax, jax.numpy as jnp
        import numpy as np
        B, S, C = (8, 256, 64)
        H, KD = (8, 64)
        HEAD_DIM = KD // H
        b, s, c = x.shape
        q = jnp.einsum('bsc,oc->bso', x, Wq).reshape(b, s, H, KD).transpose(0, 2, 1, 3)
        k = jnp.einsum('bsc,oc->bos', x, Wk)
        v_conv = jnp.einsum('bsc,oc->bos', x, Wv)
        v = v_conv.reshape(b, s, KD)
        scale = 1.0 / np.sqrt(HEAD_DIM).astype(np.float32)
        scores = jnp.einsum('bhsd,bdt->bhst', q, k) * scale
        attn = jax.nn.softmax(scores, axis=-1)
        ctx = jnp.einsum('bhst,btd->bhsd', attn, v)
        ctx = ctx.transpose(0, 2, 1, 3).reshape(b, H * KD, s)
        out = jnp.einsum('bcp,oc->bop', ctx, Wo)
        return out.transpose(0, 2, 1)

    def _L1_ffn_ref(x, Wq_pk, pk_keys, Wq, keys_table, values_table, Wo):
        import jax, jax.numpy as jnp
        import numpy as np
        DIM = 64
        HEADS = 8
        NUM_KEYS = 64
        NUM_KV = NUM_KEYS ** 2
        PK_TOPK = 16
        FINAL_TOPK = 16
        DIM_KEY = DIM // 2
        P = 2

        def _pk(x, Wq_pk, pk_keys):
            b, n, _ = x.shape
            q = (x @ Wq_pk).reshape(b, n, P, HEADS, DIM_KEY).transpose(2, 0, 1, 3, 4)
            sim = jnp.einsum('pbnhd,pkhd->pbnhk', q, pk_keys)
            scores, idx = jax.lax.top_k(sim, PK_TOPK)
            idx0 = idx[0]
            idx1 = idx[1] * NUM_KEYS
            index = (idx0[..., :, None] + idx1[..., None, :]).reshape(b, n, HEADS, PK_TOPK * PK_TOPK)
            score = (scores[0][..., :, None] + scores[1][..., None, :]).reshape(b, n, HEADS, PK_TOPK * PK_TOPK)
            final_scores, pk_idx = jax.lax.top_k(score, FINAL_TOPK)
            final_indices = jnp.take_along_axis(index, pk_idx, axis=-1)
            final_scores = jax.nn.softmax(final_scores, axis=-1)
            return (final_scores, final_indices)
        b, n, d = x.shape
        q = (x @ Wq).reshape(b, n, HEADS, DIM) * DIM ** (-0.5)
        kv_scores, indices = _pk(x, Wq_pk, pk_keys)
        offsets = jnp.arange(HEADS, dtype=indices.dtype) * NUM_KV
        ind = indices + offsets[None, None, :, None]
        k = jnp.einsum('bnhk,bnhkd->bnhd', kv_scores, keys_table[ind])
        v = jnp.einsum('bnhk,bnhkd->bnhd', kv_scores, values_table[ind])
        sim = jnp.einsum('bihd,bjhd->bhij', q, k)
        neg = -jnp.finfo(sim.dtype).max
        causal = jnp.tril(jnp.ones((n, n), dtype=bool))
        sim = jnp.where(causal, sim, neg)
        attn = jax.nn.softmax(sim, axis=-1)
        out = jnp.einsum('bhij,bjhd->bhid', attn, v)
        out = out.transpose(0, 2, 1, 3).reshape(b, n, HEADS * DIM)
        return out @ Wo
    h = _L0_tok_ref(x, L0_tok_fc0_w, L0_tok_fc0_b, L0_tok_sw0, L0_tok_cw0, L0_tok_cb0, L0_tok_sw1, L0_tok_cw1, L0_tok_cb1, L0_tok_sw2, L0_tok_cw2, L0_tok_cb2, L0_tok_sw3, L0_tok_cw3, L0_tok_cb3, L0_tok_fc1_w, L0_tok_fc1_b, L0_tok_fc2_w, L0_tok_fc2_b)
    h = jnp.concatenate([h, txt], axis=1)
    h = h + _L0_attn_ref(_layernorm(h, axis=-1), L0_attn_W_ih, L0_attn_W_hh, L0_attn_b_ih, L0_attn_b_hh)
    h = h + _L0_ffn_ref(_layernorm(h, axis=-1), L0_ffn_gate_w, L0_ffn_gate_b, L0_ffn_w1, L0_ffn_b1, L0_ffn_w2, L0_ffn_b2)
    h = h + _L1_attn_ref(_layernorm(h, axis=-1), L1_attn_Wq, L1_attn_Wk, L1_attn_Wv, L1_attn_Wo)
    h = h + _L1_ffn_ref(_layernorm(h, axis=-1), L1_ffn_Wq_pk, L1_ffn_pk_keys, L1_ffn_Wq, L1_ffn_keys_table, L1_ffn_values_table, L1_ffn_Wo)
    return h

_drawn_inputs = setup_inputs


def setup_inputs(seed=0):
    import zlib

    import numpy as np

    out = dict(_drawn_inputs(seed))
    spreads = {'L0_tok_fc0_b': (0.0, 0.399),
     'L0_tok_cb0': (0.0, 0.1),
     'L0_tok_cb1': (0.0, 0.1),
     'L0_tok_cb2': (0.0, 0.1),
     'L0_tok_cb3': (0.0, 0.1),
     'L0_tok_fc1_b': (0.0, 0.1),
     'L0_ffn_gate_b': (0.0, 0.1),
     'L0_ffn_b1': (0.0, 0.415),
     'L0_ffn_b2': (0.0, 0.308)}
    factors = {'L0_tok_sw0': 7.004,
     'L0_tok_sw1': 8.0,
     'L0_tok_sw2': 8.0,
     'L0_tok_sw3': 8.0,
     'L1_attn_Wq': 8.0,
     'L1_attn_Wk': 8.0,
     'L1_attn_Wv': 5.467,
     'L1_attn_Wo': 5.354,
     'L1_ffn_Wq_pk': 8.0,
     'L1_ffn_pk_keys': 8.0,
     'L1_ffn_Wq': 64.0,
     'L1_ffn_keys_table': 64.0,
     'L1_ffn_values_table': 8.0,
     'L1_ffn_Wo': 8.0}
    for name, (base, spread) in spreads.items():
        noise = np.random.default_rng([zlib.crc32(name.encode()), seed]).standard_normal(out[name].shape)
        drawn = base * np.exp(spread * noise) if base else spread * noise
        out[name] = jnp.asarray(drawn.astype(out[name].dtype))
    for name, factor in factors.items():
        out[name] = (out[name] * factor).astype(out[name].dtype)
    return out
```

```python
import numpy as np
import concourse.bass as bass
from concourse import mybir
from contextlib import ExitStack

F32 = mybir.dt.float32
I32 = mybir.dt.int32
U32 = mybir.dt.uint32
ALU = mybir.AluOpType
ACT = mybir.ActivationFunctionType
AX = mybir.AxisListType

B, SIDE, WID, MODES, LAYERS = 32, 64, 32, 20, 4
Q4 = 4
GB = 2
GROUPS = B // (Q4 * GB)
POS = SIDE * SIDE
ROWQ = POS // 512
CHUNKS = 10
KHC = MODES // CHUNKS
KWG = [(0, 4), (4, 4), (8, 4), (12, 4), (16, 2), (18, 2)]
KW2 = MODES // 2
TG = [(0, 3), (3, 3), (6, 2), (8, 2)]

F_T = ROWQ + len(KWG)
I_T = len(TG) + ROWQ
I_M = KW2 + ROWQ
T_LAYER = GB * (F_T + I_T)
M_LAYER = GB * F_T + CHUNKS + GB * I_M
M_IN = GB * ROWQ
M_GROUP = M_IN + LAYERS * M_LAYER + GB * ROWQ * 2
T_GROUP = LAYERS * T_LAYER + GB * ROWQ
CREDIT = 2


def fourier_constants():
    k, p = np.arange(MODES), np.arange(SIDE)
    ang = 2 * np.pi * np.outer(p, k) / SIDE
    cos, sin = np.cos(ang), np.sin(ang)
    f1 = np.zeros((2, SIDE, 2, MODES, 2))
    for a in range(2):
        f1[a, :, a, :, 0], f1[a, :, a, :, 1] = cos, -sin
    f2 = np.zeros((SIDE, 2, MODES, 2))
    f2[:, 0, :, 0], f2[:, 1, :, 0] = cos, sin
    f2[:, 0, :, 1], f2[:, 1, :, 1] = -sin, cos
    f2 /= SIDE
    g3 = np.zeros((2, MODES, 2, SIDE, 2, 2))
    for a in range(2):
        g3[a, :, 0, :, a, 0], g3[a, :, 1, :, a, 0] = cos.T, -sin.T
        g3[a, :, 0, :, a, 1], g3[a, :, 1, :, a, 1] = sin.T, cos.T
    twice = np.where(k == 0, 1.0, 2.0)[:, None] / SIDE
    g4 = np.zeros((2, MODES, 2, 2, SIDE))
    for a in range(2):
        g4[a, :, 0, a], g4[a, :, 1, a] = twice * cos.T, -twice * sin.T
    return [np.ascontiguousarray(x, np.float32) for x in (
        f1.reshape(128, 80), f2.reshape(128, 40), g3.reshape(80, 256), g4.reshape(80, 128))]



SEQ, D = 192, 64
PAIRS = B // 2
TOK = 2 * SEQ
NT3 = TOK // 128
E, FF, CAP = 8, 256, 960
H, TOPK, NK = 8, 16, 64
CAND = [TOPK // (i + 1) for i in range(TOPK)]
NC50 = sum(CAND)
EPS = 1e-5
FMAX = float(np.finfo(np.float32).max)
RING = 3

FRONT = [("xT", 0, 1), ("rnn", 1, 2), ("rnn_back", 2, 1),
         ("moeT", 0, 1), ("gate", 1, 1), ("place", 1, 1), ("hidA", 2, 8), ("hidB", 3, 8), ("expert", 0, 4), ("expertB", 1, 4),
         ("attT", 0, 1), ("qkvA", 2, 5), ("qkvB", 3, 5), ("scoreA", 2, 6), ("scoreB", 3, 6),
         ("z", 0, 2), ("z2", 1, 2), ("att", 2, 1),
         ("pkT", 0, 1), ("qpkA", 2, 2), ("qpkB", 3, 2), ("simA", 2, 3), ("simB", 3, 3)]
BACK = [("q5A", 2, 4), ("q5B", 3, 4), ("kvA", 2, 3), ("kvB", 3, 3), ("vwA", 2, 3), 
        ("s5A", 2, 6), ("s5B", 3, 6), ("pt0", 0, 6), ("out", 1, 6)]


def number(plan, name, k):
    at = 0
    bank = next(b for n, b, _ in plan if n == name)
    for n, b, c in plan:
        if n == name:
            return bank, at + k
        if b == bank:
            at += c


def total(plan, bank):
    return sum(c for _, b, c in plan if b == bank)


PLANS = {"front": FRONT, "back": BACK}




TAKES = {False: {"forward0": 2, "rnn": 1, "forward1": 2, "moe": 2, "att": 2, "pk": 1, "mix": 0, "top": 1, "inverse0": 2, "inverse1": 2},
         True: {"forward0": 2, "forward1": 2, "mix": 4, "inverse0": 2, "inverse1": 2, "tokens": 1, "rnn": 1, "moe": 2, "att": 2, "pk": 1}}
HALF = POS // 2


def early_fusion(nc, xT, fc0, sw, cwb, fc1, fc2, f1, f2, g3, g4, txt, wrnn, brnn, gw, w1, w2, b2, wq, wk, wv, wot, wpk, keysT, wq5, wo5,
                 table, ident_in, tri_in, iota_in, eight_in, hbase_in, later_in, out):
    tok = nc.dram_tensor("tokens", (B, POS), F32, kind="Internal").ap()
    ctx = ExitStack()
    with ctx:
        sb = lambda n, s, d=F32: ctx.enter_context(nc.sbuf_tensor(n, s, d))
        sem = lambda n: ctx.enter_context(nc.semaphore(n))
        TP = [ctx.enter_context(nc.psum_tensor(f"TP{i}", [128, 512], F32)) for i in range(2)]
        MM = [ctx.enter_context(nc.psum_tensor(f"MM{i}", [128, 512], F32)) for i in range(2)]
        PB = [ctx.enter_context(nc.psum_tensor(f"PB{i}", [128, 512], F32)) for i in range(4)]

        IMG = sb("IMG", [128, GB, POS])
        U = sb("U", [128, SIDE * 2 * MODES])
        COORDS = U[0:Q4 * 3, 0:HALF]
        ROW = U[0:Q4, 0:HALF]
        SPEC = sb("SPEC", [128, GB, 2 * MODES * MODES])
        TURN = sb("TURN", [128, 2, 512])
        AREAF = sb("AREAF", [128, KW2 * 128])
        TURN3 = AREAF[0:80, :].rearrange("p (k n) -> p k n", n=128)
        FHID = AREAF[:, 0:1024].rearrange("p (a n) -> p a n", a=2)
        SW = sb("SW", [128, 2, KHC * MODES, WID])
        CONV = sb("CONV", [128, 129])
        F1, F2, G3, G4 = (sb(n, s) for n, s in (("F1", [128, 80]), ("F2", [128, 40]), ("G3", [80, 256]), ("G4", [80, 128])))
        FW0 = sb("FW0", [Q4 * 3, 128]); FB0 = sb("FB0", [128, 1])
        FW1 = sb("FW1", [128, 2, 128]); FB1 = sb("FB1", [128, 1])
        FW2 = sb("FW2", [128, 2, 4]); FB2 = sb("FB2", [4, 1])

        WRNN = sb("WRNN", [128, D]); BRNN = sb("BRNN", [128, 2]); BSUM = sb("BSUM", [128, 1])
        GW = sb("GW", [65, E]); W1 = sb("W1E", [65, E * FF]); W2 = sb("W2E", [128, 2 * E * D]); B2 = sb("B2E", [1, E * D])
        WQ = sb("WQ", [64, H * D]); WK = sb("WK", [64, D]); WV = sb("WV", [64, D]); WOT = sb("WOT", [128, 4, D])
        WPK = sb("WPK", [64, 512]); KB = sb("KB", [128, 4, 256]); WQ5 = sb("WQ5", [64, 512]); WO5 = sb("WO5", [128, H, D])
        ID = sb("IDB", [128, 128]); TRI = sb("TRI", [128, 128]); ONES = sb("ONES", [128, 128])
        IOTA = sb("IOTA", [128, NC50]); EIGHT = sb("EIGHT", [128, E]); HBASE = sb("HBASE", [128, H])
        LATER = sb("LATER", [128, D], I32); NEG = sb("NEG", [128, 1]); BIG = sb("BIG", [128, 2])
        AREA1 = sb("AREA1", [128, 24 * SEQ + 64]); AREA2 = sb("AREA2", [128, H * TOK]); AREA3 = sb("AREA3", [128, 4 * TOK]); AREA4 = sb("AREA4", [128, 3 * 512])
        X = sb("XH", [128, NT3, D]); N = sb("N", [128, NT3, D]); TMP = sb("TMP", [128, NT3, D])
        ST = sb("ST", [128, 6, NT3]); RS = sb("RS", [128, 2, SEQ]); NTR = sb("NTR", [65, TOK]); NT4 = sb("NT4", [64, TOK])
        LG = sb("LG", [128, NT3, E]); LE = sb("LE", [128, NT3, E]); OH = sb("OH", [128, NT3, E]); OHS = sb("OHS", [128, E])
        G1 = sb("G1", [128, 8, NT3]); HID = AREA3[:, 0:4 * TOK].rearrange("p (s n) -> p s n", s=4); Y = sb("Y", [128, NT3, D]); YM = sb("YM", [128, NT3, D])
        QT = AREA2[0:64, :].rearrange("p (h n) -> p h n", h=H); KT = sb("KT", [64, TOK]); VC = sb("VC", [64, TOK])
        P = AREA1[:, 0:24 * SEQ].rearrange("p (r t) -> p r t", t=SEQ); NM = sb("NM", [128, 24]); DEN = sb("DEN", [128, 24]); WON = AREA3[:, 0:12 * D].rearrange("p (r d) -> p r d", d=D); Z = AREA3[0:64, 12 * D:12 * D + 3 * SEQ].rearrange("p (c t) -> p c t", c=3)
        QPK = AREA2[:, 0:4 * TOK].rearrange("p (r t) -> p r t", t=TOK); SIM = AREA1[:, 0:3072].rearrange("p (t a k) -> p t a k", t=NT3, a=2)
        SIMR = AREA4[:, 0:1024].rearrange("p (a k) -> p a k", a=2); V16 = sb("V16", [128, 2, H, TOPK]); I16 = sb("I16", [128, 2, H, TOPK], U32); IF = sb("IF", [128, 2, H, TOPK])
        C50, CI, CR = (AREA2[:, 1536 + 400 * n:1936 + 400 * n].rearrange("p (h c) -> p h c", h=H) for n in range(3))
        FV = sb("FV", [128, H, TOPK]); FP = sb("FP", [128, H, TOPK], U32); PF = sb("PF", [128, H, TOPK]); EQ = AREA1[:, 3072:4672].rearrange("p (k c) -> p k c", c=NC50)
        FS = sb("FS", [128, H, TOPK]); S8 = sb("S8", [128, 2, H])
        IDXN = sb("IDXN", [128, NT3, H, TOPK], I32); WTN = sb("WTN", [128, NT3, H, TOPK])
        IDX = sb("IDX", [128, NT3, H, TOPK], I32); WT = sb("WT", [128, NT3, H, TOPK]); XC = sb("XC", [128, NT3, D]); NTC = sb("NTC", [64, TOK])
        GATH = sb("GATH", [128, RING, TOPK, 2 * D]); KV = sb("KV", [128, NT3, H, 2 * D])
        Q5 = QT; KVT = AREA1[:, 0:3072].rearrange("p (h n) -> p h n", h=H); VW = AREA3[:, :].rearrange("p (t h d) -> p t h d", t=NT3, h=H)
        P5 = AREA1[:, 3072:4608].rearrange("p (s h t) -> p s h t", s=2, h=4); NM5 = sb("NM5", [128, 2, 4]); DEN5 = sb("DEN5", [128, 2, 4]); PT = AREA4[:, :].rearrange("p (s n) -> p s n", s=3)
        OUTB = sb("OUTB", [128, NT3, D])

        full = {(k, b): sem(f"{k}_full{b}") for k in PLANS for b in range(4)}
        empt = {(k, b): sem(f"{k}_out{b}") for k in PLANS for b in range(4)}
        PER = {"x_in": 80, "normed": 4, "shifted": 1, "exped": 1, "one_hot": 1, "h_kept": 1, "maxed": 24, "masked": 12,
               "rden": 2, "shift_top": NT3, "exp_top": NT3, "selected": 1, "kept_idx": 1, "kept_x": 1,
               "gather_free": NT3 * H, "weighted": 1, "maxed5": 12, "scaled5": 6, "out_sb": 1, "stored": 16, "multiplied": NT3 * H}
        S = {n: sem(n) for n in PER}
        gath = [sem(f"gathered{r}") for r in range(RING)]
        const_in, zeroed = sem("weights_in"), sem("buffers_zeroed")
        coords_in = sem("coords_in"); sw_in = [sem("sw_in0"), sem("sw_in1")]; conv_in = sem("conv_in")
        tp_full = sem("turned"); tp_out = sem("turned_out"); mm_full = sem("multiplied_full"); mm_out = sem("multiplied_out")
        row_out = sem("tokens_stored")
        passed = {x: sem(f"{x}_passed") for x in ("PE", "DVE", "Pool")}
        block = ctx.enter_context(nc.Block())

        def fence(e):
            e.sem_inc(passed[str(e.engine).split(".")[-1]], 1)


        def event(name, it, k):
            return S[name], (it + 1) * PER[name] + k

        def filled(kind, it, name, k=0):
            b, n = number(PLANS[kind], name, k)
            return full[kind, b], (it + 1) * total(PLANS[kind], b) + n + 1

        def emptied(kind, it, name, k=0):
            b, n = number(PLANS[kind], name, k)
            return empt[kind, b], (it + 1) * total(PLANS[kind], b) + n + 1

        def free(kind, it, name, k=0):
            b, n = number(PLANS[kind], name, k)
            return empt[kind, b], (it + 1) * total(PLANS[kind], b) + n

        def bank(kind, name):
            return number(PLANS[kind], name, 0)[0]

        def credits(e, names, banks=()):
            for n in names: e.sem_inc(S[n], PER[n])
            for k, b in banks:
                e.sem_inc(full[k, b], total(PLANS[k], b)); e.sem_inc(empt[k, b], total(PLANS[k], b))
        tokv = tok.rearrange("b (h w) -> (b h) w", w=D)

        def mm_group(g): return M_GROUP * g
        def mm_layer(g, l): return M_GROUP * g + M_IN + M_LAYER * l
        def tp_layer(g, l): return T_GROUP * g + T_LAYER * l
        def mm_last(g): return M_GROUP * g + M_IN + LAYERS * M_LAYER
        def tp_last(g): return T_GROUP * g + LAYERS * T_LAYER

        def sp_coords(e, g):
            for n in range(2 * GB):
                if n: e.wait_ge(mm_full, CREDIT + mm_group(g) + ROWQ // 2 * n)
                else: e.wait_ge(row_out, 16 * 2 * GB * g + 16)
                e.dma_start(COORDS, xT[bass.ds((g * GB + n // 2) * (Q4 * 3), Q4 * 3), HALF * (n % 2):HALF * (n % 2) + HALF]).then_inc(coords_in, 16)

        def sp_chunk(e, g, l, c):
            for a in range(Q4):
                e.dma_start(SW[32 * a:32 * a + 32, c % 2, :, :].rearrange("p m o -> p (m o)"),
                            sw[bass.ds((l * CHUNKS + c) * WID, WID), :]).then_inc(sw_in[c % 2], 16)

        def sp_forward(e, g, l):
            e.wait_ge(mm_full, CREDIT + mm_layer(g, l))
            sp_chunk(e, g, l, 0)
            sp_chunk(e, g, l, 1)
            e.wait_ge(mm_out, CREDIT + mm_layer(g, l))
            for a in range(Q4):
                r = slice(32 * a, 32 * a + 32)
                e.dma_start(CONV[r, r], cwb[bass.ds(l * WID, WID), 0:WID]).then_inc(conv_in, 16)
                e.dma_start(CONV[r, 128:129], cwb[bass.ds(l * WID, WID), WID:WID + 1], allow_slow_non_contiguous=True).then_inc(conv_in, 16)

        def sp_mix(e, g, l):
            for c in range(2, CHUNKS):
                e.wait_ge(mm_full, CREDIT + mm_layer(g, l) + GB * F_T + c - 1)
                sp_chunk(e, g, l, c)

        def sp_tokens(e, g):
            for n in range(2 * GB):
                e.wait_ge(tp_out, CREDIT + tp_last(g) + ROWQ // 2 * (n + 1))
                e.dma_start(tok[bass.ds((g * GB + n // 2) * Q4, Q4), HALF * (n % 2):HALF * (n % 2) + HALF], ROW).then_inc(row_out, 16)

        def t_coords(e, g):
            for n in range(GB * ROWQ):
                if n % (ROWQ // 2) == 0:
                    e.wait_ge(coords_in, g * (2 * GB * 16) + 16 * (n // (ROWQ // 2)) + 16)
                c = n % (ROWQ // 2)
                p = mm_slot(e, mm_group(g), n)
                fence(e)
                e.matmul(p[:, :], FW0[:, :], COORDS[:, 512 * c:512 * c + 512], start=True, stop=True).then_inc(mm_full, 1)

        def mm_slot(e, base, n):
            e.wait_ge(mm_out, CREDIT + base + n - 1)
            return MM[n % 2]
        def tp_slot(e, base, n):
            e.wait_ge(tp_out, CREDIT + base + n - 1)
            return TP[n % 2]
        def t_forward(e, g, l, q):
            tb, mb = tp_layer(g, l) + q * F_T, mm_layer(g, l) + q * F_T
            if q == 0:
                e.wait_ge(mm_out, CREDIT + mb)
            def turn(c):
                t = tp_slot(e, tb, c)
                for j in range(4):
                    m = e.transpose(t[:, 128 * j:128 * j + 128], IMG[:, q, 512 * c + 128 * j:512 * c + 128 * j + 128], ID[:, :])
                m.then_inc(tp_full, 1)
            def along_w(c):
                e.wait_ge(tp_out, CREDIT + tb + c + 1)
                p = mm_slot(e, mb, c)
                for j in range(4):
                    m = e.matmul(p[:, 80 * j:80 * j + 80], TURN[:, c % 2, 128 * j:128 * j + 128], F1[:, :], start=True, stop=True)
                m.then_inc(mm_full, 1)
            turn(0)
            for c in range(ROWQ):
                if c + 1 < ROWQ: turn(c + 1)
                along_w(c)
            e.wait_ge(mm_out, CREDIT + mb + ROWQ)
            Uv = U[:, :].rearrange("p (k m) -> p k m", k=MODES)
            def turn2(i):
                t = tp_slot(e, tb, ROWQ + i)
                for j in range(KWG[i][1]):
                    m = e.transpose(t[:, 128 * j:128 * j + 128], Uv[:, KWG[i][0] + j, :], ID[:, :])
                m.then_inc(tp_full, 1)
            def along_h(i):
                e.wait_ge(tp_out, CREDIT + tb + ROWQ + i + 1)
                p = mm_slot(e, mb, ROWQ + i)
                for j in range(KWG[i][1]):
                    m = e.matmul(p[:, 40 * j:40 * j + 40], TURN[:, (ROWQ + i) % 2, 128 * j:128 * j + 128], F2[:, :], start=True, stop=True)
                m.then_inc(mm_full, 1)
            turn2(0)
            for i in range(len(KWG)):
                if i + 1 < len(KWG): turn2(i + 1)
                along_h(i)
        def t_mix(e, g, l):
            mb = mm_layer(g, l) + GB * F_T
            e.wait_ge(mm_out, CREDIT + mb)
            Sv = SPEC[:, :, :].rearrange("p q (m r) -> p q m r", r=2)
            for c in range(CHUNKS):
                e.wait_ge(sw_in[c % 2], (g * LAYERS + l) * (64 * CHUNKS // 2) + 64 * (c // 2) + 64)
                p = mm_slot(e, mb, c)
                fence(e)
                pv = p[:, 0:4 * MODES * KHC].rearrange("p (q m r) -> p q m r", q=GB, r=2)
                for kw in range(MODES):
                    for k5 in range(KHC):
                        m_at = kw * MODES + c * KHC + k5
                        for a in range(Q4):
                            r = slice(32 * a, 32 * a + 32)
                            m = e.matmul(pv[r, :, kw * KHC + k5, :], SW[r, c % 2, k5 * MODES + kw, :], Sv[r, :, m_at, :], start=True, stop=True)
                m.then_inc(mm_full, 1)
        def t_inverse(e, g, l, q):
            tb = tp_layer(g, l) + GB * F_T + q * I_T
            mb = mm_layer(g, l) + GB * F_T + CHUNKS + q * I_M
            if q == 0:
                e.wait_ge(mm_out, CREDIT + mb)
            for i, (k0, n) in enumerate(TG):
                t = tp_slot(e, tb, i)
                for j in range(n):
                    m = e.transpose(t[0:80, 128 * j:128 * j + 128], SPEC[:, q, 80 * (k0 + j):80 * (k0 + j) + 80], ID[:, :])
                m.then_inc(tp_full, 1)
            for i in range(KW2):
                for gi, (k0, n) in enumerate(TG):
                    if k0 == i: e.wait_ge(tp_out, CREDIT + tb + gi + 1)
                p = mm_slot(e, mb, i)
                e.matmul(p[:, 0:256], TURN3[:, i, :], G3[:, :], start=True, stop=True).then_inc(mm_full, 1)
            e.wait_ge(mm_out, CREDIT + mb + KW2)
            if q == 0:
                e.wait_ge(conv_in, (g * LAYERS + l) * 128 + 128)
            def turn4(c):
                t = tp_slot(e, tb, len(TG) + c)
                for j in range(4):
                    m = e.transpose(t[0:80, 128 * j:128 * j + 128], U[:, 80 * (4 * c + j):80 * (4 * c + j) + 80], ID[:, :])
                m.then_inc(tp_full, 1)
            def back_w(c):
                p = mm_slot(e, mb, KW2 + c)
                e.matmul(p[:, :], CONV[:, 0:128], IMG[:, q, 512 * c:512 * c + 512], start=True, stop=False, skip_group_check=True)
                e.wait_ge(tp_out, CREDIT + tb + len(TG) + c + 1)
                for j in range(4):
                    m = e.matmul(p[:, 128 * j:128 * j + 128], TURN[0:80, c % 2, 128 * j:128 * j + 128], G4[:, :], start=False, stop=True, skip_group_check=True)
                m.then_inc(mm_full, 1)
            turn4(0)
            for c in range(ROWQ):
                if c + 1 < ROWQ: turn4(c + 1)
                back_w(c)
        def t_tokens(e, g):
            mb, tb = mm_last(g), tp_last(g)
            e.wait_ge(mm_out, CREDIT + mb)
            for n in range(GB * ROWQ):
                q, c = n // ROWQ, n % ROWQ
                for pr in range(2):
                    p = mm_slot(e, mb, 2 * n + pr)
                    e.matmul(p[:, :], FW1[:, pr, :], IMG[:, q, 512 * c:512 * c + 512], start=True, stop=True).then_inc(mm_full, 1)
                t = tp_slot(e, tb, n)
                for pr in range(2):
                    e.wait_ge(mm_out, CREDIT + mb + 2 * n + pr + 1)
                    fence(e)
                    m = e.matmul(t[0:4, :], FW2[:, pr, :], FHID[:, pr, :], start=(pr == 0), stop=(pr == 1))
                m.then_inc(tp_full, 1)

        def evac(e, base, n, dst, src, func=ACT.Copy, **kw):
            e.wait_ge(mm_full, CREDIT + base + n + 1)
            e.activation(dst, MM[n % 2][src] if not callable(src) else src(MM[n % 2]), func, **kw).then_inc(mm_out, 1)
        def a_forward(e, g, l, q):
            mb = mm_layer(g, l) + q * F_T
            Uf = U[:, :].rearrange("p (k h r) -> p h k r", k=MODES, r=2)
            for c in range(ROWQ):
                evac(e, mb, c, Uf[:, 8 * c:8 * c + 8, :, :], lambda m: m[:, 0:320].rearrange("p (h k r) -> p h k r", k=MODES, r=2))
            for i, (k0, n) in enumerate(KWG):
                evac(e, mb, ROWQ + i, SPEC[:, q, 40 * k0:40 * (k0 + n)], (slice(None), slice(0, 40 * n)))
        def a_mix(e, g, l):
            mb = mm_layer(g, l) + GB * F_T
            Sv = SPEC[:, :, :].rearrange("p q (w c r) -> p c q w r", w=MODES, c=CHUNKS)
            for c in range(CHUNKS):
                evac(e, mb, c, Sv[:, c, :, :, :],
                     lambda m: m[:, 0:4 * MODES * KHC].rearrange("p (q w r) -> p q w r", q=GB, w=MODES))
        def a_inverse(e, g, l, q):
            mb = mm_layer(g, l) + GB * F_T + CHUNKS + q * I_M
            Uv = U[:, :].rearrange("p (h k r) -> p k h r", k=KW2, r=4)
            for i in range(KW2):
                evac(e, mb, i, Uv[:, i, :, :], lambda m: m[:, 0:256].rearrange("p (h r) -> p h r", r=4))
            for c in range(ROWQ):
                evac(e, mb, KW2 + c, IMG[:, q, 512 * c:512 * c + 512], (slice(None), slice(None)), ACT.Gelu, bias=CONV[:, 128:129])
        def a_coords(e, g):
            for n in range(GB * ROWQ):
                evac(e, mm_group(g), n, IMG[:, n // ROWQ, 512 * (n % ROWQ):512 * (n % ROWQ) + 512], (slice(None), slice(None)), ACT.Identity, bias=FB0[:, :])

        def a_tokens(e, g):
            for n in range(GB * ROWQ):
                for pr in range(2):
                    e.wait_ge(tp_full, CREDIT + tp_last(g) + n)
                    evac(e, mm_last(g), 2 * n + pr, FHID[:, pr, :], (slice(None), slice(None)), ACT.Gelu, bias=FB1[:, :])

        def copy(e, base, n, dst, rows, cols):
            e.wait_ge(tp_full, CREDIT + base + n + 1)
            e.tensor_copy(dst, TP[n % 2][0:rows, 0:cols]).then_inc(tp_out, 1)
        def v_forward(e, g, l, q):
            tb, mb = tp_layer(g, l) + q * F_T, mm_layer(g, l) + q * F_T
            for c in range(ROWQ):
                e.wait_ge(mm_full, CREDIT + mb + c - 1)
                copy(e, tb, c, TURN[:, c % 2, :], 128, 512)
            for i, (k0, n) in enumerate(KWG):
                e.wait_ge(mm_full, CREDIT + mb + ROWQ + i - 1)
                copy(e, tb, ROWQ + i, TURN[:, i % 2, 0:128 * n], 128, 128 * n)
        def v_inverse(e, g, l, q):
            tb = tp_layer(g, l) + GB * F_T + q * I_T
            mb = mm_layer(g, l) + GB * F_T + CHUNKS + q * I_M
            e.wait_ge(mm_full, CREDIT + mb - ROWQ if q else mb)
            for i, (k0, n) in enumerate(TG):
                copy(e, tb, i, TURN3[:, k0:k0 + n, :].rearrange("p k n -> p (k n)"), 80, 128 * n)
            for c in range(ROWQ):
                e.wait_ge(mm_full, CREDIT + mb + KW2 + c - 1)
                copy(e, tb, len(TG) + c, TURN[0:80, c % 2, :], 80, 512)
        def v_tokens(e, g):
            for n in range(GB * ROWQ):
                e.wait_ge(tp_full, CREDIT + tp_last(g) + n + 1)
                if n % (ROWQ // 2) == 0:
                    e.wait_ge(row_out, 16 * (2 * GB * g + n // (ROWQ // 2)) + 16)
                c = n % (ROWQ // 2)
                e.tensor_scalar(ROW[:, 512 * c:512 * c + 512], TP[n % 2][0:4, :], FB2[:, :], None, ALU.add).then_inc(tp_out, 1)

        def sp_setup(e):
            credits(e, ["x_in", "stored"])
            e.sem_inc(row_out, 16)
            e.wait_ge(zeroed, 9)
            n = [0]
            def load(d, s, **k):
                e.dma_start(d, s, **k).then_inc(const_in, 16); n[0] += 1
            load(WRNN[:, :], wrnn)
            for i in range(2): load(BRNN[64:128, i:i + 1], brnn[i, :].rearrange("(a b) -> a b", b=1))
            for d, s in ((GW, gw), (W1, w1), (W2, w2), (B2, b2), (WQ, wq), (WK, wk), (WV, wv), (WPK, wpk), (WQ5, wq5),
                         (ID, ident_in), (TRI, tri_in), (IOTA, iota_in), (EIGHT, eight_in), (HBASE, hbase_in), (LATER, later_in)):
                load(d[:, :], s)
            load(WOT[:, :, :].rearrange("p a b -> p (a b)"), wot)
            load(WO5[64:128, :, :].rearrange("p a b -> p (a b)"), wo5)
            for p in range(2):
                for h in range(H):
                    load(KB[32 * (h % 4):32 * (h % 4) + 32, 2 * p + h // 4, 64 * (h % 4):64 * (h % 4) + 64], keysT[(p * H + h) * 32:(p * H + h) * 32 + 32, :])
            for d, s in ((F1, f1), (F2, f2), (G3, g3), (G4, g4)):
                load(d[:, :], s)
            for a in range(Q4):
                load(FW0[3 * a:3 * a + 3, 32 * a:32 * a + 32], fc0[0:3, :])
                load(FB0[32 * a:32 * a + 32, :], fc0[3, :].rearrange("(a b) -> a b", b=1))
                load(FW1[32 * a:32 * a + 32, a // 2, 64 * (a % 2):64 * (a % 2) + 64], fc1[0:WID, :])
                load(FW2[64 * (a % 2):64 * (a % 2) + 64, a // 2, a:a + 1], fc2[0:64, :])
                load(FB2[a:a + 1, :], fc2[64:65, :])
            for a in range(2):
                load(FB1[64 * a:64 * a + 64, :], fc1[WID, :].rearrange("(a b) -> a b", b=1))
            assert n[0] == NLOADS, n[0]
        NLOADS = 1 + 2 + 15 + 2 + 16 + 4 + 5 * Q4 + 2

        def sp_front(e, j, stored):
            e.wait_ge(*event("kept_x", j - 1, 1))
            e.wait_ge(row_out, 16 * 2 * GB * stored + 16)
            for d, s in ((X[0:64, 0, :], tokv[bass.ds(j * 128, 64), :]), (X[64:128, 0, :], txt[bass.ds(j * 256, 64), :]),
                         (X[0:64, 1, :], txt[bass.ds(j * 256 + 64, 64), :]), (X[64:128, 1, :], tokv[bass.ds(j * 128 + 64, 64), :]),
                         (X[:, 2, :], txt[bass.ds(j * 256 + 128, 128), :])):
                e.dma_start(d, s).then_inc(S["x_in"], 16)

        def sp_back(e, i):
            e.wait_ge(*event("out_sb", i, 1))
            e.dma_start(out[bass.ds(i * TOK, TOK), :].rearrange("(t p) d -> p t d", p=128), OUTB[:, :, :]).then_inc(S["stored"], 16)

        def pool_gather(e, i):
            e.wait_ge(*event("kept_idx", i, 1))
            for u in range(NT3 * H):
                r = u % RING
                e.wait_ge(*event("gather_free", i, u + 1 - RING))
                fence(e)
                for k in range(TOPK):
                    e.indirect_dma_start(GATH[:, r, k, :], None, table, bass.IndirectOffsetOnAxis(IDX[:, u // H, u % H, k:k + 1], 0)).then_inc(gath[r], 16)

        def bc(ap, n):
            return ap.rearrange("p (t o) -> p t o", o=1).to_broadcast([ap.shape[0], ap.shape[1], n])

        def normalize(e):
            mean, var, y, a, b, c = (ST[:, i, :] for i in range(6))
            e.drain()
            e.tensor_reduce(mean, X[:, :, :], AX.X, ALU.add); e.drain()
            e.tensor_scalar(mean, mean, 1.0 / D, None, ALU.mult); e.drain()
            e.tensor_tensor(N[:, :, :], X[:, :, :], bc(mean, D), ALU.subtract); e.drain()
            e.tensor_tensor(TMP[:, :, :], N[:, :, :], N[:, :, :], ALU.mult); e.drain()
            e.tensor_reduce(var, TMP[:, :, :], AX.X, ALU.add); e.drain()
            e.tensor_scalar(var, var, 1.0 / D, EPS, ALU.mult, ALU.add); e.drain()
            e.tensor_scalar(a.bitcast(I32), var.bitcast(I32), 1, None, ALU.logical_shift_right); e.drain()
            e.tensor_scalar(y.bitcast(I32), a.bitcast(I32), -1.0, float(0x5F3759DF), ALU.mult, ALU.add); e.drain()
            for _ in range(4):
                e.tensor_tensor(b, y, y, ALU.mult); e.drain()
                e.tensor_tensor(c, b, var, ALU.mult); e.drain()
                e.tensor_scalar(c, c, -0.5, 1.5, ALU.mult, ALU.add); e.drain()
                e.tensor_tensor(y, y, c, ALU.mult); e.drain()
            e.tensor_tensor(N[:, :, :], N[:, :, :], bc(y, D), ALU.mult).then_inc(S["normed"], 1)

        def v_rnn(e, j):
            e.wait_ge(*event("x_in", j, 80))
            fence(e)
            normalize(e)
            e.wait_ge(*filled("front", j, "rnn_back"))
            e.tensor_tensor(X[:, :, :], X[:, :, :], PB[2][:, 0:192].rearrange("p (t d) -> p t d", d=D), ALU.add).then_inc(empt["front", 2], 1)

        def v_moe(e, j):
            normalize(e)
            e.wait_ge(*filled("front", j, "gate"))
            m, sm, r, pm, w, pos, keep, sc = (G1[:, i, :] for i in range(8))
            L = PB[1][:, 0:24].rearrange("p (t e) -> p t e", e=E)
            e.tensor_reduce(m, L, AX.X, ALU.max); e.drain()
            e.tensor_tensor(LG[:, :, :], L, bc(m, E), ALU.subtract).then_inc(empt["front", 1], 1)
            e.wait_ge(*emptied("front", j, "gate"))
            fence(e)
            e.drain().then_inc(S["shifted"], 1)
            e.memset(Y[:, :, :], 0.0)
            e.wait_ge(*event("exped", j, 1))
            e.tensor_reduce(sm, LE[:, :, :], AX.X, ALU.add); e.drain()
            e.reciprocal(r, sm); e.drain()
            e.tensor_tensor(LE[:, :, :], LE[:, :, :], bc(r, E), ALU.mult); e.drain()
            e.tensor_reduce(pm, LE[:, :, :], AX.X, ALU.max); e.drain()
            e.tensor_tensor(LG[:, :, :], LE[:, :, :], bc(pm, E), ALU.is_equal); e.drain()
            e.tensor_tensor(LG[:, :, :], LG[:, :, :], EIGHT[:, :].rearrange("p (o e) -> p o e", o=1).to_broadcast([128, NT3, E]), ALU.mult); e.drain()
            e.tensor_reduce(w, LG[:, :, :], AX.X, ALU.max); e.drain()
            e.tensor_tensor(OH[:, :, :], LG[:, :, :], bc(w, E), ALU.is_equal).then_inc(S["one_hot"], 1)
            e.wait_ge(*filled("front", j, "place"))
            e.tensor_tensor(LG[:, :, :], PB[1][:, 0:24].rearrange("p (t e) -> p t e", e=E), OH[:, :, :], ALU.mult).then_inc(empt["front", 1], 1)
            for t in range(NT3):
                e.drain()
                e.tensor_tensor(OHS[:, :], OHS[:, :], OH[:, t, :], ALU.add)
            e.drain()
            e.tensor_reduce(pos, LG[:, :, :], AX.X, ALU.add); e.drain()
            e.tensor_scalar(keep, pos, float(CAP), None, ALU.is_le); e.drain()
            e.tensor_tensor(sc, keep, pm, ALU.mult)
            for x in range(E):
                name = ("expert", "expertB")[x % 2]
                e.wait_ge(*filled("front", j, name, x // 2))
                fence(e)
                e.drain()
                b = bank("front", name)
                e.copy_predicated(Y[:, :, :], OH[:, :, x:x + 1].to_broadcast([128, NT3, D]).bitcast(I32),
                                  PB[b][:, 0:192].rearrange("p (t d) -> p t d", d=D)).then_inc(empt["front", b], 1)
            e.drain()
            e.tensor_tensor(Y[:, :, :], Y[:, :, :], bc(sc, D), ALU.mult); e.drain()
            e.tensor_tensor(YM[:, :, :], Y[:, :, :], Y[:, :, :], ALU.is_equal)
            e.memset(TMP[:, :, :], 0.0); e.drain()
            e.copy_predicated(TMP[:, :, :], YM[:, :, :].bitcast(I32), Y[:, :, :]); e.drain()
            e.tensor_scalar(YM[:, :, :], TMP[:, :, :], FMAX, None, ALU.is_gt); e.drain()
            e.copy_predicated(TMP[:, :, :], YM[:, :, :].bitcast(I32), BIG[:, 0:1].rearrange("p (a b) -> p a b", b=1).to_broadcast([128, NT3, D])); e.drain()
            e.tensor_scalar(YM[:, :, :], TMP[:, :, :], -FMAX, None, ALU.is_lt); e.drain()
            e.copy_predicated(TMP[:, :, :], YM[:, :, :].bitcast(I32), BIG[:, 1:2].rearrange("p (a b) -> p a b", b=1).to_broadcast([128, NT3, D])); e.drain()
            e.tensor_tensor(X[:, :, :], X[:, :, :], TMP[:, :, :], ALU.add)

        def v_att(e, j):
            normalize(e)
            for n in range(5):
                e.wait_ge(*filled("front", j, "qkvB", n))
                dst = QT[:, 2 * n + 1, :] if n < 4 else VC[:, :]
                if n < 4:
                    ins = e.tensor_scalar(dst, PB[3][0:64, 0:TOK], float(1 / np.sqrt(np.float32(8))), None, ALU.mult)
                else:
                    ins = e.tensor_copy(dst, PB[3][0:64, 0:TOK])
                ins.then_inc(empt["front", 3], 1)
            def finish(b):
                e.wait_ge(*emptied("front", j, "scoreB", 3 * b + 2)); e.wait_ge(*emptied("front", j, "scoreA", 3 * b + 2))
                if b: e.wait_ge(*free("front", j, "z2", b)); e.wait_ge(*emptied("front", j, "z2", 0))
                e.reciprocal(DEN[:, 12 * b:12 * b + 12], DEN[:, 12 * b:12 * b + 12]); e.drain()
                e.tensor_tensor(WON[:, :, :].rearrange("p (a c) d -> p a c d", a=3),
                                WOT[:, :, :].rearrange("p (o c) d -> p o c d", o=1).to_broadcast([128, 3, 4, D]),
                                DEN[:, 12 * b:12 * b + 12].rearrange("p (a c o) -> p a c o", a=3, o=1).to_broadcast([128, 3, 4, D]),
                                ALU.mult).then_inc(S["rden"], 1)
            def z_out(b):
                e.wait_ge(*filled("front", j, "z", b))
                e.wait_ge(*filled("front", j, "z2", b))
                if b: e.wait_ge(*filled("front", j, "z2", b))
                e.tensor_copy(Z[:, 0:2, :].rearrange("p a b -> p (a b)"), PB[0][0:64, 0:384]).then_inc(empt["front", 0], 1)
                e.tensor_copy(Z[:, 2, :], PB[1][0:64, 0:192]).then_inc(empt["front", 1], 1)
            for n in range(12):
                name = ("scoreA", "scoreB")[n % 2]
                e.wait_ge(*filled("front", j, name, n // 2))
                e.tensor_reduce(NM[:, 2 * n:2 * n + 2], PB[bank("front", name)][:, 0:384].rearrange("p (a t) -> p a t", t=SEQ), AX.X, ALU.max, negate=True).then_inc(S["maxed"], 2)
                if n == 7: finish(0)
            z_out(0)
            finish(1)
            z_out(1)
            e.wait_ge(*filled("front", j, "att"))
            e.tensor_tensor(X[:, :, :], X[:, :, :], PB[2][:, 0:192].rearrange("p (t d) -> p t d", d=D), ALU.add).then_inc(empt["front", 2], 1)

        def v_pk(e, j):
            normalize(e)
            for n in range(2):
                e.wait_ge(*filled("front", j, "qpkB", n))
                e.tensor_copy(QPK[:, 2 * n + 1, :], PB[3][:, 0:TOK]).then_inc(empt["front", 3], 1)
            for t in range(NT3):
                e.wait_ge(*filled("front", j, "simB", t))
                e.tensor_copy(SIM[:, t, 1, :], PB[3][:, :]).then_inc(empt["front", 3], 1)

        def v_top(e, j, cut=lambda n: None):
            for t in range(NT3):
                e.wait_ge(*emptied("front", j, "simA", t))
                fence(e)
                lists = [(p, h) for p in range(2) for h in range(H)]
                e.drain()
                for p, h in lists: e.max(V16[:, p, h, 0:8], SIM[:, t, p, 64 * h:64 * h + 64])
                e.drain()
                for p, h in lists:
                    e.match_replace(SIMR[:, p, 64 * h:64 * h + 64], V16[:, p, h, 0:8], SIM[:, t, p, 64 * h:64 * h + 64], -FMAX)
                    e.max_index(I16[:, p, h, 0:8], V16[:, p, h, 0:8], SIM[:, t, p, 64 * h:64 * h + 64])
                e.drain()
                for p, h in lists: e.max(V16[:, p, h, 8:16], SIMR[:, p, 64 * h:64 * h + 64])
                e.drain()
                for p, h in lists: e.max_index(I16[:, p, h, 8:16], V16[:, p, h, 8:16], SIMR[:, p, 64 * h:64 * h + 64])
                e.drain()
                cut(1)
                e.tensor_copy(IF[:, :, :, :].rearrange("p a h k -> p (a h k)"), I16[:, :, :, :].rearrange("p a h k -> p (a h k)")); e.drain()
                e.tensor_scalar(IF[:, 1, :, :], IF[:, 1, :, :], float(NK), None, ALU.mult); e.drain()
                e.tensor_tensor(IF[:, 1, :, :], IF[:, 1, :, :], HBASE[:, :].rearrange("p (h o) -> p h o", o=1).to_broadcast([128, H, TOPK]), ALU.add); e.drain()
                for src, dst in ((V16, C50), (IF, CI)):
                    at = 0
                    for i in range(8):
                        m = CAND[i]
                        e.tensor_tensor(dst[:, :, at:at + m], src[:, 0, :, i:i + 1].to_broadcast([128, H, m]), src[:, 1, :, 0:m], ALU.add)
                        at += m
                    e.tensor_tensor(dst[:, :, at:at + 8], src[:, 0, :, 8:16], src[:, 1, :, 0:1].to_broadcast([128, H, 8]), ALU.add)
                e.drain()
                for h in range(H): e.max(FV[:, h, 0:8], C50[:, h, :])
                e.drain()
                for h in range(H):
                    e.match_replace(CR[:, h, :], FV[:, h, 0:8], C50[:, h, :], -FMAX)
                    e.max_index(FP[:, h, 0:8], FV[:, h, 0:8], C50[:, h, :])
                e.drain()
                for h in range(H): e.max(FV[:, h, 8:16], CR[:, h, :])
                e.drain()
                for h in range(H): e.max_index(FP[:, h, 8:16], FV[:, h, 8:16], CR[:, h, :])
                e.tensor_tensor(FS[:, :, :], FV[:, :, :], FV[:, :, 0:1].to_broadcast([128, H, TOPK]), ALU.subtract); e.drain().then_inc(S["shift_top"], 1)
                e.tensor_copy(PF[:, :, :], FP[:, :, :]); e.drain()
                for g in range(H // 2):
                    e.tensor_tensor(EQ[:, :, :], IOTA[:, :].rearrange("p (o c) -> p o c", o=1).to_broadcast([128, 2 * TOPK, NC50]),
                                    PF[:, 2 * g:2 * g + 2, :].rearrange("p h (k o) -> p (h k) o", o=1).to_broadcast([128, 2 * TOPK, NC50]), ALU.is_equal); e.drain()
                    e.tensor_tensor(EQ[:, :, :].rearrange("p (h k) c -> p h k c", h=2), EQ[:, :, :].rearrange("p (h k) c -> p h k c", h=2),
                                    CI[:, 2 * g:2 * g + 2, :].rearrange("p h (o c) -> p h o c", o=1).to_broadcast([128, 2, TOPK, NC50]), ALU.mult); e.drain()
                    e.tensor_reduce(PF[:, 2 * g:2 * g + 2, :].rearrange("p h k -> p (h k)"), EQ[:, :, :], AX.X, ALU.add); e.drain()
                e.tensor_copy(IDXN[:, t, :, :], PF[:, :, :])
                e.wait_ge(*event("exp_top", j, t + 1))
                e.tensor_reduce(S8[:, 0, :], FS[:, :, :], AX.X, ALU.add); e.drain()
                e.reciprocal(S8[:, 1, :], S8[:, 0, :]); e.drain()
                e.tensor_tensor(WTN[:, t, :, :], FS[:, :, :], S8[:, 1, :].rearrange("p (h o) -> p h o", o=1).to_broadcast([128, H, TOPK]), ALU.mult)
                cut(2)
            e.drain().then_inc(S["selected"], 1)

        def a_consume(e, i, u):
            r = u % RING
            e.wait_ge(gath[r], (i * (NT3 * H // RING) + u // RING + 1) * 16 * TOPK)
            e.wait_ge(*event("kept_idx", i, 1))
            for k in range(TOPK):
                m = e.activation(GATH[:, r, k, :], GATH[:, r, k, :], ACT.Copy, scale=WT[:, u // H, u % H, k:k + 1])
            m.then_inc(S["multiplied"], 1)

        def v_consume(e, i, u):
            e.wait_ge(*event("multiplied", i, u + 1))
            e.tensor_reduce(KV[:, u // H, u % H, :], GATH[:, u % RING, :, :].rearrange("p k d -> p d k"), AX.X, ALU.add).then_inc(S["gather_free"], 1)

        def v_keep_idx(e):
            e.drain()
            e.tensor_copy(IDX[:, :, :, :].rearrange("p a b c -> p (a b c)"), IDXN[:, :, :, :].rearrange("p a b c -> p (a b c)"))
            e.tensor_copy(WT[:, :, :, :].rearrange("p a b c -> p (a b c)"), WTN[:, :, :, :].rearrange("p a b c -> p (a b c)"))
            e.drain().then_inc(S["kept_idx"], 1)

        def v_keep_x(e, j):
            e.drain()
            e.wait_ge(*emptied("front", j, "pkT"))
            e.tensor_copy(XC[:, :, :], X[:, :, :])
            e.tensor_copy(NTC[:, :], NT4[:, :])
            e.drain().then_inc(S["kept_x"], 1)

        def v_back(e, i):
            e.drain().then_inc(S["weighted"], 1)
            for n in range(4):
                e.wait_ge(*filled("back", i, "q5B", n))
                e.tensor_scalar(Q5[:, 2 * n + 1, :], PB[3][0:64, 0:TOK], D ** -0.5, None, ALU.mult).then_inc(empt["back", 3], 1)
            for n in range(3):
                e.wait_ge(*filled("back", i, "kvB", n))
                kvt_out(e, 2 * n + 1).then_inc(empt["back", 3], 1)
            for n in range(12):
                b, ib, half = n // 6, n // 2 % 3, n % 2
                name = ("s5A", "s5B")[half]
                jn = 64 * (ib + 1)
                s = PB[bank("back", name)][:, 0:384].rearrange("p (a t) -> p a t", t=SEQ)
                e.wait_ge(*filled("back", i, name, n // 2))
                fence(e)
                e.copy_predicated(s[:, :, jn - 64:jn], LATER[:, :].rearrange("p (o c) -> p o c", o=1).to_broadcast([128, 2, D]),
                                  NEG[:, 0:1].rearrange("p (a b) -> p a b", b=1).to_broadcast([128, 2, D])); e.drain()
                sl = n // 2 % 2
                e.tensor_reduce(NM5[:, sl, 2 * half:2 * half + 2], s[:, :, 0:jn], AX.X, ALU.max, negate=True).then_inc(S["maxed5"], 1)
                if half == 0 and n > 0: v_scale5(e, i, n // 2 - 1)
                if half == 0 and n > 2: v_out5(e, i, n // 2 - 2)
            v_scale5(e, i, 5)
            v_out5(e, i, 4)
            v_out5(e, i, 5)
            e.drain().then_inc(S["out_sb"], 1)

        def v_out5(e, i, nb):
            e.wait_ge(*filled("back", i, "out", nb))
            if nb == 0: e.wait_ge(*event("stored", i - 1, 16))
            p, t = slice(64 * (nb % 2), 64 * (nb % 2) + 64), nb // 2
            e.tensor_tensor(OUTB[p, t, :], XC[p, t, :], PB[1][p, 64 * t:64 * t + 64], ALU.add).then_inc(empt["back", 1], 1)

        def v_scale5(e, i, nb):
            sl, jn = nb % 2, 64 * (nb % 3 + 1)
            e.wait_ge(*emptied("back", i, "s5A", nb)); e.wait_ge(*emptied("back", i, "s5B", nb))
            e.reciprocal(DEN5[:, sl, :], DEN5[:, sl, :]); e.drain()
            e.tensor_tensor(P5[:, sl, :, 0:jn], P5[:, sl, :, 0:jn], DEN5[:, sl, :].rearrange("p (h o) -> p h o", o=1).to_broadcast([128, 4, jn]), ALU.mult).then_inc(S["scaled5"], 1)

        def kvt_out(e, n):
            t, hh = n // 2, n % 2
            dst = KVT[:, 4 * hh:4 * hh + 4, 128 * t:128 * t + 128]
            src = PB[2 + n % 2][:, :].rearrange("p (h n) -> p h n", n=128)
            return e.tensor_copy(dst, src) if n % 2 else e.activation(dst, src, ACT.Copy)

        def a_rnn(e, j):
            e.wait_ge(*filled("front", j, "xT"))
            e.activation(RS[0:64, :, :].rearrange("p a b -> p (a b)"), PB[0][0:64, 0:TOK], ACT.Copy).then_inc(empt["front", 0], 1)
            for s in range(2):
                e.wait_ge(*filled("front", j, "rnn", s))
                e.activation(RS[64:128, 1 - s, :], PB[1][64:128, 0:SEQ], ACT.Tanh, bias=BSUM[64:128, :]).then_inc(empt["front", 1], 1)

        def a_moe(e, j):
            e.wait_ge(*filled("front", j, "moeT"))
            e.activation(NTR[0:64, :], PB[0][0:64, 0:TOK], ACT.Copy).then_inc(empt["front", 0], 1)
            e.wait_ge(*event("shifted", j, 1))
            e.activation(LE[:, :, :], LG[:, :, :], ACT.Exp).then_inc(S["exped"], 1)
            for n in range(16):
                name = ("hidA", "hidB")[n % 2]
                e.wait_ge(*filled("front", j, name, n // 2))
                e.activation(HID[:, n % 4, :], PB[2 + n % 2][:, 0:TOK], ACT.Relu).then_inc(empt["front", 2 + n % 2], 1)

        def a_att(e, j):
            e.wait_ge(*filled("front", j, "attT"))
            e.activation(NTR[0:64, :], PB[0][0:64, 0:TOK], ACT.Copy).then_inc(empt["front", 0], 1)
            for n in range(5):
                e.wait_ge(*filled("front", j, "qkvA", n))
                e.activation(QT[:, 2 * n, :] if n < 4 else KT[:, :], PB[2][0:64, 0:TOK], ACT.Copy, scale=float(1 / np.sqrt(np.float32(8))) if n < 4 else 1.0).then_inc(empt["front", 2], 1)
            for n in range(12):
                name = ("scoreA", "scoreB")[n % 2]
                e.wait_ge(*event("maxed", j, 2 * n + 2))
                for a in range(2):
                    ins = e.activation(P[:, 2 * n + a, :], PB[2 + n % 2][:, SEQ * a:SEQ * a + SEQ], ACT.Exp, bias=NM[:, 2 * n + a:2 * n + a + 1], accum_out=DEN[:, 2 * n + a:2 * n + a + 1])
                ins.then_inc(empt["front", 2 + n % 2], 1)

        def a_pk(e, j):
            e.wait_ge(*filled("front", j, "pkT"))
            e.wait_ge(*event("kept_x", j - 1, 1))
            e.activation(NT4[:, :], PB[0][0:64, 0:TOK], ACT.Copy).then_inc(empt["front", 0], 1)
            for n in range(2):
                e.wait_ge(*filled("front", j, "qpkA", n))
                e.activation(QPK[:, 2 * n, :], PB[2][:, 0:TOK], ACT.Copy).then_inc(empt["front", 2], 1)
            for t in range(NT3):
                e.wait_ge(*filled("front", j, "simA", t))
                e.activation(SIM[:, t, 0, :], PB[2][:, :], ACT.Copy).then_inc(empt["front", 2], 1)

        def a_top(e, j, cut=lambda n: None):
            for t in range(NT3):
                cut(1)
                e.wait_ge(*event("shift_top", j, t + 1))
                e.activation(FS[:, :, :], FS[:, :, :], ACT.Exp).then_inc(S["exp_top"], 1)
                cut(2)

        def a_back(e, i):
            for n in range(4):
                e.wait_ge(*filled("back", i, "q5A", n))
                e.activation(Q5[:, 2 * n, :], PB[2][0:64, 0:TOK], ACT.Copy, scale=D ** -0.5).then_inc(empt["back", 2], 1)
            for n in range(3):
                e.wait_ge(*filled("back", i, "kvA", n))
                kvt_out(e, 2 * n).then_inc(empt["back", 2], 1)
            for n in range(3):
                e.wait_ge(*filled("back", i, "vwA", n))
                e.activation(VW[:, n, :, :].rearrange("p h d -> p (h d)"), PB[2][:, :], ACT.Copy).then_inc(empt["back", 2], 1)
            for n in range(12):
                half, nb = n % 2, n // 2
                jn = 64 * (nb % 3 + 1)
                if half == 0 and nb >= 2: e.wait_ge(*emptied("back", i, "pt0", nb - 2))
                e.wait_ge(*event("maxed5", i, n + 1))
                for a in range(2):
                    hp = 2 * half + a
                    ins = e.activation(P5[:, nb % 2, hp, 0:jn], PB[2 + half][:, SEQ * a:SEQ * a + jn], ACT.Exp, bias=NM5[:, nb % 2, hp:hp + 1], accum_out=DEN5[:, nb % 2, hp:hp + 1])
                ins.then_inc(empt["back", 2 + half], 1)
                if half == 1 and nb >= 1: a_pt(e, i, nb - 1)
            a_pt(e, i, 5)

        def spans(nb):
            b, jn = nb // 3, 64 * (nb % 3 + 1)
            cut = (0, 128, 192) if b == 0 else (0, 64, 192)
            out = []
            for lo, hi in zip(cut, cut[1:]):
                hi = min(hi, jn)
                if hi > lo:
                    n = SEQ * b + lo
                    out.append((lo, hi, n % 128, n // 128))
            return out

        def slot(c, p0):
            return 2 if p0 else c

        def a_pt(e, i, nb):
            e.wait_ge(*filled("back", i, "pt0", nb))
            sp = spans(nb)
            for c, (lo, hi, p0, t) in enumerate(sp):
                ins = e.activation(PT[p0:p0 + hi - lo, slot(c, p0), :], PTB[c][p0:p0 + hi - lo, :], ACT.Copy)
            ins.then_inc(empt["back", 0], 1)
        PTB = [PB[0], PB[1]]


        def t_turn(e, j, name, k):
            e.wait_ge(*event("normed", j, k))
            e.wait_ge(*free("front", j, name))
            fence(e)
            for t in range(NT3):
                m = e.transpose(PB[0][0:64, 128 * t:128 * t + 128], N[:, t, :], ID[:, :])
            m.then_inc(full["front", 0], 1)

        def t_rnn(e, j):
            if not isinstance(j, int): e.wait_ge(*event("out_sb", j - 2, 1))
            t_turn(e, j, "xT", 1)
            e.wait_ge(*emptied("front", j, "xT"))
            for s in range(2):
                e.wait_ge(*free("front", j, "rnn", s))
                fence(e)
                e.matmul(PB[1][64:128, 0:SEQ], WRNN[:, :], RS[:, s, :], start=True, stop=True).then_inc(full["front", 1], 1)
            e.wait_ge(*emptied("front", j, "rnn", 1))
            e.wait_ge(*free("front", j, "rnn_back"))
            fence(e)
            i64 = ID[64:128, 64:128]
            e.transpose(PB[2][:, 0:64], RS[64:128, 1, 0:128], i64)
            e.transpose(PB[2][0:64, 64:128], RS[64:128, 1, 128:192], i64)
            e.matmul(PB[2][64:128, 64:128], RS[64:128, 0, 0:64], i64, start=True, stop=True)
            e.transpose(PB[2][:, 128:192], RS[64:128, 0, 64:192], i64).then_inc(full["front", 2], 1)

        def t_moe(e, j):
            t_turn(e, j, "moeT", 2)
            e.wait_ge(*emptied("front", j, "moeT"))
            e.wait_ge(*free("front", j, "gate"))
            fence(e)
            for t in range(NT3):
                m = e.matmul(PB[1][:, 8 * t:8 * t + 8], NTR[:, 128 * t:128 * t + 128], GW[:, :], start=True, stop=True)
            m.then_inc(full["front", 1], 1)
            def hid(n):
                name = ("hidA", "hidB")[n % 2]
                e.wait_ge(*free("front", j, name, n // 2))
                fence(e)
                e.matmul(PB[2 + n % 2][:, 0:TOK], W1[:, 128 * n:128 * n + 128], NTR[:, :], start=True, stop=True).then_inc(full["front", 2 + n % 2], 1)
            hid(0); hid(1)
            e.wait_ge(*event("one_hot", j, 1))
            e.wait_ge(*free("front", j, "place"))
            fence(e)
            for t in range(NT3):
                e.matmul(PB[1][:, 8 * t:8 * t + 8], TRI[:, :], OH[:, t, :], start=True, stop=False)
                for s in range(t):
                    e.matmul(PB[1][:, 8 * t:8 * t + 8], ONES[:, :], OH[:, s, :], start=False, stop=False)
                m = e.matmul(PB[1][:, 8 * t:8 * t + 8], ONES[:, :], OHS[:, :], start=False, stop=True)
            m.then_inc(full["front", 1], 1)
            for x in range(E):
                if x + 1 < E: hid(2 * x + 2); hid(2 * x + 3)
                name = ("expert", "expertB")[x % 2]
                b = bank("front", name)
                e.wait_ge(*free("front", j, name, x // 2))
                e.wait_ge(*emptied("front", j, "hidA", x)); e.wait_ge(*emptied("front", j, "hidB", x))
                fence(e)
                for t in range(NT3):
                    o = PB[b][:, 64 * t:64 * t + 64]
                    e.matmul(o, ONES[0:1, :], B2[:, 64 * x:64 * x + 64], start=True, stop=False)
                    for f in range(2):
                        n = 2 * x + f
                        m = e.matmul(o, HID[:, n % 4, 128 * t:128 * t + 128], W2[:, 64 * n:64 * n + 64], start=False, stop=(f == 1))
                m.then_inc(full["front", b], 1)

        def t_att(e, j):
            t_turn(e, j, "attT", 3)
            e.wait_ge(*emptied("front", j, "attT"))
            for n in range(10):
                name = ("qkvA", "qkvB")[n % 2]
                e.wait_ge(*free("front", j, name, n // 2))
                fence(e)
                w = WQ[:, 64 * n:64 * n + 64] if n < 8 else (WK, WV)[n - 8][:, :]
                e.matmul(PB[2 + n % 2][0:64, 0:TOK], w, NTR[0:64, :], start=True, stop=True).then_inc(full["front", 2 + n % 2], 1)
            e.wait_ge(*emptied("front", j, "qkvA", 4)); e.wait_ge(*emptied("front", j, "qkvB", 4))
            def scores(n):
                name = ("scoreA", "scoreB")[n % 2]
                e.wait_ge(*free("front", j, name, n // 2))
                fence(e)
                for a in range(2):
                    rt = 2 * n + a
                    b, pp, jj = rt // 12, rt % 12 // 4, rt % 4
                    for h2 in range(2):
                        u = 3 * (2 * jj + h2) + pp
                        r, h = u // 8, u % 8
                        m = e.matmul(PB[2 + n % 2][64 * h2:64 * h2 + 64, SEQ * a:SEQ * a + SEQ], QT[:, h, SEQ * b + r:SEQ * b + r + 190:3], KT[:, SEQ * b:SEQ * b + SEQ], start=True, stop=True)
                m.then_inc(full["front", 2 + n % 2], 1)
            def zs(b):
                e.wait_ge(*event("rden", j, b + 1))
                e.wait_ge(*free("front", j, "z", b)); e.wait_ge(*free("front", j, "z2", b))
                fence(e)
                for jc in range(3):
                    for pp in range(3):
                        o = PB[0][0:64, 192 * jc + 64 * pp:192 * jc + 64 * pp + 64] if jc < 2 else PB[1][0:64, 64 * pp:64 * pp + 64]
                        for jj in range(4):
                            m = e.matmul(o, P[:, 12 * b + 4 * pp + jj, jc:jc + 190:3], WON[:, 4 * pp + jj, :], start=(jj == 0), stop=(jj == 3))
                    if jc == 1: m.then_inc(full["front", 0], 1)
                m.then_inc(full["front", 1], 1)
            def outs(b):
                e.wait_ge(*emptied("front", j, "z", b)); e.wait_ge(*emptied("front", j, "z2", b))
                if b == 0: e.wait_ge(*free("front", j, "att"))
                fence(e)
                for pp in range(3):
                    nb = 3 * b + pp
                    for jc in range(3):
                        m = e.matmul(PB[2][64 * (nb % 2):64 * (nb % 2) + 64, 64 * (nb // 2):64 * (nb // 2) + 64],
                                     VC[:, SEQ * b + 64 * jc:SEQ * b + 64 * jc + 64], Z[:, jc, 64 * pp:64 * pp + 64], start=(jc == 0), stop=(jc == 2))
                if b: m.then_inc(full["front", 2], 1)
            for n in range(12): scores(n)
            zs(0); outs(0); zs(1); outs(1)

        def t_pk(e, j):
            t_turn(e, j, "pkT", 4)
            e.wait_ge(*emptied("front", j, "pkT"))
            for n in range(4):
                name = ("qpkA", "qpkB")[n % 2]
                e.wait_ge(*free("front", j, name, n // 2))
                fence(e)
                e.matmul(PB[2 + n % 2][:, 0:TOK], WPK[:, 128 * n:128 * n + 128], NT4[:, :], start=True, stop=True).then_inc(full["front", 2 + n % 2], 1)
            e.wait_ge(*emptied("front", j, "qpkA", 1)); e.wait_ge(*emptied("front", j, "qpkB", 1))
            for t in range(NT3):
                for p in range(2):
                    name = ("simA", "simB")[p]
                    e.wait_ge(*free("front", j, name, t))
                    fence(e)
                    for hh in range(2):
                        m = e.matmul(PB[2 + p][:, 256 * hh:256 * hh + 256], QPK[:, 2 * p + hh, 128 * t:128 * t + 128], KB[:, 2 * p + hh, :], start=True, stop=True)
                    m.then_inc(full["front", 2 + p], 1)

        def t_back(e, i):
            e.wait_ge(*event("weighted", i, 1))
            for n in range(8):
                name = ("q5A", "q5B")[n % 2]
                e.wait_ge(*free("back", i, name, n // 2))
                fence(e)
                e.matmul(PB[2 + n % 2][0:64, 0:TOK], WQ5[:, 64 * n:64 * n + 64], NTC[:, :], start=True, stop=True).then_inc(full["back", 2 + n % 2], 1)
            for n in range(6):
                t, hh = n // 2, n % 2
                e.wait_ge(*free("back", i, ("kvA", "kvB")[n % 2], n // 2))
                fence(e)
                for h in range(4):
                    m = e.transpose(PB[2 + n % 2][:, 128 * h:128 * h + 128], KV[:, t, 4 * hh + h, :], ID[:, :])
                m.then_inc(full["back", 2 + n % 2], 1)
            e.wait_ge(*emptied("back", i, "kvA", 2)); e.wait_ge(*emptied("back", i, "kvB", 2))
            for t in range(NT3):
                e.wait_ge(*free("back", i, "vwA", t))
                fence(e)
                for h in range(H):
                    m = e.matmul(PB[2][:, 64 * h:64 * h + 64], KVT[64:128, h, 128 * t:128 * t + 128], WO5[64:128, h, :], start=True, stop=True)
                m.then_inc(full["back", 2], 1)
            def sims(n):
                b, ib, half = n // 6, n // 2 % 3, n % 2
                jn = 64 * (ib + 1)
                e.wait_ge(*free("back", i, ("s5A", "s5B")[half], n // 2))
                fence(e)
                for a in range(2):
                    for h2 in range(2):
                        h = 2 * (2 * half + a) + h2
                        m = e.matmul(PB[2 + half][64 * h2:64 * h2 + 64, SEQ * a:SEQ * a + jn], Q5[:, h, SEQ * b + 64 * ib:SEQ * b + 64 * ib + 64], KVT[0:64, h, SEQ * b:SEQ * b + jn], start=True, stop=True)
                m.then_inc(full["back", 2 + half], 1)
            def turnp(nb):
                e.wait_ge(*event("scaled5", i, nb + 1))
                e.wait_ge(*free("back", i, "pt0", nb)); e.wait_ge(*free("back", i, "out", nb))
                fence(e)
                for c, (lo, hi, p0, t) in enumerate(spans(nb)):
                    for hp in range(4):
                        o = PTB[c][p0:p0 + hi - lo, 128 * hp:128 * hp + 128]
                        m = (e.matmul(o, P5[:, nb % 2, hp, lo:hi], ID[:, :], start=True, stop=True) if p0
                             else e.transpose(o, P5[:, nb % 2, hp, lo:hi], ID[:, :]))
                m.then_inc(full["back", 0], 1)
            def outs(nb):
                e.wait_ge(*emptied("back", i, "pt0", nb))
                if nb == 0: e.wait_ge(*emptied("back", i, "vwA", 2))
                fence(e)
                o = PB[1][64 * (nb % 2):64 * (nb % 2) + 64, 64 * (nb // 2):64 * (nb // 2) + 64]
                sp = spans(nb)
                for h in range(H):
                    for c, (lo, hi, p0, t) in enumerate(sp):
                        m = e.matmul(o, PT[0:p0 + hi - lo, slot(c, p0), 64 * h:64 * h + 64], VW[0:p0 + hi - lo, t, h, :],
                                     start=(h == 0 and c == 0), stop=(h == H - 1 and c == len(sp) - 1))
                m.then_inc(full["back", 1], 1)
            sims(0); sims(1)
            for nb in range(6):
                if nb < 5: sims(2 * nb + 2); sims(2 * nb + 3)
                turnp(nb)
                outs(nb)

        ORDER = ["forward0", "rnn", "forward1", "moe", "att", "pk", "mix", "top", "inverse0", "inverse1"]
        ORDER_LAST = ["forward0", "forward1", "mix", "inverse0", "inverse1", "tokens", "rnn", "moe", "att", "pk", "top"]
        MIXERS = ("rnn", "moe", "att", "pk", "top")

        def rounds(e, run, before, setup=None):
            before(e)
            run(e, ["coords"], None, None, 0, None)
            with e.Fori(0, LAYERS) as l:
                run(e, ["forward0", "forward1", "mix", "inverse0", "inverse1"], None, None, 0, l)
            run(e, ["tokens"], None, None, 0, None)
            run(e, list(MIXERS) + ["keep_idx", "keep_x"], None, 0, 1, None)
            with e.Fori(0, GROUPS - 1) as g:
                run(e, ["coords"], None, None, g + 1, None)
                with e.Fori(0, LAYERS - 1) as l:
                    i = g * LAYERS + l
                    run(e, ORDER + ["keep_idx", "back", "keep_x"], i, i + 1, g + 1, l)
                i = g * LAYERS + (LAYERS - 1)
                run(e, ORDER_LAST + ["keep_idx", "back", "keep_x"], i, i + 1, g + 1, LAYERS - 1)
            with e.Fori(PAIRS - LAYERS, PAIRS - 1) as i:
                run(e, list(MIXERS) + ["keep_idx", "back", "keep_x"], i, i + 1, GROUPS, None)
            run(e, ["back"], PAIRS - 1, None, None, None)

        def runner(prefix, take=None):
            here = SECTIONS[prefix]
            def run(e, order, i, j, g, l):
                units = [0]
                def cut(n):
                    if take and i is not None:
                        for _ in range(n):
                            if units[0] < NT3 * H:
                                take(e, i, units[0]); units[0] += 1
                if i is not None and take is None and "pool" == prefix:
                    pool_gather(e, i)
                rest = order.index("keep_idx") if "keep_idx" in order else order.index("back") if "back" in order else None
                for n, s in enumerate(order):
                    if n == rest:
                        cut(NT3 * H)
                    f = here.get(s.rstrip("01"))
                    if f: f(e, s, i, j, g, l, cut, None if g is None else g + ("tokens" in order))
                    if i is not None: cut(TAKES["tokens" in order].get(s, 0))
            return run

        def call(f, *what):
            return lambda e, s, i, j, g, l, cut, stored: f(e, *[{"i": i, "j": j, "g": g, "l": l, "q": int(s[-1]) if s[-1] in "01" else 0, "cut": cut, "stored": stored}[w] for w in what])

        def sp_forward_once(e, g, l, q):
            if q == 0: sp_forward(e, g, l)

        SECTIONS = {
            "sp": {"coords": call(sp_coords, "g"), "forward": call(sp_forward_once, "g", "l", "q"), "mix": call(sp_mix, "g", "l"), "tokens": call(sp_tokens, "g"),
                   "rnn": call(sp_front, "j", "stored"), "back": call(sp_back, "i")},
            "pool": {},
            "t": {"coords": call(t_coords, "g"), "forward": call(t_forward, "g", "l", "q"), "mix": call(t_mix, "g", "l"), "inverse": call(t_inverse, "g", "l", "q"),
                  "tokens": call(t_tokens, "g"), "rnn": call(t_rnn, "j"), "moe": call(t_moe, "j"), "att": call(t_att, "j"), "pk": call(t_pk, "j"), "back": call(t_back, "i")},
            "a": {"coords": call(a_coords, "g"), "forward": call(a_forward, "g", "l", "q"), "mix": call(a_mix, "g", "l"), "inverse": call(a_inverse, "g", "l", "q"),
                  "tokens": call(a_tokens, "g"), "rnn": call(a_rnn, "j"), "moe": call(a_moe, "j"), "att": call(a_att, "j"), "pk": call(a_pk, "j"),
                  "top": call(a_top, "j", "cut"), "back": call(a_back, "i")},
            "v": {"forward": call(v_forward, "g", "l", "q"), "inverse": call(v_inverse, "g", "l", "q"), "tokens": call(v_tokens, "g"),
                  "rnn": call(v_rnn, "j"), "moe": call(v_moe, "j"), "att": call(v_att, "j"), "pk": call(v_pk, "j"), "top": call(v_top, "j", "cut"),
                  "keep_idx": call(v_keep_idx), "keep_x": call(v_keep_x, "j"), "back": call(v_back, "i")},
        }

        @block.sync
        def _(e):
            rounds(e, runner("sp"), sp_setup)
            e.wait_ge(*event("stored", PAIRS - 1, 16))

        @block.gpsimd
        def _(e):
            def before(e):
                for t in (KB, ONES, RS, OHS, AREA4, FW0, FW1, FW2, CONV):
                    e.memset(t[:], 1.0 if t is ONES else 0.0).then_inc(zeroed, 1)
            rounds(e, runner("pool"), before)

        @block.vector
        def _(e):
            def before(e):
                credits(e, ["normed", "shifted", "one_hot", "maxed", "rden", "shift_top", "selected", "kept_idx", "kept_x", "gather_free", "weighted", "maxed5", "scaled5", "out_sb"],
                        [(k, b) for k in PLANS for b in range(4)])
                e.sem_inc(tp_out, CREDIT); e.sem_inc(tp_full, CREDIT)
                e.memset(NTR[64:65, :], 1.0); e.memset(NEG[:, :], -FMAX); e.memset(BIG[:, 0:1], 1e4); e.memset(BIG[:, 1:2], -1e4)
                e.wait_ge(const_in, 16 * NLOADS)
                e.tensor_tensor(BSUM[64:128, :], BRNN[64:128, 0:1], BRNN[64:128, 1:2], ALU.add)
                e.drain().then_inc(zeroed, 1)
            rounds(e, runner("v", v_consume), before)

        @block.scalar
        def _(e):
            def before(e):
                credits(e, ["exped", "exp_top", "multiplied"])
                e.sem_inc(mm_out, CREDIT); e.sem_inc(mm_full, CREDIT)
                e.wait_ge(const_in, 16 * NLOADS); e.wait_ge(zeroed, 10)
            rounds(e, runner("a", a_consume), before)

        @block.tensor
        def _(e):
            def before(e):
                e.wait_ge(const_in, 16 * NLOADS); e.wait_ge(zeroed, 10)
            rounds(e, runner("t"), before)


def layouts(inputs):
    g = {n: np.asarray(a) for n, a in inputs.items()}
    return [
        g["x"].transpose(0, 3, 1, 2).reshape(B * 3, POS),
        np.concatenate([g["L0_tok_fc0_w"], g["L0_tok_fc0_b"][None]], 0),
        np.stack([g[f"L0_tok_sw{n}"] for n in range(LAYERS)]).reshape(LAYERS, WID, WID, CHUNKS, KHC, MODES)
          .transpose(0, 3, 1, 4, 5, 2).reshape(LAYERS * CHUNKS * WID, KHC * MODES * WID),
        np.concatenate([np.concatenate([g[f"L0_tok_cw{n}"].T, g[f"L0_tok_cb{n}"][:, None]], 1) for n in range(LAYERS)], 0),
        np.concatenate([g["L0_tok_fc1_w"], g["L0_tok_fc1_b"][None]], 0),
        np.concatenate([g["L0_tok_fc2_w"], g["L0_tok_fc2_b"][None]], 0),
        *fourier_constants(),
        g["txt"].reshape(B * 128, D),
        np.concatenate([g["L0_attn_W_ih"].T, g["L0_attn_W_hh"].T], 0),
        np.stack([g["L0_attn_b_ih"], g["L0_attn_b_hh"]]),
        np.concatenate([g["L0_ffn_gate_w"], g["L0_ffn_gate_b"][None]], 0),
        np.concatenate([g["L0_ffn_w1"].transpose(1, 0, 2).reshape(D, E * FF), g["L0_ffn_b1"].reshape(1, E * FF)], 0),
        g["L0_ffn_w2"].reshape(E, 2, 128, D).transpose(2, 0, 1, 3).reshape(128, 2 * E * D),
        g["L0_ffn_b2"].reshape(1, E * D),
        g["L1_attn_Wq"].T, g["L1_attn_Wk"].T, g["L1_attn_Wv"].T,
        g["L1_attn_Wo"].T.reshape(64, 4, 2, D).transpose(2, 0, 1, 3).reshape(128, 4 * D),
        g["L1_ffn_Wq_pk"],
        g["L1_ffn_pk_keys"].transpose(0, 2, 3, 1).reshape(2 * H * 32, NK),
        g["L1_ffn_Wq"],
        g["L1_ffn_Wo"].reshape(H, D, D).transpose(1, 0, 2).reshape(D, H * D),
        np.concatenate([g["L1_ffn_keys_table"], g["L1_ffn_values_table"]], 1),
        *shape_constants(),
    ]


def shape_constants():
    row = np.arange(128)
    every = lambda v: np.tile(np.asarray(v, np.float32), (128, 1))
    return [
        np.eye(128, dtype=np.float32),
        np.triu(np.ones((128, 128), np.float32)),
        every(np.arange(NC50)),
        every(E - np.arange(E)),
        every(NK * NK * np.arange(H)),
        (np.arange(D)[None, :] > (row % D)[:, None]).astype(np.int32),
    ]


_NAMES = ["xT", "fc0", "sw", "cwb", "fc1", "fc2", "f1", "f2", "g3", "g4", "txt", "wrnn", "brnn", "gw", "w1", "w2", "b2", "wq", "wk", "wv",
          "wot", "wpk", "keysT", "wq5", "wo5", "table", "ident", "tri", "iota", "eight", "hbase", "later"]


def kernel(**inputs):
    import concourse.bacc as _bacc
    from concourse.bass_utils import run_bass_kernel_spmd as _run

    nc = _bacc.Bacc("TRN2", target_bir_lowering=False, num_devices=1)
    arrays, args = {}, []
    for name, a in zip(_NAMES, layouts(inputs)):
        a = np.ascontiguousarray(a)
        arrays[f"in_{name}"] = a
        args.append(nc.dram_tensor(f"in_{name}", a.shape, mybir.dt.from_np(a.dtype), kind="ExternalInput").ap())
    args.append(nc.dram_tensor("out", (B * SEQ, D), F32, kind="ExternalOutput").ap())
    early_fusion(nc, *args)
    r = _run(nc, [arrays], core_ids=[0])
    return r.results[0]["out"].reshape(B, SEQ, D)
```

```python
import numpy as np
import concourse.bass as bass
from concourse import mybir
from contextlib import ExitStack

F32 = mybir.dt.float32
I32 = mybir.dt.int32
U32 = mybir.dt.uint32
ALU = mybir.AluOpType
ACT = mybir.ActivationFunctionType
AX = mybir.AxisListType

B, SIDE, WID, MODES, LAYERS = 32, 64, 32, 20, 4
Q4 = 4
GB = 2
GROUPS = B // (Q4 * GB)
POS = SIDE * SIDE
ROWQ = POS // 512
CHUNKS = MODES // Q4
KWQ = CHUNKS * MODES * 2
KWG = [(0, 4), (4, 4), (8, 4), (12, 4), (16, 2), (18, 2)]
KW2 = MODES // 2
TG = [(0, 3), (3, 3), (6, 2), (8, 2)]
TURN_AT = [0, 0, 1, 2]

F_T = ROWQ + len(KWG)
I_T = len(TG) + ROWQ
I_M = KW2 + ROWQ
T_LAYER = GB * (F_T + I_T)
M_LAYER = GB * F_T + CHUNKS + GB * I_M
M_IN = GB * ROWQ
M_GROUP = M_IN + LAYERS * M_LAYER + GB * ROWQ * 2
T_GROUP = LAYERS * T_LAYER + GB * ROWQ
CREDIT = 2


def fourier_constants():
    k, p = np.arange(MODES), np.arange(SIDE)
    ang = 2 * np.pi * np.outer(p, k) / SIDE
    cos, sin = np.cos(ang), np.sin(ang)
    f1 = np.zeros((2, SIDE, 2, MODES, 2))
    for a in range(2):
        f1[a, :, a, :, 0], f1[a, :, a, :, 1] = cos, -sin
    f2 = np.zeros((SIDE, 2, MODES, 2))
    f2[:, 0, :, 0], f2[:, 1, :, 0] = cos, sin
    f2[:, 0, :, 1], f2[:, 1, :, 1] = -sin, cos
    f2 /= SIDE
    g3 = np.zeros((2, MODES, 2, SIDE, 2, 2))
    for a in range(2):
        g3[a, :, 0, :, a, 0], g3[a, :, 1, :, a, 0] = cos.T, -sin.T
        g3[a, :, 0, :, a, 1], g3[a, :, 1, :, a, 1] = sin.T, cos.T
    twice = np.where(k == 0, 1.0, 2.0)[:, None] / SIDE
    g4 = np.zeros((2, MODES, 2, 2, SIDE))
    for a in range(2):
        g4[a, :, 0, a], g4[a, :, 1, a] = twice * cos.T, -twice * sin.T
    return [np.ascontiguousarray(x, np.float32) for x in (
        f1.reshape(128, 80), f2.reshape(128, 40), g3.reshape(80, 256), g4.reshape(80, 128))]



SEQ, D = 192, 64
PAIRS = B // 2
TOK = 2 * SEQ
NT3 = TOK // 128
E, FF, CAP = 8, 256, 960
H, TOPK, NK = 8, 16, 64
CAND = [TOPK // (i + 1) for i in range(TOPK)]
NC50 = sum(CAND)
EPS = 1e-5
FMAX = float(np.finfo(np.float32).max)
RING = 3

FRONT = [("xT", 0, 1), ("rnn", 1, 2), ("rnn_back", 2, 1),
         ("moeT", 0, 1), ("gate", 1, 1), ("place", 1, 1), ("hidA", 2, 8), ("hidB", 3, 8), ("expert", 0, 4), ("expertB", 1, 4),
         ("attT", 0, 1), ("qkvA", 2, 5), ("qkvB", 3, 5), ("scoreA", 2, 6), ("scoreB", 3, 6),
         ("z", 0, 2), ("z2", 1, 2), ("att", 2, 1),
         ("pkT", 0, 1), ("qpkA", 2, 2), ("qpkB", 3, 2), ("simA", 2, 3), ("simB", 3, 3)]
BACK = [("kvA", 2, 3), ("kvB", 3, 3), ("q5A", 2, 4), ("q5B", 3, 4), ("vwA", 2, 3), 
        ("s5A", 2, 6), ("s5B", 3, 6), ("pt0", 0, 6), ("out", 1, 6)]


def number(plan, name, k):
    at = 0
    bank = next(b for n, b, _ in plan if n == name)
    for n, b, c in plan:
        if n == name:
            return bank, at + k
        if b == bank:
            at += c


def total(plan, bank):
    return sum(c for _, b, c in plan if b == bank)


PLANS = {"front": FRONT, "back": BACK}




TOP_STEPS = 11
STEPS = {"coords": [2] * (GB * ROWQ), "forward0": [2] * F_T, "mix": [8] + [6] * (CHUNKS - 1) + [4], "inverse0": [1.5] * KW2 + [3] * ROWQ,
         "tokens": [3.5] * (GB * ROWQ),
         "rnn": [3, 3, 3, 3, 3, 2, 2, 3], "moe": [3, 3, 3, 3, 6, 4, 4] + [3] * E + [6],
         "att": [3, 3, 3, 3, 3] + [2.5] * 5 + [3] * 6 + [4, 4], "pk": [3, 3, 3, 3, 3, 3, 3, 3, 3, 3],
         "top": [3, 3, 3, 3, 4, 4, 5, 5, 5, 5, 2] * NT3,
         "back": [3] * 3 + [2.5] * 4 + [3] * 3 + [6] * 7 + [4], "keep_x": [2], "rows": [1] * NT3 * H, "next_rows": [1] * NT3 * H}
STEPS["forward1"], STEPS["inverse1"] = STEPS["forward0"], STEPS["inverse0"]
BACK_IN = 3
U0, U1 = 6, 15


def when(section, mark):
    return float(np.interp(mark, range(len(STEPS[section]) + 1), np.cumsum([0] + STEPS[section])))


def weave(engine, chains, begun):
    ends = [sum(when(s, b) - when(s, a) for s, a, b in chain) for chain in chains]
    at = [0.0] * len(chains)
    left = [list(chain) for chain in chains]
    while any(left):
        first = None
        for n, chain in enumerate(left):
            while chain:
                section, a, b = chain[0]
                if section not in begun:
                    steps = engine.get(section)
                    steps = steps() if steps else iter(())
                    begun[section] = [next(steps, None), steps]
                mark = begun[section][0]
                if mark is not None and mark < b:
                    time = (at[n] + when(section, mark) - when(section, a)) / ends[n]
                    if first is None or time < first[0]: first = (time, section)
                    break
                at[n] += when(section, b) - when(section, a)
                chain.pop(0)
        if first:
            begun[first[1]][0] = next(begun[first[1]][1], None)


def whole(*sections):
    return [(s, 0, len(STEPS[s])) for s in sections]


def a_round(begin=(), layer=True, end=(), rows=True, back=True):
    tokenizer = [[*begin, "forward0", "forward1"], ["mix", "inverse0"] if end else ["mix"],
                 [*(() if end else ("inverse0",)), "inverse1", *end]] if layer else [[], [], []]
    return [[whole("rnn", "moe", "att", "pk"), whole(*tokenizer[0]), [("rows", U0, U1)] if rows else []],
            [whole("top"), whole(*tokenizer[1]), [("rows", U1, NT3 * H)] if rows else []],
            [[("back", 0, BACK_IN)] if back else []],
            [([("back", BACK_IN, len(STEPS["back"]))] if back else []) + whole("keep_x"), whole(*tokenizer[2]), [("next_rows", 0, U0)]]]


HALF = POS // 2


def early_fusion(nc, xT, fc0, sw, cwb, fc1, fc2, f1, f2, g3, g4, txt, wrnn, brnn, gw, w1, w2, b2, wq, wk, wv, wot, wpk, keysT, wq5, wo5,
                 table, ident_in, tri_in, iota_in, eight_in, hbase_in, later_in, out):
    tok = nc.dram_tensor("tokens", (B, POS), F32, kind="Internal").ap()
    ctx = ExitStack()
    with ctx:
        sb = lambda n, s, d=F32: ctx.enter_context(nc.sbuf_tensor(n, s, d))
        sem = lambda n: ctx.enter_context(nc.semaphore(n))
        TP = [ctx.enter_context(nc.psum_tensor(f"TP{i}", [128, 512], F32)) for i in range(2)]
        MM = [ctx.enter_context(nc.psum_tensor(f"MM{i}", [128, 512], F32)) for i in range(2)]
        PB = [ctx.enter_context(nc.psum_tensor(f"PB{i}", [128, 512], F32)) for i in range(4)]

        IMG = sb("IMG", [128, GB, POS])
        U = sb("U", [128, SIDE * 2 * MODES])
        COORDS = U[0:Q4 * 3, 0:HALF]
        ROW = U[0:Q4, 0:HALF]
        SPEC = sb("SPEC", [128, GB, 2 * MODES * MODES])
        TURN = sb("TURN", [128, 2, 512])
        AREAF = sb("AREAF", [128, KW2 * 128])
        TURN3 = AREAF[0:80, :].rearrange("p (k n) -> p k n", n=128)
        FHID = AREAF[:, 0:1024].rearrange("p (a n) -> p a n", a=2)
        BYMODE = sb("BYMODE", [128, Q4 * GB, KWQ])
        SW = sb("SW", [128, 2, MODES, WID])
        CONV = sb("CONV", [128, 129])
        F1, F2, G3, G4 = (sb(n, s) for n, s in (("F1", [128, 80]), ("F2", [128, 40]), ("G3", [80, 256]), ("G4", [80, 128])))
        FW0 = sb("FW0", [Q4 * 3, 128]); FB0 = sb("FB0", [128, 1])
        FW1 = sb("FW1", [128, 2, 128]); FB1 = sb("FB1", [128, 1])
        FW2 = sb("FW2", [128, 2, 4]); FB2 = sb("FB2", [4, 1])

        WRNN = sb("WRNN", [128, D]); BRNN = sb("BRNN", [128, 2]); BSUM = sb("BSUM", [128, 1])
        GW = sb("GW", [65, E]); W1 = sb("W1E", [65, E * FF]); W2 = sb("W2E", [128, 2 * E * D]); B2 = sb("B2E", [1, E * D])
        WQ = sb("WQ", [64, H * D]); WK = sb("WK", [64, D]); WV = sb("WV", [64, D]); WOT = sb("WOT", [128, 4, D])
        WPK = sb("WPK", [64, 512]); KB = sb("KB", [128, 4, 256]); WQ5 = sb("WQ5", [64, 512]); WO5 = sb("WO5", [128, H, D])
        ID = sb("IDB", [128, 128]); TRI = sb("TRI", [128, 128]); ONES = sb("ONES", [128, 128])
        IOTA = sb("IOTA", [128, NC50]); EIGHT = sb("EIGHT", [128, E]); HBASE = sb("HBASE", [128, H])
        LATER = sb("LATER", [128, D], I32); NEG = sb("NEG", [128, 1]); BIG = sb("BIG", [128, 2])
        AREA1 = sb("AREA1", [128, 24 * SEQ + 64]); AREA2 = sb("AREA2", [128, H * TOK]); AREA3 = sb("AREA3", [128, 4 * TOK]); AREA4 = sb("AREA4", [128, 3 * 512])
        X = sb("XH", [128, NT3, D]); N = sb("N", [128, NT3, D]); TMP = sb("TMP", [128, NT3, D])
        ST = sb("ST", [128, 6, NT3]); RS = sb("RS", [128, 2, SEQ]); NTR = sb("NTR", [65, TOK]); NT4 = sb("NT4", [64, TOK])
        LG = sb("LG", [128, NT3, E]); LE = sb("LE", [128, NT3, E]); OH = sb("OH", [128, NT3, E]); OHS = sb("OHS", [128, E])
        G1 = sb("G1", [128, 8, NT3]); HID = AREA3[:, 0:4 * TOK].rearrange("p (s n) -> p s n", s=4); Y = sb("Y", [128, NT3, D]); YM = sb("YM", [128, NT3, D])
        QT = AREA2[0:64, :].rearrange("p (h n) -> p h n", h=H); KT = sb("KT", [64, TOK]); VC = sb("VC", [64, TOK])
        P = AREA1[:, 0:24 * SEQ].rearrange("p (r t) -> p r t", t=SEQ); NM = sb("NM", [128, 24]); DEN = sb("DEN", [128, 24]); WON = AREA3[:, 0:12 * D].rearrange("p (r d) -> p r d", d=D); Z = AREA3[0:64, 12 * D:12 * D + 3 * SEQ].rearrange("p (c t) -> p c t", c=3)
        QPK = AREA2[:, 0:4 * TOK].rearrange("p (r t) -> p r t", t=TOK); SIM = AREA1[:, 0:3072].rearrange("p (t a k) -> p t a k", t=NT3, a=2)
        SIMR = AREA4[:, 0:1024].rearrange("p (a k) -> p a k", a=2); V16 = sb("V16", [128, 2, H, TOPK]); I16 = sb("I16", [128, 2, H, TOPK], U32); IF = sb("IF", [128, 2, H, TOPK])
        C50, CI, CR = (AREA2[:, 1536 + 400 * n:1936 + 400 * n].rearrange("p (h c) -> p h c", h=H) for n in range(3))
        FV = sb("FV", [128, H, TOPK]); FP = sb("FP", [128, H, TOPK], U32); PF = sb("PF", [128, H, TOPK]); EQ = AREA1[:, 3072:4672].rearrange("p (k c) -> p k c", c=NC50)
        FS = sb("FS", [128, H, TOPK]); S8 = sb("S8", [128, 2, H])
        IDX = sb("IDX", [128, NT3, H, TOPK], I32); WT = sb("WT", [128, NT3, H, TOPK]); XC = sb("XC", [128, NT3, D]); NTC = sb("NTC", [64, TOK])
        GATH = sb("GATH", [128, RING, TOPK, 2 * D]); KV = sb("KV", [128, NT3, H, 2 * D])
        Q5 = QT; KVT = AREA1[:, 0:3072].rearrange("p (h n) -> p h n", h=H); VW = AREA3[:, :].rearrange("p (t h d) -> p t h d", t=NT3, h=H)
        P5 = AREA1[:, 3072:4608].rearrange("p (s h t) -> p s h t", s=2, h=4); NM5 = sb("NM5", [128, 2, 4]); DEN5 = sb("DEN5", [128, 2, 4]); PT = AREA4[:, :].rearrange("p (s n) -> p s n", s=3)
        OUTB = sb("OUTB", [128, NT3, D])

        full = {(k, b): sem(f"{k}_full{b}") for k in PLANS for b in range(4)}
        empt = {(k, b): sem(f"{k}_out{b}") for k in PLANS for b in range(4)}
        PER = {"x_in": 80, "normed": 4, "shifted": 1, "exped": 1, "one_hot": 1, "h_kept": 1, "maxed": 24, "masked": 12,
               "rden": 2, "shift_top": NT3, "exp_top": NT3, "kept_idx": NT3, "kept_x": 1,
               "gather_free": NT3 * H, "weighted": 1, "maxed5": 12, "scaled5": 6, "out_sb": 1, "stored": 16, "multiplied": NT3 * H}
        S = {n: sem(n) for n in PER}
        gath = [sem(f"gathered{r}") for r in range(RING)]
        const_in, zeroed = sem("weights_in"), sem("buffers_zeroed")
        coords_in = sem("coords_in"); by_mode = sem("modes_side_by_side"); by_image = sem("images_side_by_side"); sw_in = [sem("sw_in0"), sem("sw_in1")]; conv_in = sem("conv_in")
        tp_full = sem("turned"); tp_out = sem("turned_out"); mm_full = sem("multiplied_full"); mm_out = sem("multiplied_out")
        row_out = sem("tokens_stored")
        passed = {x: sem(f"{x}_passed") for x in ("PE", "DVE", "Pool")}
        block = ctx.enter_context(nc.Block())

        def fence(e):
            e.sem_inc(passed[str(e.engine).split(".")[-1]], 1)


        def event(name, it, k):
            return S[name], (it + 1) * PER[name] + k

        def filled(kind, it, name, k=0):
            b, n = number(PLANS[kind], name, k)
            return full[kind, b], (it + 1) * total(PLANS[kind], b) + n + 1

        def emptied(kind, it, name, k=0):
            b, n = number(PLANS[kind], name, k)
            return empt[kind, b], (it + 1) * total(PLANS[kind], b) + n + 1

        def free(kind, it, name, k=0):
            b, n = number(PLANS[kind], name, k)
            return empt[kind, b], (it + 1) * total(PLANS[kind], b) + n

        def bank(kind, name):
            return number(PLANS[kind], name, 0)[0]

        def credits(e, names, banks=()):
            for n in names: e.sem_inc(S[n], PER[n])
            for k, b in banks:
                e.sem_inc(full[k, b], total(PLANS[k], b)); e.sem_inc(empt[k, b], total(PLANS[k], b))
        tokv = tok.rearrange("b (h w) -> (b h) w", w=D)

        def mm_group(g): return M_GROUP * g
        def mm_layer(g, l): return M_GROUP * g + M_IN + M_LAYER * l
        def tp_layer(g, l): return T_GROUP * g + T_LAYER * l
        def mm_last(g): return M_GROUP * g + M_IN + LAYERS * M_LAYER
        def tp_last(g): return T_GROUP * g + LAYERS * T_LAYER

        def sp_coords(e, g):
            for n in range(2 * GB):
                yield ROWQ // 2 * n
                if n: e.wait_ge(mm_full, CREDIT + mm_group(g) + ROWQ // 2 * n)
                else: e.wait_ge(row_out, 16 * 2 * GB * g + 16)
                e.dma_start(COORDS, xT[bass.ds((g * GB + n // 2) * (Q4 * 3), Q4 * 3), HALF * (n % 2):HALF * (n % 2) + HALF]).then_inc(coords_in, 16)

        def sp_chunk(e, l, c):
            e.dma_start(SW[:, c % 2, :, :].rearrange("p m o -> p (m o)"), sw[bass.ds((l * CHUNKS + c) * 128, 128), :]).then_inc(sw_in[c % 2], 16)

        def sp_forward(e, g, l, q):
            if q: return
            yield 0
            e.wait_ge(mm_full, CREDIT + mm_layer(g, l))
            sp_chunk(e, l, 0)
            sp_chunk(e, l, 1)
            e.wait_ge(mm_out, CREDIT + mm_layer(g, l))
            for a in range(Q4):
                r = slice(32 * a, 32 * a + 32)
                e.dma_start(CONV[r, r], cwb[bass.ds(l * WID, WID), 0:WID]).then_inc(conv_in, 16)
                e.dma_start(CONV[r, 128:129], cwb[bass.ds(l * WID, WID), WID:WID + 1], allow_slow_non_contiguous=True).then_inc(conv_in, 16)

        def turned(e, there, done):
            for a in range(Q4):
                for b in range(Q4):
                    m, i = BYMODE[32 * a:32 * a + 32, GB * b:GB * b + GB, :], SPEC[32 * b:32 * b + 32, :, KWQ * a:KWQ * a + KWQ]
                    e.dma_start(*((m, i) if there else (i, m))).then_inc(done, 16)

        def sp_mix(e, g, l):
            yield 0
            e.wait_ge(mm_out, CREDIT + mm_layer(g, l) + GB * F_T)
            e.wait_ge(by_image, 16 * Q4 * Q4 * (g * LAYERS + l) + 16)
            turned(e, True, by_mode)
            for c in range(2, CHUNKS):
                yield c - 0.8
                e.wait_ge(mm_full, CREDIT + mm_layer(g, l) + GB * F_T + c - 1)
                sp_chunk(e, l, c)
            yield CHUNKS + 0.1
            e.wait_ge(mm_out, CREDIT + mm_layer(g, l) + GB * F_T + CHUNKS)
            turned(e, False, by_image)

        def sp_tokens(e, g):
            for n in range(2 * GB):
                yield ROWQ // 2 * (n + 1) - 0.05
                e.wait_ge(tp_out, CREDIT + tp_last(g) + ROWQ // 2 * (n + 1))
                e.dma_start(tok[bass.ds((g * GB + n // 2) * Q4, Q4), HALF * (n % 2):HALF * (n % 2) + HALF], ROW).then_inc(row_out, 16)

        def t_coords(e, g):
            for n in range(GB * ROWQ):
                yield n
                if n % (ROWQ // 2) == 0:
                    e.wait_ge(coords_in, g * (2 * GB * 16) + 16 * (n // (ROWQ // 2)) + 16)
                c = n % (ROWQ // 2)
                p = mm_slot(e, mm_group(g), n)
                fence(e)
                e.matmul(p[:, :], FW0[:, :], COORDS[:, 512 * c:512 * c + 512], start=True, stop=True).then_inc(mm_full, 1)

        def mm_slot(e, base, n):
            e.wait_ge(mm_out, CREDIT + base + n - 1)
            return MM[n % 2]
        def tp_slot(e, base, n):
            e.wait_ge(tp_out, CREDIT + base + n - 1)
            return TP[n % 2]
        def t_forward(e, g, l, q):
            tb, mb = tp_layer(g, l) + q * F_T, mm_layer(g, l) + q * F_T
            def turn(c):
                t = tp_slot(e, tb, c)
                for j in range(4):
                    m = e.transpose(t[:, 128 * j:128 * j + 128], IMG[:, q, 512 * c + 128 * j:512 * c + 128 * j + 128], ID[:, :])
                m.then_inc(tp_full, 1)
            def along_w(c):
                e.wait_ge(tp_out, CREDIT + tb + c + 1)
                p = mm_slot(e, mb, c)
                for j in range(4):
                    m = e.matmul(p[:, 80 * j:80 * j + 80], TURN[:, c % 2, 128 * j:128 * j + 128], F1[:, :], start=True, stop=True)
                m.then_inc(mm_full, 1)
            yield 0
            if q == 0:
                e.wait_ge(mm_out, CREDIT + mb)
            turn(0)
            for c in range(ROWQ):
                yield c
                if c + 1 < ROWQ: turn(c + 1)
                yield c + 0.5
                along_w(c)
            yield ROWQ
            e.wait_ge(mm_out, CREDIT + mb + ROWQ)
            Uv = U[:, :].rearrange("p (k m) -> p k m", k=MODES)
            def turn2(i):
                t = tp_slot(e, tb, ROWQ + i)
                for j in range(KWG[i][1]):
                    m = e.transpose(t[:, 128 * j:128 * j + 128], Uv[:, KWG[i][0] + j, :], ID[:, :])
                m.then_inc(tp_full, 1)
            def along_h(i):
                e.wait_ge(tp_out, CREDIT + tb + ROWQ + i + 1)
                p = mm_slot(e, mb, ROWQ + i)
                for j in range(KWG[i][1]):
                    m = e.matmul(p[:, 40 * j:40 * j + 40], TURN[:, (ROWQ + i) % 2, 128 * j:128 * j + 128], F2[:, :], start=True, stop=True)
                m.then_inc(mm_full, 1)
            turn2(0)
            for i in range(len(KWG)):
                yield ROWQ + i
                if i + 1 < len(KWG): turn2(i + 1)
                yield ROWQ + i + 0.5
                along_h(i)
        def t_mix(e, g, l):
            mb = mm_layer(g, l) + GB * F_T
            yield 0
            e.wait_ge(by_mode, 16 * Q4 * Q4 * (g * LAYERS + l + 1))
            Bv = BYMODE[:, :, :].rearrange("p q (m r) -> p q m r", r=2)
            for c in range(CHUNKS):
                yield c
                per_layer = (CHUNKS + 1 - c % 2) // 2
                e.wait_ge(sw_in[c % 2], 16 * (per_layer * (g * LAYERS + l) + c // 2 + 1))
                p = mm_slot(e, mb, c)
                fence(e)
                pv = p[:, 0:Q4 * GB * MODES * 2].rearrange("p (q m r) -> p q m r", q=Q4 * GB, r=2)
                for k in range(MODES):
                    for a in range(Q4):
                        r = slice(32 * a, 32 * a + 32)
                        m = e.matmul(pv[r, :, k, :], SW[r, c % 2, k, :], Bv[r, :, c * MODES + k, :], start=True, stop=True)
                m.then_inc(mm_full, 1)
        def t_inverse(e, g, l, q):
            tb = tp_layer(g, l) + GB * F_T + q * I_T
            mb = mm_layer(g, l) + GB * F_T + CHUNKS + q * I_M
            yield 0
            if q == 0:
                e.wait_ge(mm_out, CREDIT + mb)
            e.wait_ge(by_image, 16 * Q4 * Q4 * (g * LAYERS + l + 1) + 16)
            def turn3(i):
                k0, n = TG[i]
                t = tp_slot(e, tb, i)
                for j in range(n):
                    m = e.transpose(t[0:80, 128 * j:128 * j + 128], SPEC[:, q, 80 * (k0 + j):80 * (k0 + j) + 80], ID[:, :])
                m.then_inc(tp_full, 1)
            for i in range(KW2):
                yield i
                for gi in range(len(TG)):
                    if TURN_AT[gi] == i: turn3(gi)
                yield i + 0.6
                for gi, (k0, n) in enumerate(TG):
                    if k0 == i: e.wait_ge(tp_out, CREDIT + tb + gi + 1)
                p = mm_slot(e, mb, i)
                e.matmul(p[:, 0:256], TURN3[:, i, :], G3[:, :], start=True, stop=True).then_inc(mm_full, 1)
            yield KW2
            e.wait_ge(mm_out, CREDIT + mb + KW2)
            if q == 0:
                e.wait_ge(conv_in, (g * LAYERS + l) * 128 + 128)
            def turn4(c):
                t = tp_slot(e, tb, len(TG) + c)
                for j in range(4):
                    m = e.transpose(t[0:80, 128 * j:128 * j + 128], U[:, 80 * (4 * c + j):80 * (4 * c + j) + 80], ID[:, :])
                m.then_inc(tp_full, 1)
            def back_w(c):
                p = mm_slot(e, mb, KW2 + c)
                e.matmul(p[:, :], CONV[:, 0:128], IMG[:, q, 512 * c:512 * c + 512], start=True, stop=False, skip_group_check=True)
                e.wait_ge(tp_out, CREDIT + tb + len(TG) + c + 1)
                for j in range(4):
                    m = e.matmul(p[:, 128 * j:128 * j + 128], TURN[0:80, c % 2, 128 * j:128 * j + 128], G4[:, :], start=False, stop=True, skip_group_check=True)
                m.then_inc(mm_full, 1)
            turn4(0)
            for c in range(ROWQ):
                yield KW2 + c
                if c + 1 < ROWQ: turn4(c + 1)
                yield KW2 + c + 0.5
                back_w(c)
        def t_tokens(e, g):
            mb, tb = mm_last(g), tp_last(g)
            yield 0
            e.wait_ge(mm_out, CREDIT + mb)
            for n in range(GB * ROWQ):
                yield n
                q, c = n // ROWQ, n % ROWQ
                for pr in range(2):
                    p = mm_slot(e, mb, 2 * n + pr)
                    e.matmul(p[:, :], FW1[:, pr, :], IMG[:, q, 512 * c:512 * c + 512], start=True, stop=True).then_inc(mm_full, 1)
                t = tp_slot(e, tb, n)
                yield n + 0.7
                for pr in range(2):
                    e.wait_ge(mm_out, CREDIT + mb + 2 * n + pr + 1)
                    fence(e)
                    m = e.matmul(t[0:4, :], FW2[:, pr, :], FHID[:, pr, :], start=(pr == 0), stop=(pr == 1))
                m.then_inc(tp_full, 1)

        def evac(e, base, n, dst, src, func=ACT.Copy, **kw):
            e.wait_ge(mm_full, CREDIT + base + n + 1)
            e.activation(dst, MM[n % 2][src] if not callable(src) else src(MM[n % 2]), func, **kw).then_inc(mm_out, 1)
        def a_forward(e, g, l, q):
            mb = mm_layer(g, l) + q * F_T
            Uf = U[:, :].rearrange("p (k h r) -> p h k r", k=MODES, r=2)
            for c in range(ROWQ):
                yield c + 0.9
                evac(e, mb, c, Uf[:, 8 * c:8 * c + 8, :, :], lambda m: m[:, 0:320].rearrange("p (h k r) -> p h k r", k=MODES, r=2))
            for i, (k0, n) in enumerate(KWG):
                yield ROWQ + i + 0.9
                evac(e, mb, ROWQ + i, SPEC[:, q, 40 * k0:40 * (k0 + n)], (slice(None), slice(0, 40 * n)))
        def a_mix(e, g, l):
            mb = mm_layer(g, l) + GB * F_T
            for c in range(CHUNKS):
                yield c + 0.9
                evac(e, mb, c, BYMODE[:, :, 2 * MODES * c:2 * MODES * (c + 1)],
                     lambda m: m[:, 0:Q4 * GB * MODES * 2].rearrange("p (q m) -> p q m", q=Q4 * GB))
        def a_inverse(e, g, l, q):
            mb = mm_layer(g, l) + GB * F_T + CHUNKS + q * I_M
            Uv = U[:, :].rearrange("p (h k r) -> p k h r", k=KW2, r=4)
            for i in range(KW2):
                yield i + 0.9
                evac(e, mb, i, Uv[:, i, :, :], lambda m: m[:, 0:256].rearrange("p (h r) -> p h r", r=4))
            for c in range(ROWQ):
                yield KW2 + c + 0.9
                evac(e, mb, KW2 + c, IMG[:, q, 512 * c:512 * c + 512], (slice(None), slice(None)), ACT.Gelu, bias=CONV[:, 128:129])
        def a_coords(e, g):
            for n in range(GB * ROWQ):
                yield n + 0.5
                evac(e, mm_group(g), n, IMG[:, n // ROWQ, 512 * (n % ROWQ):512 * (n % ROWQ) + 512], (slice(None), slice(None)), ACT.Identity, bias=FB0[:, :])

        def a_tokens(e, g):
            for n in range(GB * ROWQ):
                yield n + 0.4
                for pr in range(2):
                    e.wait_ge(tp_full, CREDIT + tp_last(g) + n)
                    evac(e, mm_last(g), 2 * n + pr, FHID[:, pr, :], (slice(None), slice(None)), ACT.Gelu, bias=FB1[:, :])

        def copy(e, base, n, dst, rows, cols):
            e.wait_ge(tp_full, CREDIT + base + n + 1)
            e.tensor_copy(dst, TP[n % 2][0:rows, 0:cols]).then_inc(tp_out, 1)
        def v_forward(e, g, l, q):
            tb, mb = tp_layer(g, l) + q * F_T, mm_layer(g, l) + q * F_T
            for c in range(ROWQ):
                yield c - 0.3 if c else 0.1
                e.wait_ge(mm_full, CREDIT + mb + c - 1)
                copy(e, tb, c, TURN[:, c % 2, :], 128, 512)
            for i, (k0, n) in enumerate(KWG):
                yield ROWQ + i - 0.3 if i else ROWQ + 0.1
                e.wait_ge(mm_full, CREDIT + mb + ROWQ + i - 1)
                copy(e, tb, ROWQ + i, TURN[:, i % 2, 0:128 * n], 128, 128 * n)
        def v_inverse(e, g, l, q):
            tb = tp_layer(g, l) + GB * F_T + q * I_T
            mb = mm_layer(g, l) + GB * F_T + CHUNKS + q * I_M
            yield 0
            e.wait_ge(mm_full, CREDIT + mb - ROWQ if q else mb)
            for i, (k0, n) in enumerate(TG):
                yield TURN_AT[i] + 0.4
                copy(e, tb, i, TURN3[:, k0:k0 + n, :].rearrange("p k n -> p (k n)"), 80, 128 * n)
            for c in range(ROWQ):
                yield KW2 + c - 0.3 if c else KW2 + 0.1
                e.wait_ge(mm_full, CREDIT + mb + KW2 + c - 1)
                copy(e, tb, len(TG) + c, TURN[0:80, c % 2, :], 80, 512)
        def v_tokens(e, g):
            for n in range(GB * ROWQ):
                yield n + 0.9
                e.wait_ge(tp_full, CREDIT + tp_last(g) + n + 1)
                if n % (ROWQ // 2) == 0:
                    e.wait_ge(row_out, 16 * (2 * GB * g + n // (ROWQ // 2)) + 16)
                c = n % (ROWQ // 2)
                e.tensor_scalar(ROW[:, 512 * c:512 * c + 512], TP[n % 2][0:4, :], FB2[:, :], None, ALU.add).then_inc(tp_out, 1)

        def sp_setup(e):
            credits(e, ["x_in", "stored"])
            e.sem_inc(row_out, 16); e.sem_inc(by_image, 16)
            e.wait_ge(zeroed, 9)
            n = [0]
            def load(d, s, **k):
                e.dma_start(d, s, **k).then_inc(const_in, 16); n[0] += 1
            load(WRNN[:, :], wrnn)
            for i in range(2): load(BRNN[64:128, i:i + 1], brnn[i, :].rearrange("(a b) -> a b", b=1))
            for d, s in ((GW, gw), (W1, w1), (W2, w2), (B2, b2), (WQ, wq), (WK, wk), (WV, wv), (WPK, wpk), (WQ5, wq5),
                         (ID, ident_in), (TRI, tri_in), (IOTA, iota_in), (EIGHT, eight_in), (HBASE, hbase_in), (LATER, later_in)):
                load(d[:, :], s)
            load(WOT[:, :, :].rearrange("p a b -> p (a b)"), wot)
            load(WO5[64:128, :, :].rearrange("p a b -> p (a b)"), wo5)
            for p in range(2):
                for h in range(H):
                    load(KB[32 * (h % 4):32 * (h % 4) + 32, 2 * p + h // 4, 64 * (h % 4):64 * (h % 4) + 64], keysT[(p * H + h) * 32:(p * H + h) * 32 + 32, :])
            for d, s in ((F1, f1), (F2, f2), (G3, g3), (G4, g4)):
                load(d[:, :], s)
            for a in range(Q4):
                load(FW0[3 * a:3 * a + 3, 32 * a:32 * a + 32], fc0[0:3, :])
                load(FB0[32 * a:32 * a + 32, :], fc0[3, :].rearrange("(a b) -> a b", b=1))
                load(FW1[32 * a:32 * a + 32, a // 2, 64 * (a % 2):64 * (a % 2) + 64], fc1[0:WID, :])
                load(FW2[64 * (a % 2):64 * (a % 2) + 64, a // 2, a:a + 1], fc2[0:64, :])
                load(FB2[a:a + 1, :], fc2[64:65, :])
            for a in range(2):
                load(FB1[64 * a:64 * a + 64, :], fc1[WID, :].rearrange("(a b) -> a b", b=1))
            assert n[0] == NLOADS, n[0]
        NLOADS = 1 + 2 + 15 + 2 + 16 + 4 + 5 * Q4 + 2

        def sp_front(e, j, g):
            yield 0
            e.wait_ge(*event("kept_x", j - 1, 1))
            e.wait_ge(row_out, 16 * 2 * GB * g + 16)
            for d, s in ((X[0:64, 0, :], tokv[bass.ds(j * 128, 64), :]), (X[64:128, 0, :], txt[bass.ds(j * 256, 64), :]),
                         (X[0:64, 1, :], txt[bass.ds(j * 256 + 64, 64), :]), (X[64:128, 1, :], tokv[bass.ds(j * 128 + 64, 64), :]),
                         (X[:, 2, :], txt[bass.ds(j * 256 + 128, 128), :])):
                e.dma_start(d, s).then_inc(S["x_in"], 16)

        def sp_back(e, i):
            yield 17.2
            e.wait_ge(*event("out_sb", i, 1))
            e.dma_start(out[bass.ds(i * TOK, TOK), :].rearrange("(t p) d -> p t d", p=128), OUTB[:, :, :]).then_inc(S["stored"], 16)

        def pool_gather(e, i):
            for u in range(NT3 * H):
                r = u % RING
                if u % H == 0: e.wait_ge(*event("kept_idx", i, u // H + 1))
                e.wait_ge(*event("gather_free", i, u + 1 - RING))
                fence(e)
                for k in range(TOPK):
                    e.indirect_dma_start(GATH[:, r, k, :], None, table, bass.IndirectOffsetOnAxis(IDX[:, u // H, u % H, k:k + 1], 0)).then_inc(gath[r], 16)

        def bc(ap, n):
            return ap.rearrange("p (t o) -> p t o", o=1).to_broadcast([ap.shape[0], ap.shape[1], n])

        def normalize(e):
            mean, var, y, a, b, c = (ST[:, i, :] for i in range(6))
            yield 0
            e.drain()
            e.tensor_reduce(mean, X[:, :, :], AX.X, ALU.add); e.drain()
            e.tensor_scalar(mean, mean, 1.0 / D, None, ALU.mult); e.drain()
            e.tensor_tensor(N[:, :, :], X[:, :, :], bc(mean, D), ALU.subtract); e.drain()
            yield 1
            e.tensor_tensor(TMP[:, :, :], N[:, :, :], N[:, :, :], ALU.mult); e.drain()
            e.tensor_reduce(var, TMP[:, :, :], AX.X, ALU.add); e.drain()
            e.tensor_scalar(var, var, 1.0 / D, EPS, ALU.mult, ALU.add); e.drain()
            e.tensor_scalar(a.bitcast(I32), var.bitcast(I32), 1, None, ALU.logical_shift_right); e.drain()
            e.tensor_scalar(y.bitcast(I32), a.bitcast(I32), -1.0, float(0x5F3759DF), ALU.mult, ALU.add); e.drain()
            for k in range(4):
                if k % 2 == 0: yield 2 + k // 2
                e.tensor_tensor(b, y, y, ALU.mult); e.drain()
                e.tensor_tensor(c, b, var, ALU.mult); e.drain()
                e.tensor_scalar(c, c, -0.5, 1.5, ALU.mult, ALU.add); e.drain()
                e.tensor_tensor(y, y, c, ALU.mult); e.drain()
            e.tensor_tensor(N[:, :, :], N[:, :, :], bc(y, D), ALU.mult).then_inc(S["normed"], 1)

        def v_rnn(e, j):
            yield 0
            e.wait_ge(*event("x_in", j, 80))
            fence(e)
            yield from normalize(e)
            yield 7.6
            e.wait_ge(*filled("front", j, "rnn_back"))
            e.tensor_tensor(X[:, :, :], X[:, :, :], PB[2][:, 0:192].rearrange("p (t d) -> p t d", d=D), ALU.add).then_inc(empt["front", 2], 1)

        def v_moe(e, j):
            yield from normalize(e)
            yield 4.7
            e.wait_ge(*filled("front", j, "gate"))
            m, sm, r, pm, w, pos, keep, sc = (G1[:, i, :] for i in range(8))
            L = PB[1][:, 0:24].rearrange("p (t e) -> p t e", e=E)
            e.tensor_reduce(m, L, AX.X, ALU.max); e.drain()
            e.tensor_tensor(LG[:, :, :], L, bc(m, E), ALU.subtract).then_inc(empt["front", 1], 1)
            e.wait_ge(*emptied("front", j, "gate"))
            fence(e)
            e.drain().then_inc(S["shifted"], 1)
            e.memset(Y[:, :, :], 0.0)
            yield 5.4
            e.wait_ge(*event("exped", j, 1))
            e.tensor_reduce(sm, LE[:, :, :], AX.X, ALU.add); e.drain()
            e.reciprocal(r, sm); e.drain()
            e.tensor_tensor(LE[:, :, :], LE[:, :, :], bc(r, E), ALU.mult); e.drain()
            e.tensor_reduce(pm, LE[:, :, :], AX.X, ALU.max); e.drain()
            e.tensor_tensor(LG[:, :, :], LE[:, :, :], bc(pm, E), ALU.is_equal); e.drain()
            e.tensor_tensor(LG[:, :, :], LG[:, :, :], EIGHT[:, :].rearrange("p (o e) -> p o e", o=1).to_broadcast([128, NT3, E]), ALU.mult); e.drain()
            e.tensor_reduce(w, LG[:, :, :], AX.X, ALU.max); e.drain()
            e.tensor_tensor(OH[:, :, :], LG[:, :, :], bc(w, E), ALU.is_equal).then_inc(S["one_hot"], 1)
            yield 6.5
            e.wait_ge(*filled("front", j, "place"))
            e.tensor_tensor(LG[:, :, :], PB[1][:, 0:24].rearrange("p (t e) -> p t e", e=E), OH[:, :, :], ALU.mult).then_inc(empt["front", 1], 1)
            for t in range(NT3):
                e.drain()
                e.tensor_tensor(OHS[:, :], OHS[:, :], OH[:, t, :], ALU.add)
            e.drain()
            e.tensor_reduce(pos, LG[:, :, :], AX.X, ALU.add); e.drain()
            e.tensor_scalar(keep, pos, float(CAP), None, ALU.is_le); e.drain()
            e.tensor_tensor(sc, keep, pm, ALU.mult)
            for x in range(E):
                yield 7.7 + x
                name = ("expert", "expertB")[x % 2]
                e.wait_ge(*filled("front", j, name, x // 2))
                fence(e)
                e.drain()
                b = bank("front", name)
                e.copy_predicated(Y[:, :, :], OH[:, :, x:x + 1].to_broadcast([128, NT3, D]).bitcast(I32),
                                  PB[b][:, 0:192].rearrange("p (t d) -> p t d", d=D)).then_inc(empt["front", b], 1)
            yield 7 + E
            e.drain()
            e.tensor_tensor(Y[:, :, :], Y[:, :, :], bc(sc, D), ALU.mult); e.drain()
            e.tensor_tensor(YM[:, :, :], Y[:, :, :], Y[:, :, :], ALU.is_equal)
            e.memset(TMP[:, :, :], 0.0); e.drain()
            e.copy_predicated(TMP[:, :, :], YM[:, :, :].bitcast(I32), Y[:, :, :]); e.drain()
            e.tensor_scalar(YM[:, :, :], TMP[:, :, :], FMAX, None, ALU.is_gt); e.drain()
            e.copy_predicated(TMP[:, :, :], YM[:, :, :].bitcast(I32), BIG[:, 0:1].rearrange("p (a b) -> p a b", b=1).to_broadcast([128, NT3, D])); e.drain()
            e.tensor_scalar(YM[:, :, :], TMP[:, :, :], -FMAX, None, ALU.is_lt); e.drain()
            e.copy_predicated(TMP[:, :, :], YM[:, :, :].bitcast(I32), BIG[:, 1:2].rearrange("p (a b) -> p a b", b=1).to_broadcast([128, NT3, D])); e.drain()
            e.tensor_tensor(X[:, :, :], X[:, :, :], TMP[:, :, :], ALU.add)

        def v_att(e, j):
            yield from normalize(e)
            for n in range(5):
                yield 5.5 + n
                e.wait_ge(*filled("front", j, "qkvB", n))
                dst = QT[:, 2 * n + 1, :] if n < 4 else VC[:, :]
                if n < 4:
                    ins = e.tensor_scalar(dst, PB[3][0:64, 0:TOK], float(1 / np.sqrt(np.float32(8))), None, ALU.mult)
                else:
                    ins = e.tensor_copy(dst, PB[3][0:64, 0:TOK])
                ins.then_inc(empt["front", 3], 1)
            def finish(b):
                e.wait_ge(*emptied("front", j, "scoreB", 3 * b + 2)); e.wait_ge(*emptied("front", j, "scoreA", 3 * b + 2))
                if b: e.wait_ge(*free("front", j, "z2", b)); e.wait_ge(*emptied("front", j, "z2", 0))
                e.reciprocal(DEN[:, 12 * b:12 * b + 12], DEN[:, 12 * b:12 * b + 12]); e.drain()
                e.tensor_tensor(WON[:, :, :].rearrange("p (a c) d -> p a c d", a=3),
                                WOT[:, :, :].rearrange("p (o c) d -> p o c d", o=1).to_broadcast([128, 3, 4, D]),
                                DEN[:, 12 * b:12 * b + 12].rearrange("p (a c o) -> p a c o", a=3, o=1).to_broadcast([128, 3, 4, D]),
                                ALU.mult).then_inc(S["rden"], 1)
            def z_out(b):
                e.wait_ge(*filled("front", j, "z", b))
                e.wait_ge(*filled("front", j, "z2", b))
                if b: e.wait_ge(*filled("front", j, "z2", b))
                e.tensor_copy(Z[:, 0:2, :].rearrange("p a b -> p (a b)"), PB[0][0:64, 0:384]).then_inc(empt["front", 0], 1)
                e.tensor_copy(Z[:, 2, :], PB[1][0:64, 0:192]).then_inc(empt["front", 1], 1)
            for n in range(12):
                yield 10.4 + n // 2
                name = ("scoreA", "scoreB")[n % 2]
                e.wait_ge(*filled("front", j, name, n // 2))
                e.tensor_reduce(NM[:, 2 * n:2 * n + 2], PB[bank("front", name)][:, 0:384].rearrange("p (a t) -> p a t", t=SEQ), AX.X, ALU.max, negate=True).then_inc(S["maxed"], 2)
                if n == 7: finish(0)
            yield 15.45
            z_out(0)
            yield 15.7
            finish(1)
            yield 16.6
            z_out(1)
            yield 17.5
            e.wait_ge(*filled("front", j, "att"))
            e.tensor_tensor(X[:, :, :], X[:, :, :], PB[2][:, 0:192].rearrange("p (t d) -> p t d", d=D), ALU.add).then_inc(empt["front", 2], 1)

        def v_pk(e, j):
            yield from normalize(e)
            for n in range(2):
                yield 5.5 + n
                e.wait_ge(*filled("front", j, "qpkB", n))
                e.tensor_copy(QPK[:, 2 * n + 1, :], PB[3][:, 0:TOK]).then_inc(empt["front", 3], 1)
            for t in range(NT3):
                yield 7.5 + t
                e.wait_ge(*filled("front", j, "simB", t))
                e.tensor_copy(SIM[:, t, 1, :], PB[3][:, :]).then_inc(empt["front", 3], 1)

        def v_top(e, j):
            for t in range(NT3):
                yield TOP_STEPS * t
                e.wait_ge(*emptied("front", j, "simA", t))
                fence(e)
                lists = [(p, h) for p in range(2) for h in range(H)]
                e.drain()
                for p, h in lists: e.max(V16[:, p, h, 0:8], SIM[:, t, p, 64 * h:64 * h + 64])
                e.drain()
                for p, h in lists:
                    if h == 0: yield TOP_STEPS * t + 1 + p
                    e.match_replace(SIMR[:, p, 64 * h:64 * h + 64], V16[:, p, h, 0:8], SIM[:, t, p, 64 * h:64 * h + 64], -FMAX)
                    e.max_index(I16[:, p, h, 0:8], V16[:, p, h, 0:8], SIM[:, t, p, 64 * h:64 * h + 64])
                yield TOP_STEPS * t + 3
                e.drain()
                for p, h in lists: e.max(V16[:, p, h, 8:16], SIMR[:, p, 64 * h:64 * h + 64])
                e.drain()
                for p, h in lists: e.max_index(I16[:, p, h, 8:16], V16[:, p, h, 8:16], SIMR[:, p, 64 * h:64 * h + 64])
                e.drain()
                yield TOP_STEPS * t + 4
                e.tensor_copy(IF[:, :, :, :].rearrange("p a h k -> p (a h k)"), I16[:, :, :, :].rearrange("p a h k -> p (a h k)")); e.drain()
                e.tensor_scalar(IF[:, 1, :, :], IF[:, 1, :, :], float(NK), None, ALU.mult); e.drain()
                e.tensor_tensor(IF[:, 1, :, :], IF[:, 1, :, :], HBASE[:, :].rearrange("p (h o) -> p h o", o=1).to_broadcast([128, H, TOPK]), ALU.add); e.drain()
                for src, dst in ((V16, C50), (IF, CI)):
                    at = 0
                    for i in range(8):
                        m = CAND[i]
                        e.tensor_tensor(dst[:, :, at:at + m], src[:, 0, :, i:i + 1].to_broadcast([128, H, m]), src[:, 1, :, 0:m], ALU.add)
                        at += m
                    e.tensor_tensor(dst[:, :, at:at + 8], src[:, 0, :, 8:16], src[:, 1, :, 0:1].to_broadcast([128, H, 8]), ALU.add)
                yield TOP_STEPS * t + 5
                e.drain()
                for h in range(H): e.max(FV[:, h, 0:8], C50[:, h, :])
                e.drain()
                for h in range(H):
                    e.match_replace(CR[:, h, :], FV[:, h, 0:8], C50[:, h, :], -FMAX)
                    e.max_index(FP[:, h, 0:8], FV[:, h, 0:8], C50[:, h, :])
                e.drain()
                for h in range(H): e.max(FV[:, h, 8:16], CR[:, h, :])
                e.drain()
                for h in range(H): e.max_index(FP[:, h, 8:16], FV[:, h, 8:16], CR[:, h, :])
                e.tensor_tensor(FS[:, :, :], FV[:, :, :], FV[:, :, 0:1].to_broadcast([128, H, TOPK]), ALU.subtract); e.drain().then_inc(S["shift_top"], 1)
                e.tensor_copy(PF[:, :, :], FP[:, :, :]); e.drain()
                for g in range(H // 2):
                    yield TOP_STEPS * t + 6 + g
                    e.tensor_tensor(EQ[:, :, :], IOTA[:, :].rearrange("p (o c) -> p o c", o=1).to_broadcast([128, 2 * TOPK, NC50]),
                                    PF[:, 2 * g:2 * g + 2, :].rearrange("p h (k o) -> p (h k) o", o=1).to_broadcast([128, 2 * TOPK, NC50]), ALU.is_equal)
                    yield TOP_STEPS * t + 6.33 + g
                    e.drain()
                    e.tensor_tensor(EQ[:, :, :].rearrange("p (h k) c -> p h k c", h=2), EQ[:, :, :].rearrange("p (h k) c -> p h k c", h=2),
                                    CI[:, 2 * g:2 * g + 2, :].rearrange("p h (o c) -> p h o c", o=1).to_broadcast([128, 2, TOPK, NC50]), ALU.mult)
                    yield TOP_STEPS * t + 6.67 + g
                    e.drain()
                    e.tensor_reduce(PF[:, 2 * g:2 * g + 2, :].rearrange("p h k -> p (h k)"), EQ[:, :, :], AX.X, ALU.add); e.drain()
                yield TOP_STEPS * t + 10
                e.tensor_copy(IDX[:, t, :, :], PF[:, :, :])
                e.wait_ge(*event("exp_top", j, t + 1))
                e.tensor_reduce(S8[:, 0, :], FS[:, :, :], AX.X, ALU.add); e.drain()
                e.reciprocal(S8[:, 1, :], S8[:, 0, :]); e.drain()
                e.tensor_tensor(WT[:, t, :, :], FS[:, :, :], S8[:, 1, :].rearrange("p (h o) -> p h o", o=1).to_broadcast([128, H, TOPK]), ALU.mult)
                e.drain().then_inc(S["kept_idx"], 1)

        def a_consume(e, i, u):
            yield u
            r = u % RING
            e.wait_ge(gath[r], (i * (NT3 * H // RING) + u // RING + 1) * 16 * TOPK)
            e.wait_ge(*event("kept_idx", i, u // H + 1))
            for k in range(TOPK):
                if k in (4, 8, 12): yield u + 0.03 * k
                m = e.activation(GATH[:, r, k, :], GATH[:, r, k, :], ACT.Copy, scale=WT[:, u // H, u % H, k:k + 1])
            m.then_inc(S["multiplied"], 1)

        def v_consume(e, i, u):
            yield u + 0.5
            e.wait_ge(*event("multiplied", i, u + 1))
            e.tensor_reduce(KV[:, u // H, u % H, :], GATH[:, u % RING, :, :].rearrange("p k d -> p d k"), AX.X, ALU.add).then_inc(S["gather_free"], 1)

        def v_keep_x(e, j):
            yield 0
            e.drain()
            e.wait_ge(*emptied("front", j, "pkT"))
            e.tensor_copy(XC[:, :, :], X[:, :, :])
            e.tensor_copy(NTC[:, :], NT4[:, :])
            e.drain().then_inc(S["kept_x"], 1)

        def v_back(e, i):
            yield 0
            e.drain().then_inc(S["weighted"], 1)
            for n in range(3):
                yield n + 0.5
                e.wait_ge(*filled("back", i, "kvB", n))
                kvt_out(e, 2 * n + 1).then_inc(empt["back", 3], 1)
            e.wait_ge(*filled("back", i, "kvA", 2))
            for n in range(4):
                yield 3.5 + n
                e.wait_ge(*filled("back", i, "q5B", n))
                e.tensor_scalar(Q5[:, 2 * n + 1, :], PB[3][0:64, 0:TOK], D ** -0.5, None, ALU.mult).then_inc(empt["back", 3], 1)
            for n in range(12):
                yield 10.4 + n // 2
                b, ib, half = n // 6, n // 2 % 3, n % 2
                name = ("s5A", "s5B")[half]
                jn = 64 * (ib + 1)
                s = PB[bank("back", name)][:, 0:384].rearrange("p (a t) -> p a t", t=SEQ)
                e.wait_ge(*filled("back", i, name, n // 2))
                fence(e)
                e.copy_predicated(s[:, :, jn - 64:jn], LATER[:, :].rearrange("p (o c) -> p o c", o=1).to_broadcast([128, 2, D]),
                                  NEG[:, 0:1].rearrange("p (a b) -> p a b", b=1).to_broadcast([128, 2, D])); e.drain()
                sl = n // 2 % 2
                e.tensor_reduce(NM5[:, sl, 2 * half:2 * half + 2], s[:, :, 0:jn], AX.X, ALU.max, negate=True).then_inc(S["maxed5"], 1)
                if half == 0 and n > 0: v_scale5(e, i, n // 2 - 1)
                if half == 0 and n > 2: v_out5(e, i, n // 2 - 2)
            yield 16.3
            v_scale5(e, i, 5)
            v_out5(e, i, 4)
            yield 17
            v_out5(e, i, 5)
            e.drain().then_inc(S["out_sb"], 1)

        def v_out5(e, i, nb):
            e.wait_ge(*filled("back", i, "out", nb))
            if nb == 0: e.wait_ge(*event("stored", i - 1, 16))
            p, t = slice(64 * (nb % 2), 64 * (nb % 2) + 64), nb // 2
            e.tensor_tensor(OUTB[p, t, :], XC[p, t, :], PB[1][p, 64 * t:64 * t + 64], ALU.add).then_inc(empt["back", 1], 1)

        def v_scale5(e, i, nb):
            sl, jn = nb % 2, 64 * (nb % 3 + 1)
            e.wait_ge(*emptied("back", i, "s5A", nb)); e.wait_ge(*emptied("back", i, "s5B", nb))
            e.reciprocal(DEN5[:, sl, :], DEN5[:, sl, :]); e.drain()
            e.tensor_tensor(P5[:, sl, :, 0:jn], P5[:, sl, :, 0:jn], DEN5[:, sl, :].rearrange("p (h o) -> p h o", o=1).to_broadcast([128, 4, jn]), ALU.mult).then_inc(S["scaled5"], 1)

        def kvt_out(e, n):
            t, hh = n // 2, n % 2
            dst = KVT[:, 4 * hh:4 * hh + 4, 128 * t:128 * t + 128]
            src = PB[2 + n % 2][:, :].rearrange("p (h n) -> p h n", n=128)
            return e.tensor_copy(dst, src) if n % 2 else e.activation(dst, src, ACT.Copy)

        def a_rnn(e, j):
            yield 4.4
            e.wait_ge(*filled("front", j, "xT"))
            e.activation(RS[0:64, :, :].rearrange("p a b -> p (a b)"), PB[0][0:64, 0:TOK], ACT.Copy).then_inc(empt["front", 0], 1)
            for s in range(2):
                yield 5.5 + s
                e.wait_ge(*filled("front", j, "rnn", s))
                e.activation(RS[64:128, 1 - s, :], PB[1][64:128, 0:SEQ], ACT.Tanh, bias=BSUM[64:128, :]).then_inc(empt["front", 1], 1)

        def a_moe(e, j):
            yield 4.3
            e.wait_ge(*filled("front", j, "moeT"))
            e.activation(NTR[0:64, :], PB[0][0:64, 0:TOK], ACT.Copy).then_inc(empt["front", 0], 1)
            yield 5
            e.wait_ge(*event("shifted", j, 1))
            e.activation(LE[:, :, :], LG[:, :, :], ACT.Exp).then_inc(S["exped"], 1)
            yield 5.2
            for n in range(16):
                name = ("hidA", "hidB")[n % 2]
                if n >= 2 and n % 2 == 0: yield 6.5 + n // 2
                e.wait_ge(*filled("front", j, name, n // 2))
                e.activation(HID[:, n % 4, :], PB[2 + n % 2][:, 0:TOK], ACT.Relu).then_inc(empt["front", 2 + n % 2], 1)

        def a_att(e, j):
            yield 4.4
            e.wait_ge(*filled("front", j, "attT"))
            e.activation(NTR[0:64, :], PB[0][0:64, 0:TOK], ACT.Copy).then_inc(empt["front", 0], 1)
            for n in range(5):
                yield 5.5 + n
                e.wait_ge(*filled("front", j, "qkvA", n))
                e.activation(QT[:, 2 * n, :] if n < 4 else KT[:, :], PB[2][0:64, 0:TOK], ACT.Copy, scale=float(1 / np.sqrt(np.float32(8))) if n < 4 else 1.0).then_inc(empt["front", 2], 1)
            for n in range(12):
                yield 10.6 + n // 2
                name = ("scoreA", "scoreB")[n % 2]
                e.wait_ge(*event("maxed", j, 2 * n + 2))
                for a in range(2):
                    ins = e.activation(P[:, 2 * n + a, :], PB[2 + n % 2][:, SEQ * a:SEQ * a + SEQ], ACT.Exp, bias=NM[:, 2 * n + a:2 * n + a + 1], accum_out=DEN[:, 2 * n + a:2 * n + a + 1])
                ins.then_inc(empt["front", 2 + n % 2], 1)

        def a_pk(e, j):
            yield 4.4
            e.wait_ge(*filled("front", j, "pkT"))
            e.wait_ge(*event("kept_x", j - 1, 1))
            e.activation(NT4[:, :], PB[0][0:64, 0:TOK], ACT.Copy).then_inc(empt["front", 0], 1)
            for n in range(2):
                yield 5.5 + n
                e.wait_ge(*filled("front", j, "qpkA", n))
                e.activation(QPK[:, 2 * n, :], PB[2][:, 0:TOK], ACT.Copy).then_inc(empt["front", 2], 1)
            for t in range(NT3):
                yield 7.5 + t
                e.wait_ge(*filled("front", j, "simA", t))
                e.activation(SIM[:, t, 0, :], PB[2][:, :], ACT.Copy).then_inc(empt["front", 2], 1)

        def a_top(e, j):
            for t in range(NT3):
                yield TOP_STEPS * t + 6.3
                e.wait_ge(*event("shift_top", j, t + 1))
                e.activation(FS[:, :, :], FS[:, :, :], ACT.Exp).then_inc(S["exp_top"], 1)

        def a_back(e, i):
            for n in range(3):
                yield n + 0.5
                e.wait_ge(*filled("back", i, "kvA", n))
                kvt_out(e, 2 * n).then_inc(empt["back", 2], 1)
            for n in range(4):
                yield 3.5 + n
                e.wait_ge(*filled("back", i, "q5A", n))
                e.activation(Q5[:, 2 * n, :], PB[2][0:64, 0:TOK], ACT.Copy, scale=D ** -0.5).then_inc(empt["back", 2], 1)
            for n in range(3):
                yield 7.5 + n
                e.wait_ge(*filled("back", i, "vwA", n))
                e.activation(VW[:, n, :, :].rearrange("p h d -> p (h d)"), PB[2][:, :], ACT.Copy).then_inc(empt["back", 2], 1)
            for n in range(12):
                yield 10.6 + n // 2
                half, nb = n % 2, n // 2
                jn = 64 * (nb % 3 + 1)
                if half == 0 and nb >= 2: e.wait_ge(*emptied("back", i, "pt0", nb - 2))
                e.wait_ge(*event("maxed5", i, n + 1))
                for a in range(2):
                    hp = 2 * half + a
                    ins = e.activation(P5[:, nb % 2, hp, 0:jn], PB[2 + half][:, SEQ * a:SEQ * a + jn], ACT.Exp, bias=NM5[:, nb % 2, hp:hp + 1], accum_out=DEN5[:, nb % 2, hp:hp + 1])
                ins.then_inc(empt["back", 2 + half], 1)
                if half == 1 and nb >= 1:
                    yield 10.8 + nb
                    a_pt(e, i, nb - 1)
            yield 16.8
            a_pt(e, i, 5)

        def spans(nb):
            b, jn = nb // 3, 64 * (nb % 3 + 1)
            cut = (0, 128, 192) if b == 0 else (0, 64, 192)
            out = []
            for lo, hi in zip(cut, cut[1:]):
                hi = min(hi, jn)
                if hi > lo:
                    n = SEQ * b + lo
                    out.append((lo, hi, n % 128, n // 128))
            return out

        def slot(c, p0):
            return 2 if p0 else c

        def a_pt(e, i, nb):
            e.wait_ge(*filled("back", i, "pt0", nb))
            sp = spans(nb)
            for c, (lo, hi, p0, t) in enumerate(sp):
                ins = e.activation(PT[p0:p0 + hi - lo, slot(c, p0), :], PTB[c][p0:p0 + hi - lo, :], ACT.Copy)
            ins.then_inc(empt["back", 0], 1)
        PTB = [PB[0], PB[1]]


        def t_turn(e, j, name, k):
            e.wait_ge(*event("normed", j, k))
            e.wait_ge(*free("front", j, name))
            fence(e)
            for t in range(NT3):
                m = e.transpose(PB[0][0:64, 128 * t:128 * t + 128], N[:, t, :], ID[:, :])
            m.then_inc(full["front", 0], 1)

        def t_rnn(e, j):
            yield 4
            if not (isinstance(j, int) and j == 0): e.wait_ge(*event("out_sb", j - 2, 1))
            t_turn(e, j, "xT", 1)
            e.wait_ge(*emptied("front", j, "xT"))
            for s in range(2):
                yield 5 + s
                e.wait_ge(*free("front", j, "rnn", s))
                fence(e)
                e.matmul(PB[1][64:128, 0:SEQ], WRNN[:, :], RS[:, s, :], start=True, stop=True).then_inc(full["front", 1], 1)
            yield 7
            e.wait_ge(*emptied("front", j, "rnn", 1))
            e.wait_ge(*free("front", j, "rnn_back"))
            fence(e)
            i64 = ID[64:128, 64:128]
            e.transpose(PB[2][:, 0:64], RS[64:128, 1, 0:128], i64)
            e.transpose(PB[2][0:64, 64:128], RS[64:128, 1, 128:192], i64)
            e.matmul(PB[2][64:128, 64:128], RS[64:128, 0, 0:64], i64, start=True, stop=True)
            e.transpose(PB[2][:, 128:192], RS[64:128, 0, 64:192], i64).then_inc(full["front", 2], 1)

        def t_moe(e, j):
            yield 4
            t_turn(e, j, "moeT", 2)
            yield 4.5
            e.wait_ge(*emptied("front", j, "moeT"))
            e.wait_ge(*free("front", j, "gate"))
            fence(e)
            for t in range(NT3):
                m = e.matmul(PB[1][:, 8 * t:8 * t + 8], NTR[:, 128 * t:128 * t + 128], GW[:, :], start=True, stop=True)
            m.then_inc(full["front", 1], 1)
            def hid(n):
                name = ("hidA", "hidB")[n % 2]
                e.wait_ge(*free("front", j, name, n // 2))
                fence(e)
                e.matmul(PB[2 + n % 2][:, 0:TOK], W1[:, 128 * n:128 * n + 128], NTR[:, :], start=True, stop=True).then_inc(full["front", 2 + n % 2], 1)
            yield 4.6
            hid(0); hid(1)
            yield 6
            e.wait_ge(*event("one_hot", j, 1))
            e.wait_ge(*free("front", j, "place"))
            fence(e)
            for t in range(NT3):
                e.matmul(PB[1][:, 8 * t:8 * t + 8], TRI[:, :], OH[:, t, :], start=True, stop=False)
                for s in range(t):
                    e.matmul(PB[1][:, 8 * t:8 * t + 8], ONES[:, :], OH[:, s, :], start=False, stop=False)
                m = e.matmul(PB[1][:, 8 * t:8 * t + 8], ONES[:, :], OHS[:, :], start=False, stop=True)
            m.then_inc(full["front", 1], 1)
            for x in range(E):
                yield 7 + x
                if x + 1 < E: hid(2 * x + 2); hid(2 * x + 3)
                yield 7.1 + x
                name = ("expert", "expertB")[x % 2]
                b = bank("front", name)
                e.wait_ge(*free("front", j, name, x // 2))
                e.wait_ge(*emptied("front", j, "hidA", x)); e.wait_ge(*emptied("front", j, "hidB", x))
                fence(e)
                for t in range(NT3):
                    o = PB[b][:, 64 * t:64 * t + 64]
                    e.matmul(o, ONES[0:1, :], B2[:, 64 * x:64 * x + 64], start=True, stop=False)
                    for f in range(2):
                        n = 2 * x + f
                        m = e.matmul(o, HID[:, n % 4, 128 * t:128 * t + 128], W2[:, 64 * n:64 * n + 64], start=False, stop=(f == 1))
                m.then_inc(full["front", b], 1)

        def t_att(e, j):
            yield 4
            t_turn(e, j, "attT", 3)
            e.wait_ge(*emptied("front", j, "attT"))
            for n in range(10):
                yield 5 + n // 2
                name = ("qkvA", "qkvB")[n % 2]
                e.wait_ge(*free("front", j, name, n // 2))
                fence(e)
                w = WQ[:, 64 * n:64 * n + 64] if n < 8 else (WK, WV)[n - 8][:, :]
                e.matmul(PB[2 + n % 2][0:64, 0:TOK], w, NTR[0:64, :], start=True, stop=True).then_inc(full["front", 2 + n % 2], 1)
            e.wait_ge(*emptied("front", j, "qkvA", 4)); e.wait_ge(*emptied("front", j, "qkvB", 4))
            def scores(n):
                name = ("scoreA", "scoreB")[n % 2]
                e.wait_ge(*free("front", j, name, n // 2))
                fence(e)
                for a in range(2):
                    rt = 2 * n + a
                    b, pp, jj = rt // 12, rt % 12 // 4, rt % 4
                    for h2 in range(2):
                        u = 3 * (2 * jj + h2) + pp
                        r, h = u // 8, u % 8
                        m = e.matmul(PB[2 + n % 2][64 * h2:64 * h2 + 64, SEQ * a:SEQ * a + SEQ], QT[:, h, SEQ * b + r:SEQ * b + r + 190:3], KT[:, SEQ * b:SEQ * b + SEQ], start=True, stop=True)
                m.then_inc(full["front", 2 + n % 2], 1)
            def zs(b):
                e.wait_ge(*event("rden", j, b + 1))
                e.wait_ge(*free("front", j, "z", b)); e.wait_ge(*free("front", j, "z2", b))
                fence(e)
                for jc in range(3):
                    for pp in range(3):
                        o = PB[0][0:64, 192 * jc + 64 * pp:192 * jc + 64 * pp + 64] if jc < 2 else PB[1][0:64, 64 * pp:64 * pp + 64]
                        for jj in range(4):
                            m = e.matmul(o, P[:, 12 * b + 4 * pp + jj, jc:jc + 190:3], WON[:, 4 * pp + jj, :], start=(jj == 0), stop=(jj == 3))
                    if jc == 1: m.then_inc(full["front", 0], 1)
                m.then_inc(full["front", 1], 1)
            def outs(b):
                e.wait_ge(*emptied("front", j, "z", b)); e.wait_ge(*emptied("front", j, "z2", b))
                if b == 0: e.wait_ge(*free("front", j, "att"))
                fence(e)
                for pp in range(3):
                    nb = 3 * b + pp
                    for jc in range(3):
                        m = e.matmul(PB[2][64 * (nb % 2):64 * (nb % 2) + 64, 64 * (nb // 2):64 * (nb // 2) + 64],
                                     VC[:, SEQ * b + 64 * jc:SEQ * b + 64 * jc + 64], Z[:, jc, 64 * pp:64 * pp + 64], start=(jc == 0), stop=(jc == 2))
                if b: m.then_inc(full["front", 2], 1)
            for n in range(12):
                yield 10 + n // 2
                scores(n)
                if n == 9:
                    yield 14.5
                    zs(0)
            yield 16
            outs(0)
            yield 16.1
            zs(1)
            yield 17
            outs(1)

        def t_pk(e, j):
            yield 4
            t_turn(e, j, "pkT", 4)
            e.wait_ge(*emptied("front", j, "pkT"))
            for n in range(4):
                yield 5 + n // 2
                name = ("qpkA", "qpkB")[n % 2]
                e.wait_ge(*free("front", j, name, n // 2))
                fence(e)
                e.matmul(PB[2 + n % 2][:, 0:TOK], WPK[:, 128 * n:128 * n + 128], NT4[:, :], start=True, stop=True).then_inc(full["front", 2 + n % 2], 1)
            e.wait_ge(*emptied("front", j, "qpkA", 1)); e.wait_ge(*emptied("front", j, "qpkB", 1))
            for t in range(NT3):
                yield 7 + t
                for p in range(2):
                    name = ("simA", "simB")[p]
                    e.wait_ge(*free("front", j, name, t))
                    fence(e)
                    for hh in range(2):
                        m = e.matmul(PB[2 + p][:, 256 * hh:256 * hh + 256], QPK[:, 2 * p + hh, 128 * t:128 * t + 128], KB[:, 2 * p + hh, :], start=True, stop=True)
                    m.then_inc(full["front", 2 + p], 1)

        def t_back(e, i):
            yield 0
            e.wait_ge(*event("weighted", i, 1))
            for n in range(6):
                yield n // 2
                t, hh = n // 2, n % 2
                e.wait_ge(*free("back", i, ("kvA", "kvB")[n % 2], n // 2))
                fence(e)
                for h in range(4):
                    m = e.transpose(PB[2 + n % 2][:, 128 * h:128 * h + 128], KV[:, t, 4 * hh + h, :], ID[:, :])
                m.then_inc(full["back", 2 + n % 2], 1)
            for n in range(8):
                yield 3 + n // 2
                name = ("q5A", "q5B")[n % 2]
                e.wait_ge(*free("back", i, name, n // 2))
                fence(e)
                e.matmul(PB[2 + n % 2][0:64, 0:TOK], WQ5[:, 64 * n:64 * n + 64], NTC[:, :], start=True, stop=True).then_inc(full["back", 2 + n % 2], 1)
            yield 7
            e.wait_ge(*emptied("back", i, "kvA", 2)); e.wait_ge(*emptied("back", i, "kvB", 2))
            for t in range(NT3):
                yield 7 + t
                e.wait_ge(*free("back", i, "vwA", t))
                fence(e)
                for h in range(H):
                    m = e.matmul(PB[2][:, 64 * h:64 * h + 64], KVT[64:128, h, 128 * t:128 * t + 128], WO5[64:128, h, :], start=True, stop=True)
                m.then_inc(full["back", 2], 1)
            def sims(n):
                b, ib, half = n // 6, n // 2 % 3, n % 2
                jn = 64 * (ib + 1)
                e.wait_ge(*free("back", i, ("s5A", "s5B")[half], n // 2))
                fence(e)
                for a in range(2):
                    for h2 in range(2):
                        h = 2 * (2 * half + a) + h2
                        m = e.matmul(PB[2 + half][64 * h2:64 * h2 + 64, SEQ * a:SEQ * a + jn], Q5[:, h, SEQ * b + 64 * ib:SEQ * b + 64 * ib + 64], KVT[0:64, h, SEQ * b:SEQ * b + jn], start=True, stop=True)
                m.then_inc(full["back", 2 + half], 1)
            def turnp(nb):
                e.wait_ge(*event("scaled5", i, nb + 1))
                e.wait_ge(*free("back", i, "pt0", nb)); e.wait_ge(*free("back", i, "out", nb))
                fence(e)
                for c, (lo, hi, p0, t) in enumerate(spans(nb)):
                    for hp in range(4):
                        o = PTB[c][p0:p0 + hi - lo, 128 * hp:128 * hp + 128]
                        m = (e.matmul(o, P5[:, nb % 2, hp, lo:hi], ID[:, :], start=True, stop=True) if p0
                             else e.transpose(o, P5[:, nb % 2, hp, lo:hi], ID[:, :]))
                m.then_inc(full["back", 0], 1)
            def outs(nb):
                e.wait_ge(*emptied("back", i, "pt0", nb))
                if nb == 0: e.wait_ge(*emptied("back", i, "vwA", 2))
                fence(e)
                o = PB[1][64 * (nb % 2):64 * (nb % 2) + 64, 64 * (nb // 2):64 * (nb // 2) + 64]
                sp = spans(nb)
                for h in range(H):
                    for c, (lo, hi, p0, t) in enumerate(sp):
                        m = e.matmul(o, PT[0:p0 + hi - lo, slot(c, p0), 64 * h:64 * h + 64], VW[0:p0 + hi - lo, t, h, :],
                                     start=(h == 0 and c == 0), stop=(h == H - 1 and c == len(sp) - 1))
                m.then_inc(full["back", 1], 1)
            e.wait_ge(*emptied("back", i, "q5A", 3)); e.wait_ge(*emptied("back", i, "q5B", 3))
            yield 10
            sims(0); sims(1)
            for nb in range(6):
                yield 11 + nb
                if nb < 5: sims(2 * nb + 2); sims(2 * nb + 3)
                yield 11.6 + nb
                turnp(nb)
                yield 11.9 + nb
                outs(nb)

        def rounds(e, sections):
            def run(windows, i, j, g, l):
                engine, begun = sections(e, i, j, g, l), {}
                for chains in windows:
                    weave(engine, chains, begun)
            run([[whole("coords")]], None, None, 0, None)
            with e.Fori(0, LAYERS) as l:
                run([[whole("forward0", "forward1", "mix", "inverse0", "inverse1")]], None, None, 0, l)
            run([[whole("tokens")]], None, None, 0, None)
            run(a_round(begin=("coords",), rows=False, back=False), None, 0, 1, 0)
            def until_stored(i, g):
                with e.Fori(0, LAYERS - 2) as l:
                    run(a_round(), i + l, i + l + 1, g, l + 1)
                run(a_round(end=("tokens",)), i + LAYERS - 2, i + LAYERS - 1, g, LAYERS - 1)
            with e.Fori(1, GROUPS - 1) as g:
                until_stored((g - 1) * LAYERS, g)
                run(a_round(begin=("coords",)), g * LAYERS - 1, g * LAYERS, g + 1, 0)
            until_stored((GROUPS - 2) * LAYERS, GROUPS - 1)
            with e.Fori((GROUPS - 1) * LAYERS - 1, PAIRS - 1) as i:
                run(a_round(layer=False), i, i + 1, GROUPS, None)
            run([[[("rows", U0, NT3 * H)]], [whole("back")]], PAIRS - 1, None, None, None)

        def units(consume, e, i, first):
            def steps():
                for u in range(first, NT3 * H): yield from consume(e, i, u)
            return steps

        def QUEUE(e, i, j, g, l):
            return {"coords": lambda: sp_coords(e, g), "forward0": lambda: sp_forward(e, g, l, 0), "mix": lambda: sp_mix(e, g, l),
                    "tokens": lambda: sp_tokens(e, g), "rnn": lambda: sp_front(e, j, g), "back": lambda: sp_back(e, i)}

        def TENSOR(e, i, j, g, l):
            return {"coords": lambda: t_coords(e, g), "forward0": lambda: t_forward(e, g, l, 0), "forward1": lambda: t_forward(e, g, l, 1),
                    "mix": lambda: t_mix(e, g, l), "inverse0": lambda: t_inverse(e, g, l, 0), "inverse1": lambda: t_inverse(e, g, l, 1),
                    "tokens": lambda: t_tokens(e, g), "rnn": lambda: t_rnn(e, j), "moe": lambda: t_moe(e, j), "att": lambda: t_att(e, j),
                    "pk": lambda: t_pk(e, j), "back": lambda: t_back(e, i)}

        def SCALAR(e, i, j, g, l):
            return {"coords": lambda: a_coords(e, g), "forward0": lambda: a_forward(e, g, l, 0), "forward1": lambda: a_forward(e, g, l, 1),
                    "mix": lambda: a_mix(e, g, l), "inverse0": lambda: a_inverse(e, g, l, 0), "inverse1": lambda: a_inverse(e, g, l, 1),
                    "tokens": lambda: a_tokens(e, g), "rnn": lambda: a_rnn(e, j), "moe": lambda: a_moe(e, j), "att": lambda: a_att(e, j),
                    "pk": lambda: a_pk(e, j), "top": lambda: a_top(e, j), "back": lambda: a_back(e, i),
                    "rows": units(a_consume, e, i, U0), "next_rows": units(a_consume, e, j, 0)}

        def VECTOR(e, i, j, g, l):
            return {"forward0": lambda: v_forward(e, g, l, 0), "forward1": lambda: v_forward(e, g, l, 1),
                    "inverse0": lambda: v_inverse(e, g, l, 0), "inverse1": lambda: v_inverse(e, g, l, 1),
                    "tokens": lambda: v_tokens(e, g), "rnn": lambda: v_rnn(e, j), "moe": lambda: v_moe(e, j), "att": lambda: v_att(e, j),
                    "pk": lambda: v_pk(e, j), "top": lambda: v_top(e, j), "back": lambda: v_back(e, i), "keep_x": lambda: v_keep_x(e, j),
                    "rows": units(v_consume, e, i, U0), "next_rows": units(v_consume, e, j, 0)}

        @block.sync
        def _(e):
            sp_setup(e)
            rounds(e, QUEUE)
            e.wait_ge(*event("stored", PAIRS - 1, 16))

        @block.gpsimd
        def _(e):
            def before(e):
                for t in (KB, ONES, RS, OHS, AREA4, FW0, FW1, FW2, CONV):
                    e.memset(t[:], 1.0 if t is ONES else 0.0).then_inc(zeroed, 1)
            before(e)
            with e.Fori(0, PAIRS) as i:
                pool_gather(e, i)

        @block.vector
        def _(e):
            def before(e):
                credits(e, ["normed", "shifted", "one_hot", "maxed", "rden", "shift_top", "kept_idx", "kept_x", "gather_free", "weighted", "maxed5", "scaled5", "out_sb"],
                        [(k, b) for k in PLANS for b in range(4)])
                e.sem_inc(tp_out, CREDIT); e.sem_inc(tp_full, CREDIT)
                e.memset(NTR[64:65, :], 1.0); e.memset(NEG[:, :], -FMAX); e.memset(BIG[:, 0:1], 1e4); e.memset(BIG[:, 1:2], -1e4)
                e.wait_ge(const_in, 16 * NLOADS)
                e.tensor_tensor(BSUM[64:128, :], BRNN[64:128, 0:1], BRNN[64:128, 1:2], ALU.add)
                e.drain().then_inc(zeroed, 1)
            before(e)
            rounds(e, VECTOR)

        @block.scalar
        def _(e):
            def before(e):
                credits(e, ["exped", "exp_top", "multiplied"])
                e.sem_inc(mm_out, CREDIT); e.sem_inc(mm_full, CREDIT)
                e.wait_ge(const_in, 16 * NLOADS); e.wait_ge(zeroed, 10)
            before(e)
            rounds(e, SCALAR)

        @block.tensor
        def _(e):
            def before(e):
                e.wait_ge(const_in, 16 * NLOADS); e.wait_ge(zeroed, 10)
            before(e)
            rounds(e, TENSOR)


def layouts(inputs):
    g = {n: np.asarray(a) for n, a in inputs.items()}
    return [
        g["x"].transpose(0, 3, 1, 2).reshape(B * 3, POS),
        np.concatenate([g["L0_tok_fc0_w"], g["L0_tok_fc0_b"][None]], 0),
        np.stack([g[f"L0_tok_sw{n}"] for n in range(LAYERS)]).reshape(LAYERS, WID, WID, MODES, Q4, CHUNKS)
          .transpose(0, 5, 4, 1, 3, 2).reshape(LAYERS * CHUNKS * 128, MODES * WID),
        np.concatenate([np.concatenate([g[f"L0_tok_cw{n}"].T, g[f"L0_tok_cb{n}"][:, None]], 1) for n in range(LAYERS)], 0),
        np.concatenate([g["L0_tok_fc1_w"], g["L0_tok_fc1_b"][None]], 0),
        np.concatenate([g["L0_tok_fc2_w"], g["L0_tok_fc2_b"][None]], 0),
        *fourier_constants(),
        g["txt"].reshape(B * 128, D),
        np.concatenate([g["L0_attn_W_ih"].T, g["L0_attn_W_hh"].T], 0),
        np.stack([g["L0_attn_b_ih"], g["L0_attn_b_hh"]]),
        np.concatenate([g["L0_ffn_gate_w"], g["L0_ffn_gate_b"][None]], 0),
        np.concatenate([g["L0_ffn_w1"].transpose(1, 0, 2).reshape(D, E * FF), g["L0_ffn_b1"].reshape(1, E * FF)], 0),
        g["L0_ffn_w2"].reshape(E, 2, 128, D).transpose(2, 0, 1, 3).reshape(128, 2 * E * D),
        g["L0_ffn_b2"].reshape(1, E * D),
        g["L1_attn_Wq"].T, g["L1_attn_Wk"].T, g["L1_attn_Wv"].T,
        g["L1_attn_Wo"].T.reshape(64, 4, 2, D).transpose(2, 0, 1, 3).reshape(128, 4 * D),
        g["L1_ffn_Wq_pk"],
        g["L1_ffn_pk_keys"].transpose(0, 2, 3, 1).reshape(2 * H * 32, NK),
        g["L1_ffn_Wq"],
        g["L1_ffn_Wo"].reshape(H, D, D).transpose(1, 0, 2).reshape(D, H * D),
        np.concatenate([g["L1_ffn_keys_table"], g["L1_ffn_values_table"]], 1),
        *shape_constants(),
    ]


def shape_constants():
    row = np.arange(128)
    every = lambda v: np.tile(np.asarray(v, np.float32), (128, 1))
    return [
        np.eye(128, dtype=np.float32),
        np.triu(np.ones((128, 128), np.float32)),
        every(np.arange(NC50)),
        every(E - np.arange(E)),
        every(NK * NK * np.arange(H)),
        (np.arange(D)[None, :] > (row % D)[:, None]).astype(np.int32),
    ]


_NAMES = ["xT", "fc0", "sw", "cwb", "fc1", "fc2", "f1", "f2", "g3", "g4", "txt", "wrnn", "brnn", "gw", "w1", "w2", "b2", "wq", "wk", "wv",
          "wot", "wpk", "keysT", "wq5", "wo5", "table", "ident", "tri", "iota", "eight", "hbase", "later"]


def kernel(**inputs):
    import concourse.bacc as _bacc
    from concourse.bass_utils import run_bass_kernel_spmd as _run

    nc = _bacc.Bacc("TRN2", target_bir_lowering=False, num_devices=1)
    arrays, args = {}, []
    for name, a in zip(_NAMES, layouts(inputs)):
        a = np.ascontiguousarray(a)
        arrays[f"in_{name}"] = a
        args.append(nc.dram_tensor(f"in_{name}", a.shape, mybir.dt.from_np(a.dtype), kind="ExternalInput").ap())
    args.append(nc.dram_tensor("out", (B * SEQ, D), F32, kind="ExternalOutput").ap())
    early_fusion(nc, *args)
    r = _run(nc, [arrays], core_ids=[0])
    return r.results[0]["out"].reshape(B, SEQ, D)
```

```python
import numpy as np
import concourse.bass as bass
from concourse import mybir
from contextlib import ExitStack

F32 = mybir.dt.float32
I32 = mybir.dt.int32
U32 = mybir.dt.uint32
ALU = mybir.AluOpType
ACT = mybir.ActivationFunctionType
AX = mybir.AxisListType

B, SIDE, WID, MODES, LAYERS = 32, 64, 32, 20, 4
Q4 = 4
GB = 1
GROUPS = B // (Q4 * GB)
POS = SIDE * SIDE
ROWQ = POS // 512
CHUNKS = MODES // Q4
KWQ = CHUNKS * MODES * 2
F_T = ROWQ + CHUNKS
I_T = CHUNKS + ROWQ
T_LAYER = GB * (F_T + I_T)
M_LAYER = GB * F_T + CHUNKS + GB * I_T
M_IN = GB * ROWQ
M_GROUP = M_IN + LAYERS * M_LAYER + GB * ROWQ * 2
T_GROUP = LAYERS * T_LAYER + GB * ROWQ
CREDIT = 2


def fourier_constants():
    k, p = np.arange(MODES), np.arange(SIDE)
    ang = 2 * np.pi * np.outer(p, k) / SIDE
    cos, sin = np.cos(ang), np.sin(ang)
    f1 = np.zeros((2, SIDE, 2, MODES, 2))
    for a in range(2):
        f1[a, :, a, :, 0], f1[a, :, a, :, 1] = cos, -sin
    f2 = np.zeros((SIDE, 2, MODES, 2))
    f2[:, 0, :, 0], f2[:, 1, :, 0] = cos, sin
    f2[:, 0, :, 1], f2[:, 1, :, 1] = -sin, cos
    f2 /= SIDE
    g3 = np.zeros((MODES, 2, SIDE, 2))
    g3[:, 0, :, 0], g3[:, 1, :, 0] = cos.T, -sin.T
    g3[:, 0, :, 1], g3[:, 1, :, 1] = sin.T, cos.T
    twice = np.where(k == 0, 1.0, 2.0)[:, None] / SIDE
    g4 = np.zeros((2, MODES, 2, 2, SIDE))
    for a in range(2):
        g4[a, :, 0, a], g4[a, :, 1, a] = twice * cos.T, -twice * sin.T
    return [np.ascontiguousarray(x, np.float32) for x in (
        f1.reshape(128, 80), f2.reshape(128, 40), g3.reshape(40, 128), g4.reshape(80, 128))]



SEQ, D = 192, 64
PAIRS = B // 2
TOK = 2 * SEQ
NT3 = TOK // 128
E, FF, CAP = 8, 256, 960
H, TOPK, NK = 8, 16, 64
CANDIDATES = [(0, 1, 0, 8), (1, 1, 0, 4), (2, 1, 0, 2), (3, 1, 0, 2), (4, 4, 0, 1),
              (0, 1, 8, 8), (1, 1, 4, 4), (2, 1, 2, 3), (3, 1, 2, 2), (4, 1, 1, 2), (5, 3, 1, 1), (8, 8, 0, 1)]
NC20 = sum(n * m for _, n, _, m in CANDIDATES[:5])
NC50 = sum(n * m for _, n, _, m in CANDIDATES)
assert sorted((i, j) for i0, n, j0, m in CANDIDATES for i in range(i0, i0 + n) for j in range(j0, j0 + m)) == [
    (i, j) for i in range(TOPK) for j in range(TOPK) if (i + 1) * (j + 1) <= TOPK]
LOOKUPS = [(h, 4, 0, NC20) for h in (0, 4)] + [(h, 2, 8, NC50) for h in (0, 2, 4, 6)]
EPS = 1e-5
FMAX = float(np.finfo(np.float32).max)
RING = 4

FRONT = [("xT", 0, 1), ("rnn", 1, 2), ("rnn_back", 2, 1),
         ("moeT", 0, 1), ("gate", 1, 1), ("place", 1, 1), ("hidA", 2, 8), ("hidB", 3, 8), ("expert", 0, 4), ("expertB", 1, 4),
         ("attT", 0, 1), ("qkvA", 2, 5), ("qkvB", 3, 5), ("scoreA", 2, 6), ("scoreB", 3, 6),
         ("z", 0, 2), ("z2", 1, 2), ("att", 2, 1),
         ("pkT", 0, 1), ("qpkA", 2, 2), ("qpkB", 3, 2), ("simA", 2, 3), ("simB", 3, 3)]
BACK = [("kvA", 2, 3), ("kvB", 3, 3), ("q5A", 2, 4), ("q5B", 3, 4), ("vwA", 2, 3), 
        ("s5A", 2, 6), ("s5B", 3, 6), ("pt0", 0, 6), ("out", 1, 6)]


def number(plan, name, k):
    at = 0
    bank = next(b for n, b, _ in plan if n == name)
    for n, b, c in plan:
        if n == name:
            return bank, at + k
        if b == bank:
            at += c


def total(plan, bank):
    return sum(c for _, b, c in plan if b == bank)


PLANS = {"front": FRONT, "back": BACK}




TOP_STEPS = 11
STEPS = {"coords": [2.2] * (GB * ROWQ), "forward0": [1.7] * F_T, "mix0": [5.3] * CHUNKS, "inverse0": [2.8] * CHUNKS + [2.2] * ROWQ,
         "tokens": [3.5] * (GB * ROWQ),
         "rnn": [4, 3, 2.5, 2.5, 1.2, 1.2, 1.2, 1.2], "moe": [2, 2.5, 2.5, 2.5, 3, 3, 2] + [5] * E + [6],
         "att": [2, 2.5, 2.5, 2.5, 1.5] + [3] * 5 + [3.3] * 6 + [5, 5], "pk": [2, 2.5, 2.5, 2.5, 1.5, 2.5, 2.5, 2.7, 2.7, 2.7],
         "top": [3, 3, 3, 3, 4, 4, 4, 4, 4, 4, 2] * NT3,
         "back": [3.5] * 3 + [2.6] * 4 + [2.2] * 3 + [7] * 7 + [4], "keep_x": [2], "rows": [1] * NT3 * H, "hold": [1]}
STEPS.update({s + "1": STEPS[s + "0"] for s in ("forward", "mix", "inverse")})
BACK_IN = 3
U1 = 11


def when(section, mark):
    return float(np.interp(mark, range(len(STEPS[section]) + 1), np.cumsum([0] + STEPS[section])))


def weave(engine, chains, begun):
    ends = [sum(when(s, b) - when(s, a) for s, a, b in chain) for chain in chains]
    at = [0.0] * len(chains)
    left = [list(chain) for chain in chains]
    while any(left):
        first = None
        for n, chain in enumerate(left):
            while chain:
                section, a, b = chain[0]
                if section not in begun:
                    steps = engine.get(section)
                    steps = steps() if steps else iter(())
                    begun[section] = [next(steps, None), steps]
                mark = begun[section][0]
                if mark is not None and mark < b:
                    time = (at[n] + when(section, mark) - when(section, a)) / ends[n]
                    if first is None or time < first[0]: first = (time, section)
                    break
                at[n] += when(section, b) - when(section, a)
                chain.pop(0)
        if first:
            begun[first[1]][0] = next(begun[first[1]][1], None)


def whole(*sections):
    return [(s, 0, len(STEPS[s])) for s in sections]


LAYER_0, LAYER_1 = (tuple(s + str(n) for s in ("forward", "mix", "inverse")) for n in range(2))


def a_round(begin=(), layers=True, end=(), front=True, rows=True, back=True):
    tokenizer = [[*begin, *LAYER_0], ["forward1", "mix1", "inverse1", *end]] if layers else [[], []]
    turned = [("back", 0, BACK_IN)] if back else []
    return ([] if front else [[turned]]) + [
            [turned + whole("rnn", "moe", "att", "pk") if front else [], whole(*tokenizer[0]), whole("hold") + [("rows", 0, U1)] if rows else []],
            [whole("top") if front else [], [("back", BACK_IN, len(STEPS["back"]))] if back else [], whole(*tokenizer[1]),
             [("rows", U1, NT3 * H)] if rows else []],
            [whole("keep_x")]]


HALF = POS // 2


def early_fusion(nc, xT, fc0, sw, cwb, fc1, fc2, f1, f2, g3, g4, txt, wrnn, brnn, gw, w1, w2, b2, wq, wk, wv, wot, wpk, keysT, wq5, wo5,
                 table, ident_in, tri_in, iota_in, eight_in, hbase_in, later_in, out):
    tok = nc.dram_tensor("tokens", (B, POS), F32, kind="Internal").ap()
    ctx = ExitStack()
    with ctx:
        sb = lambda n, s, d=F32: ctx.enter_context(nc.sbuf_tensor(n, s, d))
        sem = lambda n: ctx.enter_context(nc.semaphore(n))
        TP = [ctx.enter_context(nc.psum_tensor(f"TP{i}", [128, 512], F32)) for i in range(2)]
        MM = [ctx.enter_context(nc.psum_tensor(f"MM{i}", [128, 512], F32)) for i in range(2)]
        PB = [ctx.enter_context(nc.psum_tensor(f"PB{i}", [128, 512], F32)) for i in range(4)]

        IMG = sb("IMG", [128, GB, POS])
        U = sb("U", [128, SIDE * 2 * MODES])
        COORDS = U[0:Q4 * 3, 0:HALF]
        ROW = U[0:Q4, 0:HALF]
        TURN = sb("TURN", [128, 2, 512])
        FHID = sb("FHID", [128, 2, 512])
        SPEC = sb("SPEC", [128, Q4, KWQ])
        SW = sb("SW", [128, 2, MODES, WID])
        CONV = sb("CONV", [128, 129])
        F1, F2, G3, G4 = (sb(n, s) for n, s in (("F1", [128, 80]), ("F2", [128, 40]), ("G3", [40, 128]), ("G4", [80, 128])))
        FW0 = sb("FW0", [Q4 * 3, 128]); FB0 = sb("FB0", [128, 1])
        FW1 = sb("FW1", [128, 2, 128]); FB1 = sb("FB1", [128, 1])
        FW2 = sb("FW2", [128, 2, 4]); FB2 = sb("FB2", [4, 1])

        WRNN = sb("WRNN", [128, D]); BRNN = sb("BRNN", [128, 2]); BSUM = sb("BSUM", [128, 1])
        GW = sb("GW", [65, E]); W1 = sb("W1E", [65, E * FF]); W2 = sb("W2E", [128, 2 * E * D]); B2 = sb("B2E", [1, E * D])
        WQ = sb("WQ", [64, H * D]); WK = sb("WK", [64, D]); WV = sb("WV", [64, D]); WOT = sb("WOT", [128, 4, D])
        WPK = sb("WPK", [64, 512]); KB = sb("KB", [128, 4, 256]); W5 = sb("W5", [128, 512]); WQ5 = W5[0:64, :]; WO5 = W5[:, :].rearrange("p (h d) -> p h d", h=H)
        ID = sb("IDB", [128, 128]); TRI = sb("TRI", [128, 128]); ONES = sb("ONES", [128, 128])
        IOTA = sb("IOTA", [128, NC50]); EIGHT = sb("EIGHT", [128, E]); HBASE = sb("HBASE", [128, H])
        LATER = sb("LATER", [128, D], I32); NEG = sb("NEG", [128, 1]); BIG = sb("BIG", [128, 2])
        AREA1 = sb("AREA1", [128, 24 * SEQ]); AREA2 = sb("AREA2", [128, H * TOK]); AREA3 = sb("AREA3", [128, 4 * TOK]); AREA4 = sb("AREA4", [128, 3 * 512])
        SEARCH = sb("SEARCH", [128, 1600])
        X = sb("XH", [128, NT3, D]); N = sb("N", [128, NT3, D]); TMP = sb("TMP", [128, NT3, D])
        ST = sb("ST", [128, 6, NT3]); RS = sb("RS", [128, 2, SEQ]); NTR = sb("NTR", [65, TOK]); NT4 = sb("NT4", [64, TOK])
        LG = sb("LG", [128, NT3, E]); LE = sb("LE", [128, NT3, E]); OH = sb("OH", [128, NT3, E]); OHS = sb("OHS", [128, E])
        G1 = sb("G1", [128, 8, NT3]); HID = AREA3[:, 0:4 * TOK].rearrange("p (s n) -> p s n", s=4); Y = sb("Y", [128, NT3, D]); YM = sb("YM", [128, NT3, D])
        QT = AREA2[0:64, :].rearrange("p (h n) -> p h n", h=H); KT = sb("KT", [64, TOK]); VC = sb("VC", [64, TOK])
        P = AREA1[:, 0:24 * SEQ].rearrange("p (r t) -> p r t", t=SEQ); NM = sb("NM", [128, 24]); DEN = sb("DEN", [128, 24]); WON = AREA3[:, 0:12 * D].rearrange("p (r d) -> p r d", d=D); Z = AREA3[0:64, 12 * D:12 * D + 3 * SEQ].rearrange("p (c t) -> p c t", c=3)
        QPK = AREA2[:, 0:4 * TOK].rearrange("p (r t) -> p r t", t=TOK); SIM = AREA1[:, 0:3072].rearrange("p (t a k) -> p t a k", t=NT3, a=2)
        SIMR = SEARCH[:, 0:1024].rearrange("p (a k) -> p a k", a=2); V16 = sb("V16", [128, 2, H, TOPK]); I16 = sb("I16", [128, 2, H, TOPK], U32); IF = sb("IF", [128, 2, H, TOPK])
        C50, CI, CR = (SEARCH[:, 400 * n:400 * n + 400].rearrange("p (h c) -> p h c", h=H) for n in range(3))
        FV = sb("FV", [128, H, TOPK]); FP = sb("FP", [128, H, TOPK], U32); PF = sb("PF", [128, H, TOPK]); EQ = SEARCH[:, 800:1600]
        FS = sb("FS", [128, H, TOPK]); S8 = sb("S8", [128, 2, H])
        IDX = sb("IDX", [128, NT3, H, TOPK], I32); WT = sb("WT", [128, NT3, H, TOPK]); XK = sb("XK", [128, NT3, D]); NT2 = sb("NT2", [128, TOK]); NTK = NT2[64:128, :]
        XC = sb("XC", [128, NT3, D]); NTC = NT2[0:64, :]
        GATH = sb("GATH", [128, RING, TOPK, 2 * D]); KV = sb("KV", [128, NT3, H, 2 * D])
        Q5 = QT; KVT = sb("KVT", [128, H, TOK]); VW = AREA3[:, :].rearrange("p (t h d) -> p t h d", t=NT3, h=H)
        P5 = AREA1[:, 3072:4608].rearrange("p (s h t) -> p s h t", s=2, h=4); NM5 = sb("NM5", [128, 2, 4]); DEN5 = sb("DEN5", [128, 2, 4]); PT = AREA4[:, :].rearrange("p (s n) -> p s n", s=3)
        OUTB = sb("OUTB", [128, NT3, D])

        full = {(k, b): sem(f"{k}_full{b}") for k in PLANS for b in range(4)}
        empt = {(k, b): sem(f"{k}_out{b}") for k in PLANS for b in range(4)}
        PER = {"x_in": 80, "normed": 4, "shifted": 1, "exped": 1, "one_hot": 1, "h_kept": 1, "maxed": 24, "masked": 12,
               "rden": 2, "shift_top": NT3, "exp_top": NT3, "kept_idx": NT3, "kept_x": 1,
               "gather_free": NT3 * H, "weighted": 1, "maxed5": 12, "scaled5": 6, "out_sb": 1, "stored": 16, "multiplied": NT3 * H}
        S = {n: sem(n) for n in PER}
        gath = [sem(f"gathered{r}") for r in range(RING)]
        tokenizer_in, const_in, zeroed = sem("tokenizer_weights_in"), sem("mixer_weights_in"), sem("buffers_zeroed")
        coords_in = sem("coords_in"); sw_in = [sem("sw_in0"), sem("sw_in1")]; conv_in = sem("conv_in")
        tp_full = sem("turned"); tp_out = sem("turned_out"); mm_full = sem("multiplied_full"); mm_out = sem("multiplied_out")
        row_out = sem("tokens_stored")
        passed = {x: sem(f"{x}_passed") for x in ("PE", "DVE", "Pool")}
        block = ctx.enter_context(nc.Block())

        def fence(e):
            e.sem_inc(passed[str(e.engine).split(".")[-1]], 1)


        def event(name, it, k):
            return S[name], (it + 1) * PER[name] + k

        def filled(kind, it, name, k=0):
            b, n = number(PLANS[kind], name, k)
            return full[kind, b], (it + 1) * total(PLANS[kind], b) + n + 1

        def emptied(kind, it, name, k=0):
            b, n = number(PLANS[kind], name, k)
            return empt[kind, b], (it + 1) * total(PLANS[kind], b) + n + 1

        def free(kind, it, name, k=0):
            b, n = number(PLANS[kind], name, k)
            return empt[kind, b], (it + 1) * total(PLANS[kind], b) + n

        def bank(kind, name):
            return number(PLANS[kind], name, 0)[0]

        def credits(e, names, banks=()):
            for n in names: e.sem_inc(S[n], PER[n])
            for k, b in banks:
                e.sem_inc(full[k, b], total(PLANS[k], b)); e.sem_inc(empt[k, b], total(PLANS[k], b))
        tokv = tok.rearrange("b (h w) -> (b h) w", w=D)

        def mm_group(g): return M_GROUP * g
        def mm_layer(g, l): return M_GROUP * g + M_IN + M_LAYER * l
        def tp_layer(g, l): return T_GROUP * g + T_LAYER * l
        def mm_last(g): return M_GROUP * g + M_IN + LAYERS * M_LAYER
        def tp_last(g): return T_GROUP * g + LAYERS * T_LAYER

        def sp_coords(e, g):
            for n in range(2 * GB):
                yield ROWQ // 2 * n
                if n: e.wait_ge(mm_full, CREDIT + mm_group(g) + ROWQ // 2 * n)
                else: e.wait_ge(row_out, 16 * 2 * GB * g + 16)
                e.dma_start(COORDS, xT[bass.ds((g * GB + n // 2) * (Q4 * 3), Q4 * 3), HALF * (n % 2):HALF * (n % 2) + HALF]).then_inc(coords_in, 16)

        def sp_chunk(e, l, c):
            e.dma_start(SW[:, c % 2, :, :].rearrange("p m o -> p (m o)"), sw[bass.ds((l * CHUNKS + c) * 128, 128), :]).then_inc(sw_in[c % 2], 16)

        def sp_forward(e, g, l):
            yield 0
            e.wait_ge(mm_full, CREDIT + mm_layer(g, l))
            sp_chunk(e, l, 0)
            sp_chunk(e, l, 1)
            e.wait_ge(mm_out, CREDIT + mm_layer(g, l))
            for a in range(Q4):
                r = slice(32 * a, 32 * a + 32)
                e.dma_start(CONV[r, r], cwb[bass.ds(l * WID, WID), 0:WID]).then_inc(conv_in, 16)
                e.dma_start(CONV[r, 128:129], cwb[bass.ds(l * WID, WID), WID:WID + 1], allow_slow_non_contiguous=True).then_inc(conv_in, 16)

        def sp_mix(e, g, l):
            for c in range(2, CHUNKS):
                yield c - 0.8
                e.wait_ge(mm_full, CREDIT + mm_layer(g, l) + GB * F_T + c - 1)
                sp_chunk(e, l, c)

        def sp_tokens(e, g):
            for n in range(2 * GB):
                yield ROWQ // 2 * (n + 1) - 0.05
                e.wait_ge(tp_out, CREDIT + tp_last(g) + ROWQ // 2 * (n + 1))
                e.dma_start(tok[bass.ds((g * GB + n // 2) * Q4, Q4), HALF * (n % 2):HALF * (n % 2) + HALF], ROW).then_inc(row_out, 16)

        def t_coords(e, g):
            for n in range(GB * ROWQ):
                yield n
                if n % (ROWQ // 2) == 0:
                    e.wait_ge(coords_in, g * (2 * GB * 16) + 16 * (n // (ROWQ // 2)) + 16)
                c = n % (ROWQ // 2)
                p = mm_slot(e, mm_group(g), n)
                fence(e)
                e.matmul(p[:, :], FW0[:, :], COORDS[:, 512 * c:512 * c + 512], start=True, stop=True).then_inc(mm_full, 1)

        def mm_slot(e, base, n):
            e.wait_ge(mm_out, CREDIT + base + n - 1)
            return MM[n % 2]
        def tp_slot(e, base, n):
            e.wait_ge(tp_out, CREDIT + base + n - 1)
            return TP[n % 2]
        def t_forward(e, g, l, q):
            tb, mb = tp_layer(g, l) + q * F_T, mm_layer(g, l) + q * F_T
            def turn(c):
                t = tp_slot(e, tb, c)
                for j in range(4):
                    m = e.transpose(t[:, 128 * j:128 * j + 128], IMG[:, q, 512 * c + 128 * j:512 * c + 128 * j + 128], ID[:, :])
                m.then_inc(tp_full, 1)
            def along_w(c):
                e.wait_ge(tp_out, CREDIT + tb + c + 1)
                p = mm_slot(e, mb, c)
                for j in range(4):
                    m = e.matmul(p[:, 80 * j:80 * j + 80], TURN[:, c % 2, 128 * j:128 * j + 128], F1[:, :], start=True, stop=True)
                m.then_inc(mm_full, 1)
            yield 0
            if q == 0:
                e.wait_ge(mm_out, CREDIT + mb)
            turn(0)
            for c in range(ROWQ):
                yield c
                if c + 1 < ROWQ: turn(c + 1)
                yield c + 0.5
                along_w(c)
            yield ROWQ
            e.wait_ge(mm_out, CREDIT + mb + ROWQ)
            Uv = U[:, :].rearrange("p (k m) -> p k m", k=MODES)
            def turn2(i):
                t = tp_slot(e, tb, ROWQ + i)
                for a in range(Q4):
                    m = e.transpose(t[:, 128 * a:128 * a + 128], Uv[:, CHUNKS * a + i, :], ID[:, :])
                m.then_inc(tp_full, 1)
            def along_h(i):
                e.wait_ge(tp_out, CREDIT + tb + ROWQ + i + 1)
                p = mm_slot(e, mb, ROWQ + i)
                for b in range(Q4):
                    m = e.matmul(p[:, 40 * b:40 * b + 40], TURN[:, (ROWQ + i) % 2, 128 * b:128 * b + 128], F2[:, :], start=True, stop=True)
                m.then_inc(mm_full, 1)
            turn2(0)
            for i in range(CHUNKS):
                yield ROWQ + i
                if i + 1 < CHUNKS: turn2(i + 1)
                yield ROWQ + i + 0.5
                along_h(i)
        def t_mix(e, g, l):
            mb = mm_layer(g, l) + GB * F_T
            yield 0
            e.wait_ge(mm_out, CREDIT + mb)
            Sv = SPEC[:, :, :].rearrange("p q (m r) -> p q m r", r=2)
            for c in range(CHUNKS):
                yield c
                per_layer = (CHUNKS + 1 - c % 2) // 2
                e.wait_ge(sw_in[c % 2], 16 * (per_layer * (g * LAYERS + l) + c // 2 + 1))
                p = mm_slot(e, mb, c)
                fence(e)
                pv = p[:, 0:Q4 * GB * MODES * 2].rearrange("p (q m r) -> p q m r", q=Q4 * GB, r=2)
                for k in range(MODES):
                    for a in range(Q4):
                        r = slice(32 * a, 32 * a + 32)
                        m = e.matmul(pv[r, :, k, :], SW[r, c % 2, k, :], Sv[r, :, c * MODES + k, :], start=True, stop=True)
                m.then_inc(mm_full, 1)
        def t_inverse(e, g, l, q):
            tb = tp_layer(g, l) + GB * F_T + q * I_T
            mb = mm_layer(g, l) + GB * F_T + CHUNKS + q * I_T
            def turn3(i):
                t = tp_slot(e, tb, i)
                fence(e)
                for b in range(Q4):
                    m = e.transpose(t[0:40, 128 * b:128 * b + 128], SPEC[:, b, 40 * i:40 * i + 40], ID[:, :])
                m.then_inc(tp_full, 1)
            def back_h(i):
                e.wait_ge(tp_out, CREDIT + tb + i + 1)
                p = mm_slot(e, mb, i)
                for a in range(Q4):
                    m = e.matmul(p[:, 128 * a:128 * a + 128], TURN[0:40, i % 2, 128 * a:128 * a + 128], G3[:, :], start=True, stop=True)
                m.then_inc(mm_full, 1)
            yield 0
            e.wait_ge(mm_out, CREDIT + mb)
            turn3(0)
            for i in range(CHUNKS):
                yield i
                if i + 1 < CHUNKS: turn3(i + 1)
                yield i + 0.5
                back_h(i)
            yield CHUNKS
            e.wait_ge(mm_out, CREDIT + mb + CHUNKS)
            if q == 0:
                e.wait_ge(conv_in, (g * LAYERS + l) * 128 + 128)
            def turn4(c):
                t = tp_slot(e, tb, CHUNKS + c)
                for j in range(4):
                    m = e.transpose(t[0:80, 128 * j:128 * j + 128], U[:, 80 * (4 * c + j):80 * (4 * c + j) + 80], ID[:, :])
                m.then_inc(tp_full, 1)
            def back_w(c):
                p = mm_slot(e, mb, CHUNKS + c)
                e.matmul(p[:, :], CONV[:, 0:128], IMG[:, q, 512 * c:512 * c + 512], start=True, stop=False, skip_group_check=True)
                e.wait_ge(tp_out, CREDIT + tb + CHUNKS + c + 1)
                for j in range(4):
                    m = e.matmul(p[:, 128 * j:128 * j + 128], TURN[0:80, (CHUNKS + c) % 2, 128 * j:128 * j + 128], G4[:, :], start=False, stop=True, skip_group_check=True)
                m.then_inc(mm_full, 1)
            turn4(0)
            for c in range(ROWQ):
                yield CHUNKS + c
                if c + 1 < ROWQ: turn4(c + 1)
                yield CHUNKS + c + 0.5
                back_w(c)
        def t_tokens(e, g):
            mb, tb = mm_last(g), tp_last(g)
            yield 0
            e.wait_ge(mm_out, CREDIT + mb)
            for n in range(GB * ROWQ):
                yield n
                q, c = n // ROWQ, n % ROWQ
                for pr in range(2):
                    p = mm_slot(e, mb, 2 * n + pr)
                    e.matmul(p[:, :], FW1[:, pr, :], IMG[:, q, 512 * c:512 * c + 512], start=True, stop=True).then_inc(mm_full, 1)
                t = tp_slot(e, tb, n)
                yield n + 0.7
                for pr in range(2):
                    e.wait_ge(mm_out, CREDIT + mb + 2 * n + pr + 1)
                    fence(e)
                    m = e.matmul(t[0:4, :], FW2[:, pr, :], FHID[:, pr, :], start=(pr == 0), stop=(pr == 1))
                m.then_inc(tp_full, 1)

        def evac(e, base, n, dst, src, func=ACT.Copy, **kw):
            e.wait_ge(mm_full, CREDIT + base + n + 1)
            e.activation(dst, MM[n % 2][src] if not callable(src) else src(MM[n % 2]), func, **kw).then_inc(mm_out, 1)
        def a_forward(e, g, l, q):
            mb = mm_layer(g, l) + q * F_T
            Uf = U[:, :].rearrange("p (k h r) -> p h k r", k=MODES, r=2)
            for c in range(ROWQ):
                yield c + 0.9
                evac(e, mb, c, Uf[:, 8 * c:8 * c + 8, :, :], lambda m: m[:, 0:320].rearrange("p (h k r) -> p h k r", k=MODES, r=2))
            for i in range(CHUNKS):
                yield ROWQ + i + 0.9
                evac(e, mb, ROWQ + i, SPEC[:, :, 40 * i:40 * i + 40], lambda m: m[:, 0:40 * Q4].rearrange("p (b m) -> p b m", b=Q4))
        def a_mix(e, g, l):
            mb = mm_layer(g, l) + GB * F_T
            for c in range(CHUNKS):
                yield c + 0.9
                evac(e, mb, c, SPEC[:, :, 2 * MODES * c:2 * MODES * (c + 1)],
                     lambda m: m[:, 0:Q4 * GB * MODES * 2].rearrange("p (q m) -> p q m", q=Q4 * GB))
        def a_inverse(e, g, l, q):
            mb = mm_layer(g, l) + GB * F_T + CHUNKS + q * I_T
            Uv = U[:, :].rearrange("p (h a k r) -> p k a h r", a=Q4, k=CHUNKS, r=2)
            for i in range(CHUNKS):
                yield i + 0.9
                evac(e, mb, i, Uv[:, i, :, :, :], lambda m: m[:, :].rearrange("p (a h r) -> p a h r", a=Q4, r=2))
            for c in range(ROWQ):
                yield CHUNKS + c + 0.9
                evac(e, mb, CHUNKS + c, IMG[:, q, 512 * c:512 * c + 512], (slice(None), slice(None)), ACT.Gelu, bias=CONV[:, 128:129])
        def a_coords(e, g):
            for n in range(GB * ROWQ):
                yield n + 0.5
                evac(e, mm_group(g), n, IMG[:, n // ROWQ, 512 * (n % ROWQ):512 * (n % ROWQ) + 512], (slice(None), slice(None)), ACT.Identity, bias=FB0[:, :])

        def a_tokens(e, g):
            for n in range(GB * ROWQ):
                yield n + 0.4
                for pr in range(2):
                    e.wait_ge(tp_full, CREDIT + tp_last(g) + n)
                    evac(e, mm_last(g), 2 * n + pr, FHID[:, pr, :], (slice(None), slice(None)), ACT.Gelu, bias=FB1[:, :])

        def copy(e, base, n, dst, rows, cols):
            e.wait_ge(tp_full, CREDIT + base + n + 1)
            e.tensor_copy(dst, TP[n % 2][0:rows, 0:cols]).then_inc(tp_out, 1)
        def swapped(e, base, n, slot, rows):
            e.wait_ge(tp_full, CREDIT + base + n + 1)
            e.tensor_copy(TURN[0:rows, slot, :].rearrange("p (x y c) -> p y x c", x=Q4, y=Q4),
                          TP[n % 2][0:rows, :].rearrange("p (y x c) -> p y x c", x=Q4, y=Q4)).then_inc(tp_out, 1)
        def v_forward(e, g, l, q):
            tb, mb = tp_layer(g, l) + q * F_T, mm_layer(g, l) + q * F_T
            for c in range(ROWQ):
                yield c - 0.3 if c else 0.1
                e.wait_ge(mm_full, CREDIT + mb + c - 1)
                copy(e, tb, c, TURN[:, c % 2, :], 128, 512)
            for i in range(CHUNKS):
                yield ROWQ + i - 0.3 if i else ROWQ + 0.1
                e.wait_ge(mm_full, CREDIT + mb + ROWQ + i - 1)
                swapped(e, tb, ROWQ + i, i % 2, 128)
        def v_inverse(e, g, l, q):
            tb = tp_layer(g, l) + GB * F_T + q * I_T
            mb = mm_layer(g, l) + GB * F_T + CHUNKS + q * I_T
            for i in range(CHUNKS):
                yield i - 0.3 if i else 0.1
                e.wait_ge(mm_full, CREDIT + mb + i - 1)
                swapped(e, tb, i, i % 2, 40)
            for c in range(ROWQ):
                yield CHUNKS + c - 0.3 if c else CHUNKS + 0.1
                e.wait_ge(mm_full, CREDIT + mb + CHUNKS + c - 1)
                copy(e, tb, CHUNKS + c, TURN[0:80, (CHUNKS + c) % 2, :], 80, 512)
        def v_tokens(e, g):
            for n in range(GB * ROWQ):
                yield n + 0.9
                e.wait_ge(tp_full, CREDIT + tp_last(g) + n + 1)
                if n % (ROWQ // 2) == 0:
                    e.wait_ge(row_out, 16 * (2 * GB * g + n // (ROWQ // 2)) + 16)
                c = n % (ROWQ // 2)
                e.tensor_scalar(ROW[:, 512 * c:512 * c + 512], TP[n % 2][0:4, :], FB2[:, :], None, ALU.add).then_inc(tp_out, 1)

        def sp_setup(e):
            credits(e, ["x_in", "stored"])
            e.sem_inc(row_out, 16)
            e.wait_ge(zeroed, 9)
            def load(d, s, **k):
                e.dma_start(d, s, **k).then_inc(tokenizer_in, 16)
            for a in range(Q4):
                load(FW0[3 * a:3 * a + 3, 32 * a:32 * a + 32], fc0[0:3, :])
                load(FB0[32 * a:32 * a + 32, :], fc0[3, :].rearrange("(a b) -> a b", b=1))
                load(FW1[32 * a:32 * a + 32, a // 2, 64 * (a % 2):64 * (a % 2) + 64], fc1[0:WID, :])
                load(FW2[64 * (a % 2):64 * (a % 2) + 64, a // 2, a:a + 1], fc2[0:64, :])
                load(FB2[a:a + 1, :], fc2[64:65, :])
            for a in range(2):
                load(FB1[64 * a:64 * a + 64, :], fc1[WID, :].rearrange("(a b) -> a b", b=1))
            for d, s in ((F1, f1), (F2, f2), (G3, g3), (G4, g4), (ID, ident_in)):
                load(d[:, :], s)
        N_TOKENIZER = 5 * Q4 + 2 + 5

        def sp_mixers(e):
            n = [0]
            def load(d, s, **k):
                e.dma_start(d, s, **k).then_inc(const_in, 16); n[0] += 1
            load(WRNN[:, :], wrnn)
            for i in range(2): load(BRNN[64:128, i:i + 1], brnn[i, :].rearrange("(a b) -> a b", b=1))
            for d, s in ((GW, gw), (W1, w1), (W2, w2), (B2, b2), (WQ, wq), (WK, wk), (WV, wv), (WPK, wpk), (WQ5, wq5),
                         (TRI, tri_in), (IOTA, iota_in), (EIGHT, eight_in), (HBASE, hbase_in), (LATER, later_in)):
                load(d[:, :], s)
            load(WOT[:, :, :].rearrange("p a b -> p (a b)"), wot)
            load(WO5[64:128, :, :].rearrange("p a b -> p (a b)"), wo5)
            for p in range(2):
                for h in range(H):
                    load(KB[32 * (h % 4):32 * (h % 4) + 32, 2 * p + h // 4, 64 * (h % 4):64 * (h % 4) + 64], keysT[(p * H + h) * 32:(p * H + h) * 32 + 32, :])
            assert n[0] == NLOADS, n[0]
        NLOADS = 1 + 2 + 14 + 2 + 16

        def sp_front(e, j, g):
            yield 0
            e.wait_ge(*event("kept_x", j - 1, 1))
            e.wait_ge(row_out, 16 * 2 * GB * g + 16)
            for d, s in ((X[0:64, 0, :], tokv[bass.ds(j * 128, 64), :]), (X[64:128, 0, :], txt[bass.ds(j * 256, 64), :]),
                         (X[0:64, 1, :], txt[bass.ds(j * 256 + 64, 64), :]), (X[64:128, 1, :], tokv[bass.ds(j * 128 + 64, 64), :]),
                         (X[:, 2, :], txt[bass.ds(j * 256 + 128, 128), :])):
                e.dma_start(d, s).then_inc(S["x_in"], 16)

        def sp_back(e, i):
            yield 17.2
            e.wait_ge(*event("out_sb", i, 1))
            e.dma_start(out[bass.ds(i * TOK, TOK), :].rearrange("(t p) d -> p t d", p=128), OUTB[:, :, :]).then_inc(S["stored"], 16)

        def pool_gather(e, i):
            for u in range(NT3 * H):
                r = u % RING
                if u % H == 0: e.wait_ge(*event("kept_idx", i, u // H + 1))
                e.wait_ge(*event("gather_free", i, u + 1 - RING))
                fence(e)
                for k in range(TOPK):
                    e.indirect_dma_start(GATH[:, r, k, :], None, table, bass.IndirectOffsetOnAxis(IDX[:, u // H, u % H, k:k + 1], 0)).then_inc(gath[r], 16)

        def bc(ap, n):
            return ap.rearrange("p (t o) -> p t o", o=1).to_broadcast([ap.shape[0], ap.shape[1], n])

        def normalize(e):
            total, var, y, a, half, c = (ST[:, i, :] for i in range(6))
            yield 0
            e.drain()
            e.tensor_reduce(total, X[:, :, :], AX.X, ALU.add); e.drain()
            e.scalar_tensor_tensor(N[:, :, :], bc(total, D), -1.0 / D, X[:, :, :], ALU.mult, ALU.add); e.drain()
            yield 1
            e.tensor_tensor(TMP[:, :, :], N[:, :, :], N[:, :, :], ALU.mult); e.drain()
            e.tensor_reduce(var, TMP[:, :, :], AX.X, ALU.add); e.drain()
            e.tensor_scalar(var, var, 1.0 / D, EPS, ALU.mult, ALU.add); e.drain()
            yield 2
            e.tensor_scalar(a.bitcast(I32), var.bitcast(I32), 1, None, ALU.logical_shift_right)
            e.tensor_scalar(half, var, -0.5, None, ALU.mult); e.drain()
            e.tensor_scalar(y.bitcast(I32), a.bitcast(I32), -1.0, float(0x5F3759DF), ALU.mult, ALU.add); e.drain()
            for k in range(4):
                if k == 1: yield 3
                e.tensor_tensor(c, y, y, ALU.mult); e.drain()
                e.tensor_tensor(c, c, half, ALU.mult); e.drain()
                e.scalar_tensor_tensor(y, c, 1.5, y, ALU.add, ALU.mult); e.drain()
            e.tensor_tensor(N[:, :, :], N[:, :, :], bc(y, D), ALU.mult).then_inc(S["normed"], 1)

        def v_rnn(e, j):
            yield 0
            e.wait_ge(*event("x_in", j, 80))
            fence(e)
            yield from normalize(e)
            yield 7.6
            e.wait_ge(*filled("front", j, "rnn_back"))
            e.tensor_tensor(X[:, :, :], X[:, :, :], PB[2][:, 0:192].rearrange("p (t d) -> p t d", d=D), ALU.add).then_inc(empt["front", 2], 1)

        def v_moe(e, j):
            yield from normalize(e)
            yield 4.7
            e.wait_ge(*filled("front", j, "gate"))
            m, sm, r, pm, w, pos, keep, sc = (G1[:, i, :] for i in range(8))
            L = PB[1][:, 0:24].rearrange("p (t e) -> p t e", e=E)
            e.tensor_reduce(m, L, AX.X, ALU.max); e.drain()
            e.tensor_tensor(LG[:, :, :], L, bc(m, E), ALU.subtract).then_inc(empt["front", 1], 1)
            e.wait_ge(*emptied("front", j, "gate"))
            fence(e)
            e.drain().then_inc(S["shifted"], 1)
            e.memset(Y[:, :, :], 0.0)
            yield 5.4
            e.wait_ge(*event("exped", j, 1))
            e.tensor_reduce(sm, LE[:, :, :], AX.X, ALU.add); e.drain()
            e.reciprocal(r, sm); e.drain()
            e.tensor_tensor(LE[:, :, :], LE[:, :, :], bc(r, E), ALU.mult); e.drain()
            e.tensor_reduce(pm, LE[:, :, :], AX.X, ALU.max); e.drain()
            e.tensor_tensor(LG[:, :, :], LE[:, :, :], bc(pm, E), ALU.is_equal); e.drain()
            e.tensor_tensor(LG[:, :, :], LG[:, :, :], EIGHT[:, :].rearrange("p (o e) -> p o e", o=1).to_broadcast([128, NT3, E]), ALU.mult); e.drain()
            e.tensor_reduce(w, LG[:, :, :], AX.X, ALU.max); e.drain()
            e.tensor_tensor(OH[:, :, :], LG[:, :, :], bc(w, E), ALU.is_equal).then_inc(S["one_hot"], 1)
            yield 6.5
            e.wait_ge(*filled("front", j, "place"))
            e.tensor_tensor(LG[:, :, :], PB[1][:, 0:24].rearrange("p (t e) -> p t e", e=E), OH[:, :, :], ALU.mult).then_inc(empt["front", 1], 1)
            for t in range(NT3):
                e.drain()
                e.tensor_tensor(OHS[:, :], OHS[:, :], OH[:, t, :], ALU.add)
            e.drain()
            e.tensor_reduce(pos, LG[:, :, :], AX.X, ALU.add); e.drain()
            e.tensor_scalar(keep, pos, float(CAP), None, ALU.is_le); e.drain()
            e.tensor_tensor(sc, keep, pm, ALU.mult)
            for x in range(E):
                yield 7.7 + x
                name = ("expert", "expertB")[x % 2]
                e.wait_ge(*filled("front", j, name, x // 2))
                fence(e)
                e.drain()
                b = bank("front", name)
                e.copy_predicated(Y[:, :, :], OH[:, :, x:x + 1].to_broadcast([128, NT3, D]).bitcast(I32),
                                  PB[b][:, 0:192].rearrange("p (t d) -> p t d", d=D)).then_inc(empt["front", b], 1)
            yield 7 + E
            e.drain()
            e.tensor_tensor(Y[:, :, :], Y[:, :, :], bc(sc, D), ALU.mult); e.drain()
            e.tensor_tensor(YM[:, :, :], Y[:, :, :], Y[:, :, :], ALU.is_equal)
            e.memset(TMP[:, :, :], 0.0); e.drain()
            e.copy_predicated(TMP[:, :, :], YM[:, :, :].bitcast(I32), Y[:, :, :]); e.drain()
            e.tensor_scalar(YM[:, :, :], TMP[:, :, :], FMAX, None, ALU.is_gt); e.drain()
            e.copy_predicated(TMP[:, :, :], YM[:, :, :].bitcast(I32), BIG[:, 0:1].rearrange("p (a b) -> p a b", b=1).to_broadcast([128, NT3, D])); e.drain()
            e.tensor_scalar(YM[:, :, :], TMP[:, :, :], -FMAX, None, ALU.is_lt); e.drain()
            e.copy_predicated(TMP[:, :, :], YM[:, :, :].bitcast(I32), BIG[:, 1:2].rearrange("p (a b) -> p a b", b=1).to_broadcast([128, NT3, D])); e.drain()
            e.tensor_tensor(X[:, :, :], X[:, :, :], TMP[:, :, :], ALU.add)

        def v_att(e, j):
            yield from normalize(e)
            for n in range(5):
                yield 5.5 + n
                e.wait_ge(*filled("front", j, "qkvB", n))
                dst = QT[:, 2 * n + 1, :] if n < 4 else VC[:, :]
                if n < 4:
                    ins = e.tensor_scalar(dst, PB[3][0:64, 0:TOK], float(1 / np.sqrt(np.float32(8))), None, ALU.mult)
                else:
                    ins = e.tensor_copy(dst, PB[3][0:64, 0:TOK])
                ins.then_inc(empt["front", 3], 1)
            def finish(b):
                e.wait_ge(*emptied("front", j, "scoreB", 3 * b + 2)); e.wait_ge(*emptied("front", j, "scoreA", 3 * b + 2))
                if b: e.wait_ge(*free("front", j, "z2", b)); e.wait_ge(*emptied("front", j, "z2", 0))
                e.reciprocal(DEN[:, 12 * b:12 * b + 12], DEN[:, 12 * b:12 * b + 12]); e.drain()
                e.tensor_tensor(WON[:, :, :].rearrange("p (a c) d -> p a c d", a=3),
                                WOT[:, :, :].rearrange("p (o c) d -> p o c d", o=1).to_broadcast([128, 3, 4, D]),
                                DEN[:, 12 * b:12 * b + 12].rearrange("p (a c o) -> p a c o", a=3, o=1).to_broadcast([128, 3, 4, D]),
                                ALU.mult).then_inc(S["rden"], 1)
            def z_out(b):
                e.wait_ge(*filled("front", j, "z", b))
                e.wait_ge(*filled("front", j, "z2", b))
                if b: e.wait_ge(*filled("front", j, "z2", b))
                e.tensor_copy(Z[:, 0:2, :].rearrange("p a b -> p (a b)"), PB[0][0:64, 0:384]).then_inc(empt["front", 0], 1)
                e.tensor_copy(Z[:, 2, :], PB[1][0:64, 0:192]).then_inc(empt["front", 1], 1)
            for n in range(12):
                yield 10.4 + n // 2
                name = ("scoreA", "scoreB")[n % 2]
                e.wait_ge(*filled("front", j, name, n // 2))
                e.tensor_reduce(NM[:, 2 * n:2 * n + 2], PB[bank("front", name)][:, 0:384].rearrange("p (a t) -> p a t", t=SEQ), AX.X, ALU.max, negate=True).then_inc(S["maxed"], 2)
                if n == 7: finish(0)
            yield 15.45
            z_out(0)
            yield 15.7
            finish(1)
            yield 16.6
            z_out(1)
            yield 17.5
            e.wait_ge(*filled("front", j, "att"))
            e.tensor_tensor(X[:, :, :], X[:, :, :], PB[2][:, 0:192].rearrange("p (t d) -> p t d", d=D), ALU.add).then_inc(empt["front", 2], 1)

        def v_pk(e, j):
            yield from normalize(e)
            for n in range(2):
                yield 5.5 + n
                e.wait_ge(*filled("front", j, "qpkB", n))
                e.tensor_copy(QPK[:, 2 * n + 1, :], PB[3][:, 0:TOK]).then_inc(empt["front", 3], 1)
            for t in range(NT3):
                yield 7.5 + t
                e.wait_ge(*filled("front", j, "simB", t))
                e.tensor_copy(SIM[:, t, 1, :], PB[3][:, :]).then_inc(empt["front", 3], 1)

        def v_top(e, j):
            for t in range(NT3):
                yield TOP_STEPS * t
                e.wait_ge(*emptied("front", j, "simA", t))
                fence(e)
                lists = [(p, h) for p in range(2) for h in range(H)]
                e.drain()
                for p, h in lists: e.max(V16[:, p, h, 0:8], SIM[:, t, p, 64 * h:64 * h + 64])
                e.drain()
                for p, h in lists:
                    if h == 0: yield TOP_STEPS * t + 1 + p
                    e.match_replace(SIMR[:, p, 64 * h:64 * h + 64], V16[:, p, h, 0:8], SIM[:, t, p, 64 * h:64 * h + 64], -FMAX)
                    e.max_index(I16[:, p, h, 0:8], V16[:, p, h, 0:8], SIM[:, t, p, 64 * h:64 * h + 64])
                yield TOP_STEPS * t + 3
                e.drain()
                for p, h in lists: e.max(V16[:, p, h, 8:16], SIMR[:, p, 64 * h:64 * h + 64])
                e.drain()
                for p, h in lists: e.max_index(I16[:, p, h, 8:16], V16[:, p, h, 8:16], SIMR[:, p, 64 * h:64 * h + 64])
                e.drain()
                yield TOP_STEPS * t + 4
                e.tensor_copy(IF[:, :, :, :].rearrange("p a h k -> p (a h k)"), I16[:, :, :, :].rearrange("p a h k -> p (a h k)")); e.drain()
                e.tensor_scalar(IF[:, 1, :, :], IF[:, 1, :, :], float(NK), None, ALU.mult); e.drain()
                e.tensor_tensor(IF[:, 1, :, :], IF[:, 1, :, :], HBASE[:, :].rearrange("p (h o) -> p h o", o=1).to_broadcast([128, H, TOPK]), ALU.add); e.drain()
                for src, dst in ((V16, C50), (IF, CI)):
                    at = 0
                    for i, n, j, m in CANDIDATES:
                        e.tensor_tensor(dst[:, :, at:at + n * m], src[:, 0, :, i:i + n].to_broadcast([128, H, m]) if n == 1 else src[:, 0, :, i:i + n],
                                        src[:, 1, :, j:j + m].to_broadcast([128, H, n]) if m == 1 and n > 1 else src[:, 1, :, j:j + m], ALU.add)
                        at += n * m
                yield TOP_STEPS * t + 5
                e.drain()
                for h in range(H): e.max(FV[:, h, 0:8], C50[:, h, :])
                e.drain()
                for h in range(H):
                    e.match_replace(CR[:, h, :], FV[:, h, 0:8], C50[:, h, :], -FMAX)
                    e.max_index(FP[:, h, 0:8], FV[:, h, 0:8], C50[:, h, :])
                e.drain()
                for h in range(H): e.max(FV[:, h, 8:16], CR[:, h, :])
                e.drain()
                for h in range(H): e.max_index(FP[:, h, 8:16], FV[:, h, 8:16], CR[:, h, :])
                e.tensor_tensor(FS[:, :, :], FV[:, :, :], FV[:, :, 0:1].to_broadcast([128, H, TOPK]), ALU.subtract); e.drain().then_inc(S["shift_top"], 1)
                yield TOP_STEPS * t + 5.5
                e.tensor_copy(PF[:, :, :], FP[:, :, :]); e.drain()
                for g, (h0, nh, k0, nc) in enumerate(LOOKUPS):
                    yield TOP_STEPS * t + 6 + g * 4 / len(LOOKUPS)
                    hit = EQ[:, 0:nh * 8 * nc].rearrange("p (h k c) -> p h k c", h=nh, k=8)
                    place = PF[:, h0:h0 + nh, k0:k0 + 8]
                    e.tensor_tensor(hit, IOTA[:, 0:nc].rearrange("p (a b c) -> p a b c", a=1, b=1).to_broadcast([128, nh, 8, nc]),
                                    place.rearrange("p h (k o) -> p h k o", o=1).to_broadcast([128, nh, 8, nc]), ALU.is_equal)
                    e.drain()
                    e.tensor_tensor(hit, hit, CI[:, h0:h0 + nh, 0:nc].rearrange("p h (o c) -> p h o c", o=1).to_broadcast([128, nh, 8, nc]), ALU.mult)
                    yield TOP_STEPS * t + 6 + (g + 0.6) * 4 / len(LOOKUPS)
                    e.drain()
                    e.tensor_reduce(place, hit, AX.X, ALU.add); e.drain()
                yield TOP_STEPS * t + 10
                e.tensor_copy(IDX[:, t, :, :], PF[:, :, :])
                e.wait_ge(*event("exp_top", j, t + 1))
                e.tensor_reduce(S8[:, 0, :], FS[:, :, :], AX.X, ALU.add); e.drain()
                e.reciprocal(S8[:, 1, :], S8[:, 0, :]); e.drain()
                e.tensor_tensor(WT[:, t, :, :], FS[:, :, :], S8[:, 1, :].rearrange("p (h o) -> p h o", o=1).to_broadcast([128, H, TOPK]), ALU.mult)
                e.drain().then_inc(S["kept_idx"], 1)

        def a_consume(e, i, u):
            yield u
            r = u % RING
            e.wait_ge(gath[r], (i * (NT3 * H // RING) + u // RING + 1) * 16 * TOPK)
            e.wait_ge(*event("kept_idx", i, u // H + 1))
            for k in range(TOPK):
                if k in (4, 8, 12): yield u + 0.03 * k
                m = e.activation(GATH[:, r, k, :], GATH[:, r, k, :], ACT.Copy, scale=WT[:, u // H, u % H, k:k + 1])
            m.then_inc(S["multiplied"], 1)

        def v_consume(e, i, u):
            yield u + 0.6
            e.wait_ge(*event("multiplied", i, u + 1))
            e.tensor_reduce(KV[:, u // H, u % H, :], GATH[:, u % RING, :, :].rearrange("p k d -> p d k"), AX.X, ALU.add).then_inc(S["gather_free"], 1)

        def v_keep_x(e, j, back, front):
            yield 0
            e.drain()
            if back:
                e.tensor_copy(XC[:, :, :], XK[:, :, :])
                e.tensor_copy(NTC[:, :], NTK[:, :])
                e.drain()
            if front:
                e.wait_ge(*emptied("front", j, "pkT"))
                e.tensor_copy(XK[:, :, :], X[:, :, :])
                e.tensor_copy(NTK[:, :], NT4[:, :])
                e.drain().then_inc(S["kept_x"], 1)

        def v_back(e, i):
            yield 0
            e.drain().then_inc(S["weighted"], 1)
            for n in range(3):
                yield n + 0.5
                e.wait_ge(*filled("back", i, "kvB", n))
                kvt_out(e, 2 * n + 1).then_inc(empt["back", 3], 1)
            e.wait_ge(*filled("back", i, "kvA", 2))
            for n in range(4):
                yield 3.5 + n
                e.wait_ge(*filled("back", i, "q5B", n))
                e.tensor_scalar(Q5[:, 2 * n + 1, :], PB[3][0:64, 0:TOK], D ** -0.5, None, ALU.mult).then_inc(empt["back", 3], 1)
            for n in range(12):
                yield 10.4 + n // 2
                b, ib, half = n // 6, n // 2 % 3, n % 2
                name = ("s5A", "s5B")[half]
                jn = 64 * (ib + 1)
                s = PB[bank("back", name)][:, 0:384].rearrange("p (a t) -> p a t", t=SEQ)
                e.wait_ge(*filled("back", i, name, n // 2))
                fence(e)
                e.copy_predicated(s[:, :, jn - 64:jn], LATER[:, :].rearrange("p (o c) -> p o c", o=1).to_broadcast([128, 2, D]),
                                  NEG[:, 0:1].rearrange("p (a b) -> p a b", b=1).to_broadcast([128, 2, D])); e.drain()
                sl = n // 2 % 2
                e.tensor_reduce(NM5[:, sl, 2 * half:2 * half + 2], s[:, :, 0:jn], AX.X, ALU.max, negate=True).then_inc(S["maxed5"], 1)
                if half == 0 and n > 0: v_scale5(e, i, n // 2 - 1)
                if half == 0 and n > 2: v_out5(e, i, n // 2 - 2)
            yield 16.3
            v_scale5(e, i, 5)
            v_out5(e, i, 4)
            yield 17
            v_out5(e, i, 5)
            e.drain().then_inc(S["out_sb"], 1)

        def v_out5(e, i, nb):
            e.wait_ge(*filled("back", i, "out", nb))
            if nb == 0: e.wait_ge(*event("stored", i - 1, 16))
            p, t = slice(64 * (nb % 2), 64 * (nb % 2) + 64), nb // 2
            e.tensor_tensor(OUTB[p, t, :], XC[p, t, :], PB[1][p, 64 * t:64 * t + 64], ALU.add).then_inc(empt["back", 1], 1)

        def v_scale5(e, i, nb):
            sl, jn = nb % 2, 64 * (nb % 3 + 1)
            e.wait_ge(*emptied("back", i, "s5A", nb)); e.wait_ge(*emptied("back", i, "s5B", nb))
            e.reciprocal(DEN5[:, sl, :], DEN5[:, sl, :]); e.drain()
            e.tensor_tensor(P5[:, sl, :, 0:jn], P5[:, sl, :, 0:jn], DEN5[:, sl, :].rearrange("p (h o) -> p h o", o=1).to_broadcast([128, 4, jn]), ALU.mult).then_inc(S["scaled5"], 1)

        def kvt_out(e, n):
            t, hh = n // 2, n % 2
            dst = KVT[:, 4 * hh:4 * hh + 4, 128 * t:128 * t + 128]
            src = PB[2 + n % 2][:, :].rearrange("p (h n) -> p h n", n=128)
            return e.tensor_copy(dst, src) if n % 2 else e.activation(dst, src, ACT.Copy)

        def a_rnn(e, j):
            yield 4.4
            e.wait_ge(*filled("front", j, "xT"))
            e.activation(RS[0:64, :, :].rearrange("p a b -> p (a b)"), PB[0][0:64, 0:TOK], ACT.Copy).then_inc(empt["front", 0], 1)
            for s in range(2):
                yield 5.5 + s
                e.wait_ge(*filled("front", j, "rnn", s))
                e.activation(RS[64:128, 1 - s, :], PB[1][64:128, 0:SEQ], ACT.Tanh, bias=BSUM[64:128, :]).then_inc(empt["front", 1], 1)

        def a_moe(e, j):
            yield 4.3
            e.wait_ge(*filled("front", j, "moeT"))
            e.activation(NTR[0:64, :], PB[0][0:64, 0:TOK], ACT.Copy).then_inc(empt["front", 0], 1)
            yield 5
            e.wait_ge(*event("shifted", j, 1))
            e.activation(LE[:, :, :], LG[:, :, :], ACT.Exp).then_inc(S["exped"], 1)
            yield 5.2
            for n in range(16):
                name = ("hidA", "hidB")[n % 2]
                if n >= 2 and n % 2 == 0: yield 6.5 + n // 2
                e.wait_ge(*filled("front", j, name, n // 2))
                e.activation(HID[:, n % 4, :], PB[2 + n % 2][:, 0:TOK], ACT.Relu).then_inc(empt["front", 2 + n % 2], 1)

        def a_att(e, j):
            yield 4.4
            e.wait_ge(*filled("front", j, "attT"))
            e.activation(NTR[0:64, :], PB[0][0:64, 0:TOK], ACT.Copy).then_inc(empt["front", 0], 1)
            for n in range(5):
                yield 5.5 + n
                e.wait_ge(*filled("front", j, "qkvA", n))
                e.activation(QT[:, 2 * n, :] if n < 4 else KT[:, :], PB[2][0:64, 0:TOK], ACT.Copy, scale=float(1 / np.sqrt(np.float32(8))) if n < 4 else 1.0).then_inc(empt["front", 2], 1)
            for n in range(12):
                yield 10.6 + n // 2
                name = ("scoreA", "scoreB")[n % 2]
                e.wait_ge(*event("maxed", j, 2 * n + 2))
                for a in range(2):
                    ins = e.activation(P[:, 2 * n + a, :], PB[2 + n % 2][:, SEQ * a:SEQ * a + SEQ], ACT.Exp, bias=NM[:, 2 * n + a:2 * n + a + 1], accum_out=DEN[:, 2 * n + a:2 * n + a + 1])
                ins.then_inc(empt["front", 2 + n % 2], 1)

        def a_pk(e, j):
            yield 4.4
            e.wait_ge(*filled("front", j, "pkT"))
            e.wait_ge(*event("kept_x", j - 1, 1))
            e.activation(NT4[:, :], PB[0][0:64, 0:TOK], ACT.Copy).then_inc(empt["front", 0], 1)
            for n in range(2):
                yield 5.5 + n
                e.wait_ge(*filled("front", j, "qpkA", n))
                e.activation(QPK[:, 2 * n, :], PB[2][:, 0:TOK], ACT.Copy).then_inc(empt["front", 2], 1)
            for t in range(NT3):
                yield 7.5 + t
                e.wait_ge(*filled("front", j, "simA", t))
                e.activation(SIM[:, t, 0, :], PB[2][:, :], ACT.Copy).then_inc(empt["front", 2], 1)

        def a_top(e, j):
            for t in range(NT3):
                yield TOP_STEPS * t + 6.3
                e.wait_ge(*event("shift_top", j, t + 1))
                e.activation(FS[:, :, :], FS[:, :, :], ACT.Exp).then_inc(S["exp_top"], 1)

        def a_back(e, i):
            for n in range(3):
                yield n + 0.5
                e.wait_ge(*filled("back", i, "kvA", n))
                kvt_out(e, 2 * n).then_inc(empt["back", 2], 1)
            for n in range(4):
                yield 3.5 + n
                e.wait_ge(*filled("back", i, "q5A", n))
                e.activation(Q5[:, 2 * n, :], PB[2][0:64, 0:TOK], ACT.Copy, scale=D ** -0.5).then_inc(empt["back", 2], 1)
            for n in range(3):
                yield 7.5 + n
                e.wait_ge(*filled("back", i, "vwA", n))
                e.activation(VW[:, n, :, :].rearrange("p h d -> p (h d)"), PB[2][:, :], ACT.Copy).then_inc(empt["back", 2], 1)
            for n in range(12):
                yield 10.6 + n // 2
                half, nb = n % 2, n // 2
                jn = 64 * (nb % 3 + 1)
                if half == 0 and nb >= 2: e.wait_ge(*emptied("back", i, "pt0", nb - 2))
                e.wait_ge(*event("maxed5", i, n + 1))
                for a in range(2):
                    hp = 2 * half + a
                    ins = e.activation(P5[:, nb % 2, hp, 0:jn], PB[2 + half][:, SEQ * a:SEQ * a + jn], ACT.Exp, bias=NM5[:, nb % 2, hp:hp + 1], accum_out=DEN5[:, nb % 2, hp:hp + 1])
                ins.then_inc(empt["back", 2 + half], 1)
                if half == 1 and nb >= 1:
                    yield 10.8 + nb
                    a_pt(e, i, nb - 1)
            yield 16.8
            a_pt(e, i, 5)

        def spans(nb):
            b, jn = nb // 3, 64 * (nb % 3 + 1)
            cut = (0, 128, 192) if b == 0 else (0, 64, 192)
            out = []
            for lo, hi in zip(cut, cut[1:]):
                hi = min(hi, jn)
                if hi > lo:
                    n = SEQ * b + lo
                    out.append((lo, hi, n % 128, n // 128))
            return out

        def slot(c, p0):
            return 2 if p0 else c

        def a_pt(e, i, nb):
            e.wait_ge(*filled("back", i, "pt0", nb))
            sp = spans(nb)
            for c, (lo, hi, p0, t) in enumerate(sp):
                ins = e.activation(PT[p0:p0 + hi - lo, slot(c, p0), :], PTB[c][p0:p0 + hi - lo, :], ACT.Copy)
            ins.then_inc(empt["back", 0], 1)
        PTB = [PB[0], PB[1]]


        def t_turn(e, j, name, k):
            e.wait_ge(*event("normed", j, k))
            e.wait_ge(*free("front", j, name))
            fence(e)
            for t in range(NT3):
                m = e.transpose(PB[0][0:64, 128 * t:128 * t + 128], N[:, t, :], ID[:, :])
            m.then_inc(full["front", 0], 1)

        def t_rnn(e, j):
            yield 4
            if not (isinstance(j, int) and j < 2):
                e.wait_ge(*event("out_sb", j - 3, 1))
                e.wait_ge(*emptied("back", j - 2, "kvA", 2)); e.wait_ge(*emptied("back", j - 2, "kvB", 2))
            t_turn(e, j, "xT", 1)
            yield 4.7
            e.wait_ge(*emptied("front", j, "xT"))
            for s in range(2):
                yield 5 + s
                e.wait_ge(*free("front", j, "rnn", s))
                fence(e)
                e.matmul(PB[1][64:128, 0:SEQ], WRNN[:, :], RS[:, s, :], start=True, stop=True).then_inc(full["front", 1], 1)
            yield 7
            e.wait_ge(*emptied("front", j, "rnn", 1))
            e.wait_ge(*free("front", j, "rnn_back"))
            fence(e)
            i64 = ID[64:128, 64:128]
            e.transpose(PB[2][:, 0:64], RS[64:128, 1, 0:128], i64)
            e.transpose(PB[2][0:64, 64:128], RS[64:128, 1, 128:192], i64)
            e.matmul(PB[2][64:128, 64:128], RS[64:128, 0, 0:64], i64, start=True, stop=True)
            e.transpose(PB[2][:, 128:192], RS[64:128, 0, 64:192], i64).then_inc(full["front", 2], 1)

        def t_moe(e, j):
            yield 4
            t_turn(e, j, "moeT", 2)
            yield 4.5
            e.wait_ge(*emptied("front", j, "moeT"))
            e.wait_ge(*free("front", j, "gate"))
            fence(e)
            for t in range(NT3):
                m = e.matmul(PB[1][:, 8 * t:8 * t + 8], NTR[:, 128 * t:128 * t + 128], GW[:, :], start=True, stop=True)
            m.then_inc(full["front", 1], 1)
            def hid(n):
                name = ("hidA", "hidB")[n % 2]
                e.wait_ge(*free("front", j, name, n // 2))
                fence(e)
                e.matmul(PB[2 + n % 2][:, 0:TOK], W1[:, 128 * n:128 * n + 128], NTR[:, :], start=True, stop=True).then_inc(full["front", 2 + n % 2], 1)
            yield 4.6
            hid(0); hid(1)
            yield 6
            e.wait_ge(*event("one_hot", j, 1))
            e.wait_ge(*free("front", j, "place"))
            fence(e)
            for t in range(NT3):
                e.matmul(PB[1][:, 8 * t:8 * t + 8], TRI[:, :], OH[:, t, :], start=True, stop=False)
                for s in range(t):
                    e.matmul(PB[1][:, 8 * t:8 * t + 8], ONES[:, :], OH[:, s, :], start=False, stop=False)
                m = e.matmul(PB[1][:, 8 * t:8 * t + 8], ONES[:, :], OHS[:, :], start=False, stop=True)
            m.then_inc(full["front", 1], 1)
            for x in range(E):
                yield 7 + x
                if x + 1 < E: hid(2 * x + 2); hid(2 * x + 3)
                yield 7.1 + x
                name = ("expert", "expertB")[x % 2]
                b = bank("front", name)
                e.wait_ge(*free("front", j, name, x // 2))
                e.wait_ge(*emptied("front", j, "hidA", x)); e.wait_ge(*emptied("front", j, "hidB", x))
                fence(e)
                for t in range(NT3):
                    o = PB[b][:, 64 * t:64 * t + 64]
                    e.matmul(o, ONES[0:1, :], B2[:, 64 * x:64 * x + 64], start=True, stop=False)
                    for f in range(2):
                        n = 2 * x + f
                        m = e.matmul(o, HID[:, n % 4, 128 * t:128 * t + 128], W2[:, 64 * n:64 * n + 64], start=False, stop=(f == 1))
                m.then_inc(full["front", b], 1)

        def t_att(e, j):
            yield 4
            t_turn(e, j, "attT", 3)
            yield 5
            e.wait_ge(*emptied("front", j, "attT"))
            for n in range(10):
                yield 5 + n // 2
                name = ("qkvA", "qkvB")[n % 2]
                e.wait_ge(*free("front", j, name, n // 2))
                fence(e)
                w = WQ[:, 64 * n:64 * n + 64] if n < 8 else (WK, WV)[n - 8][:, :]
                e.matmul(PB[2 + n % 2][0:64, 0:TOK], w, NTR[0:64, :], start=True, stop=True).then_inc(full["front", 2 + n % 2], 1)
            yield 10
            e.wait_ge(*emptied("front", j, "qkvA", 4)); e.wait_ge(*emptied("front", j, "qkvB", 4))
            def scores(n):
                name = ("scoreA", "scoreB")[n % 2]
                e.wait_ge(*free("front", j, name, n // 2))
                fence(e)
                for a in range(2):
                    rt = 2 * n + a
                    b, pp, jj = rt // 12, rt % 12 // 4, rt % 4
                    for h2 in range(2):
                        u = 3 * (2 * jj + h2) + pp
                        r, h = u // 8, u % 8
                        m = e.matmul(PB[2 + n % 2][64 * h2:64 * h2 + 64, SEQ * a:SEQ * a + SEQ], QT[:, h, SEQ * b + r:SEQ * b + r + 190:3], KT[:, SEQ * b:SEQ * b + SEQ], start=True, stop=True)
                m.then_inc(full["front", 2 + n % 2], 1)
            def zs(b):
                e.wait_ge(*event("rden", j, b + 1))
                e.wait_ge(*free("front", j, "z", b)); e.wait_ge(*free("front", j, "z2", b))
                fence(e)
                for jc in range(3):
                    for pp in range(3):
                        o = PB[0][0:64, 192 * jc + 64 * pp:192 * jc + 64 * pp + 64] if jc < 2 else PB[1][0:64, 64 * pp:64 * pp + 64]
                        for jj in range(4):
                            m = e.matmul(o, P[:, 12 * b + 4 * pp + jj, jc:jc + 190:3], WON[:, 4 * pp + jj, :], start=(jj == 0), stop=(jj == 3))
                    if jc == 1: m.then_inc(full["front", 0], 1)
                m.then_inc(full["front", 1], 1)
            def outs(b):
                e.wait_ge(*emptied("front", j, "z", b)); e.wait_ge(*emptied("front", j, "z2", b))
                if b == 0: e.wait_ge(*free("front", j, "att"))
                fence(e)
                for pp in range(3):
                    nb = 3 * b + pp
                    for jc in range(3):
                        m = e.matmul(PB[2][64 * (nb % 2):64 * (nb % 2) + 64, 64 * (nb // 2):64 * (nb // 2) + 64],
                                     VC[:, SEQ * b + 64 * jc:SEQ * b + 64 * jc + 64], Z[:, jc, 64 * pp:64 * pp + 64], start=(jc == 0), stop=(jc == 2))
                if b: m.then_inc(full["front", 2], 1)
            for n in range(12):
                yield 10 + n // 2
                scores(n)
                if n == 9:
                    yield 14.5
                    zs(0)
            yield 16
            outs(0)
            yield 16.1
            zs(1)
            yield 17
            outs(1)

        def t_pk(e, j):
            yield 4
            t_turn(e, j, "pkT", 4)
            yield 5
            e.wait_ge(*emptied("front", j, "pkT"))
            for n in range(4):
                yield 5 + n // 2
                name = ("qpkA", "qpkB")[n % 2]
                e.wait_ge(*free("front", j, name, n // 2))
                fence(e)
                e.matmul(PB[2 + n % 2][:, 0:TOK], WPK[:, 128 * n:128 * n + 128], NT4[:, :], start=True, stop=True).then_inc(full["front", 2 + n % 2], 1)
            yield 7
            e.wait_ge(*emptied("front", j, "qpkA", 1)); e.wait_ge(*emptied("front", j, "qpkB", 1))
            for t in range(NT3):
                yield 7 + t
                for p in range(2):
                    name = ("simA", "simB")[p]
                    e.wait_ge(*free("front", j, name, t))
                    fence(e)
                    for hh in range(2):
                        m = e.matmul(PB[2 + p][:, 256 * hh:256 * hh + 256], QPK[:, 2 * p + hh, 128 * t:128 * t + 128], KB[:, 2 * p + hh, :], start=True, stop=True)
                    m.then_inc(full["front", 2 + p], 1)

        def t_back(e, i):
            yield 0
            e.wait_ge(*event("weighted", i, 1))
            for n in range(6):
                yield n // 2
                t, hh = n // 2, n % 2
                e.wait_ge(*free("back", i, ("kvA", "kvB")[n % 2], n // 2))
                fence(e)
                for h in range(4):
                    m = e.transpose(PB[2 + n % 2][:, 128 * h:128 * h + 128], KV[:, t, 4 * hh + h, :], ID[:, :])
                m.then_inc(full["back", 2 + n % 2], 1)
            yield 3
            if not (isinstance(i, int) and i + 2 >= PAIRS):
                e.wait_ge(*emptied("front", i + 2, "simA", 2)); e.wait_ge(*emptied("front", i + 2, "simB", 2))
            for n in range(8):
                yield 3 + n // 2
                name = ("q5A", "q5B")[n % 2]
                e.wait_ge(*free("back", i, name, n // 2))
                fence(e)
                e.matmul(PB[2 + n % 2][0:64, 0:TOK], WQ5[:, 64 * n:64 * n + 64], NTC[:, :], start=True, stop=True).then_inc(full["back", 2 + n % 2], 1)
            yield 7
            e.wait_ge(*emptied("back", i, "kvA", 2)); e.wait_ge(*emptied("back", i, "kvB", 2))
            for t in range(NT3):
                yield 7 + t
                e.wait_ge(*free("back", i, "vwA", t))
                fence(e)
                for h in range(H):
                    m = e.matmul(PB[2][:, 64 * h:64 * h + 64], KVT[64:128, h, 128 * t:128 * t + 128], WO5[64:128, h, :], start=True, stop=True)
                m.then_inc(full["back", 2], 1)
            def sims(n):
                b, ib, half = n // 6, n // 2 % 3, n % 2
                jn = 64 * (ib + 1)
                e.wait_ge(*free("back", i, ("s5A", "s5B")[half], n // 2))
                fence(e)
                for a in range(2):
                    for h2 in range(2):
                        h = 2 * (2 * half + a) + h2
                        m = e.matmul(PB[2 + half][64 * h2:64 * h2 + 64, SEQ * a:SEQ * a + jn], Q5[:, h, SEQ * b + 64 * ib:SEQ * b + 64 * ib + 64], KVT[0:64, h, SEQ * b:SEQ * b + jn], start=True, stop=True)
                m.then_inc(full["back", 2 + half], 1)
            def turnp(nb):
                e.wait_ge(*event("scaled5", i, nb + 1))
                e.wait_ge(*free("back", i, "pt0", nb)); e.wait_ge(*free("back", i, "out", nb))
                fence(e)
                for c, (lo, hi, p0, t) in enumerate(spans(nb)):
                    for hp in range(4):
                        o = PTB[c][p0:p0 + hi - lo, 128 * hp:128 * hp + 128]
                        m = (e.matmul(o, P5[:, nb % 2, hp, lo:hi], ID[:, :], start=True, stop=True) if p0
                             else e.transpose(o, P5[:, nb % 2, hp, lo:hi], ID[:, :]))
                m.then_inc(full["back", 0], 1)
            def outs(nb):
                e.wait_ge(*emptied("back", i, "pt0", nb))
                if nb == 0: e.wait_ge(*emptied("back", i, "vwA", 2))
                fence(e)
                o = PB[1][64 * (nb % 2):64 * (nb % 2) + 64, 64 * (nb // 2):64 * (nb // 2) + 64]
                sp = spans(nb)
                for h in range(H):
                    for c, (lo, hi, p0, t) in enumerate(sp):
                        m = e.matmul(o, PT[0:p0 + hi - lo, slot(c, p0), 64 * h:64 * h + 64], VW[0:p0 + hi - lo, t, h, :],
                                     start=(h == 0 and c == 0), stop=(h == H - 1 and c == len(sp) - 1))
                m.then_inc(full["back", 1], 1)
            e.wait_ge(*emptied("back", i, "q5A", 3)); e.wait_ge(*emptied("back", i, "q5B", 3))
            yield 10
            sims(0); sims(1)
            for nb in range(6):
                yield 11 + nb
                if nb < 5: sims(2 * nb + 2); sims(2 * nb + 3)
                yield 11.6 + nb
                turnp(nb)
                yield 11.9 + nb
                outs(nb)

        def rounds(e, sections, mixers, loads=lambda e: None):
            def run(windows, i, g, l):
                engine, begun = sections(e, i - 1, i, i + 1, g, l), {}
                for chains in windows:
                    weave(engine, chains, begun)
            run([[whole("coords")]], 0, 0, None)
            loads(e)
            with e.Fori(0, LAYERS // 2) as l:
                run([[whole(*LAYER_0, *LAYER_1)]], 0, 0, 2 * l)
            run([[whole("tokens")]], 0, 0, None)
            mixers(e)
            run(a_round(begin=("coords",), rows=False, back=False), -1, 1, 0)
            run(a_round(end=("tokens",), back=False), 0, 1, 2)
            with e.Fori(1, GROUPS - 1) as g:
                run(a_round(begin=("coords",)), 2 * g - 1, g + 1, 0)
                run(a_round(end=("tokens",)), 2 * g, g + 1, 2)
            with e.Fori(2 * GROUPS - 3, PAIRS - 1) as i:
                run(a_round(layers=False), i, GROUPS, None)
            run(a_round(layers=False, front=False), PAIRS - 1, None, None)
            run([[whole("back")]], PAIRS, None, None)

        def units(consume, e, i):
            def steps():
                for u in range(NT3 * H): yield from consume(e, i, u)
            return steps

        def QUEUE(e, k, i, j, g, l):
            return {"coords": lambda: sp_coords(e, g), "forward0": lambda: sp_forward(e, g, l), "forward1": lambda: sp_forward(e, g, l + 1), "mix0": lambda: sp_mix(e, g, l), "mix1": lambda: sp_mix(e, g, l + 1),
                    "tokens": lambda: sp_tokens(e, g), "rnn": lambda: sp_front(e, j, g), "back": lambda: sp_back(e, k)}

        def TENSOR(e, k, i, j, g, l):
            return {"coords": lambda: t_coords(e, g), "forward0": lambda: t_forward(e, g, l, 0), "forward1": lambda: t_forward(e, g, l + 1, 0),
                    "mix0": lambda: t_mix(e, g, l), "mix1": lambda: t_mix(e, g, l + 1), "inverse0": lambda: t_inverse(e, g, l, 0), "inverse1": lambda: t_inverse(e, g, l + 1, 0),
                    "tokens": lambda: t_tokens(e, g), "rnn": lambda: t_rnn(e, j), "moe": lambda: t_moe(e, j), "att": lambda: t_att(e, j),
                    "pk": lambda: t_pk(e, j), "back": lambda: t_back(e, k)}

        def SCALAR(e, k, i, j, g, l):
            return {"coords": lambda: a_coords(e, g), "forward0": lambda: a_forward(e, g, l, 0), "forward1": lambda: a_forward(e, g, l + 1, 0),
                    "mix0": lambda: a_mix(e, g, l), "mix1": lambda: a_mix(e, g, l + 1), "inverse0": lambda: a_inverse(e, g, l, 0), "inverse1": lambda: a_inverse(e, g, l + 1, 0),
                    "tokens": lambda: a_tokens(e, g), "rnn": lambda: a_rnn(e, j), "moe": lambda: a_moe(e, j), "att": lambda: a_att(e, j),
                    "pk": lambda: a_pk(e, j), "top": lambda: a_top(e, j), "back": lambda: a_back(e, k),
                    "rows": units(a_consume, e, i)}

        def VECTOR(e, k, i, j, g, l):
            return {"forward0": lambda: v_forward(e, g, l, 0), "forward1": lambda: v_forward(e, g, l + 1, 0),
                    "inverse0": lambda: v_inverse(e, g, l, 0), "inverse1": lambda: v_inverse(e, g, l + 1, 0),
                    "tokens": lambda: v_tokens(e, g), "rnn": lambda: v_rnn(e, j), "moe": lambda: v_moe(e, j), "att": lambda: v_att(e, j),
                    "pk": lambda: v_pk(e, j), "top": lambda: v_top(e, j), "back": lambda: v_back(e, k), "keep_x": lambda: v_keep_x(e, j, not isinstance(i, int) or i >= 0, not isinstance(i, int) or i < PAIRS - 1),
                    "rows": units(v_consume, e, i)}

        @block.sync
        def _(e):
            sp_setup(e)
            rounds(e, QUEUE, lambda e: None, sp_mixers)
            e.wait_ge(*event("stored", PAIRS - 1, 16))

        @block.gpsimd
        def _(e):
            def before(e):
                for t in (FW0, FW1, FW2, CONV, KB, ONES, RS, OHS, AREA4):
                    e.memset(t[:], 1.0 if t is ONES else 0.0).then_inc(zeroed, 1)
            before(e)
            with e.Fori(0, PAIRS) as i:
                pool_gather(e, i)

        @block.vector
        def _(e):
            def before(e):
                credits(e, ["normed", "shifted", "one_hot", "maxed", "rden", "shift_top", "kept_idx", "kept_x", "gather_free", "weighted", "maxed5", "scaled5", "out_sb"],
                        [(k, b) for k in PLANS for b in range(4)])
                e.sem_inc(tp_out, CREDIT); e.sem_inc(tp_full, CREDIT)
                e.memset(NTR[64:65, :], 1.0); e.memset(NEG[:, :], -FMAX); e.memset(BIG[:, 0:1], 1e4); e.memset(BIG[:, 1:2], -1e4)
                e.wait_ge(tokenizer_in, 16 * N_TOKENIZER)
            def mixers(e):
                e.wait_ge(const_in, 16 * NLOADS)
                e.tensor_tensor(BSUM[64:128, :], BRNN[64:128, 0:1], BRNN[64:128, 1:2], ALU.add)
                e.drain().then_inc(zeroed, 1)
            before(e)
            rounds(e, VECTOR, mixers)

        @block.scalar
        def _(e):
            def before(e):
                credits(e, ["exped", "exp_top", "multiplied"])
                e.sem_inc(mm_out, CREDIT); e.sem_inc(mm_full, CREDIT)
                e.wait_ge(tokenizer_in, 16 * N_TOKENIZER); e.wait_ge(zeroed, 9)
            def mixers(e):
                e.wait_ge(const_in, 16 * NLOADS); e.wait_ge(zeroed, 10)
            before(e)
            rounds(e, SCALAR, mixers)

        @block.tensor
        def _(e):
            def before(e):
                e.wait_ge(tokenizer_in, 16 * N_TOKENIZER); e.wait_ge(zeroed, 9)
            def mixers(e):
                e.wait_ge(const_in, 16 * NLOADS); e.wait_ge(zeroed, 10)
            before(e)
            rounds(e, TENSOR, mixers)


def layouts(inputs):
    g = {n: np.asarray(a) for n, a in inputs.items()}
    return [
        g["x"].transpose(0, 3, 1, 2).reshape(B * 3, POS),
        np.concatenate([g["L0_tok_fc0_w"], g["L0_tok_fc0_b"][None]], 0),
        np.stack([g[f"L0_tok_sw{n}"] for n in range(LAYERS)]).reshape(LAYERS, WID, WID, MODES, Q4, CHUNKS)
          .transpose(0, 5, 4, 1, 3, 2).reshape(LAYERS * CHUNKS * 128, MODES * WID),
        np.concatenate([np.concatenate([g[f"L0_tok_cw{n}"].T, g[f"L0_tok_cb{n}"][:, None]], 1) for n in range(LAYERS)], 0),
        np.concatenate([g["L0_tok_fc1_w"], g["L0_tok_fc1_b"][None]], 0),
        np.concatenate([g["L0_tok_fc2_w"], g["L0_tok_fc2_b"][None]], 0),
        *fourier_constants(),
        g["txt"].reshape(B * 128, D),
        np.concatenate([g["L0_attn_W_ih"].T, g["L0_attn_W_hh"].T], 0),
        np.stack([g["L0_attn_b_ih"], g["L0_attn_b_hh"]]),
        np.concatenate([g["L0_ffn_gate_w"], g["L0_ffn_gate_b"][None]], 0),
        np.concatenate([g["L0_ffn_w1"].transpose(1, 0, 2).reshape(D, E * FF), g["L0_ffn_b1"].reshape(1, E * FF)], 0),
        g["L0_ffn_w2"].reshape(E, 2, 128, D).transpose(2, 0, 1, 3).reshape(128, 2 * E * D),
        g["L0_ffn_b2"].reshape(1, E * D),
        g["L1_attn_Wq"].T, g["L1_attn_Wk"].T, g["L1_attn_Wv"].T,
        g["L1_attn_Wo"].T.reshape(64, 4, 2, D).transpose(2, 0, 1, 3).reshape(128, 4 * D),
        g["L1_ffn_Wq_pk"],
        g["L1_ffn_pk_keys"].transpose(0, 2, 3, 1).reshape(2 * H * 32, NK),
        g["L1_ffn_Wq"],
        g["L1_ffn_Wo"].reshape(H, D, D).transpose(1, 0, 2).reshape(D, H * D),
        np.concatenate([g["L1_ffn_keys_table"], g["L1_ffn_values_table"]], 1),
        *shape_constants(),
    ]


def shape_constants():
    row = np.arange(128)
    every = lambda v: np.tile(np.asarray(v, np.float32), (128, 1))
    return [
        np.eye(128, dtype=np.float32),
        np.triu(np.ones((128, 128), np.float32)),
        every(np.arange(NC50)),
        every(E - np.arange(E)),
        every(NK * NK * np.arange(H)),
        (np.arange(D)[None, :] > (row % D)[:, None]).astype(np.int32),
    ]


_NAMES = ["xT", "fc0", "sw", "cwb", "fc1", "fc2", "f1", "f2", "g3", "g4", "txt", "wrnn", "brnn", "gw", "w1", "w2", "b2", "wq", "wk", "wv",
          "wot", "wpk", "keysT", "wq5", "wo5", "table", "ident", "tri", "iota", "eight", "hbase", "later"]


def kernel(**inputs):
    import concourse.bacc as _bacc
    from concourse.bass_utils import run_bass_kernel_spmd as _run

    nc = _bacc.Bacc("TRN2", target_bir_lowering=False, num_devices=1)
    arrays, args = {}, []
    for name, a in zip(_NAMES, layouts(inputs)):
        a = np.ascontiguousarray(a)
        arrays[f"in_{name}"] = a
        args.append(nc.dram_tensor(f"in_{name}", a.shape, mybir.dt.from_np(a.dtype), kind="ExternalInput").ap())
    args.append(nc.dram_tensor("out", (B * SEQ, D), F32, kind="ExternalOutput").ap())
    early_fusion(nc, *args)
    r = _run(nc, [arrays], core_ids=[0])
    return r.results[0]["out"].reshape(B, SEQ, D)
```
